# Optimizing a Trainium2 kernel written in Bass

```python
import numpy as np
import jax
import jax.numpy as jnp

def _softmax(x, axis=-1):
    return jax.nn.softmax(x, axis=axis)

def _gelu(x):
    return jax.nn.gelu(x, approximate=True)

def _silu(x):
    return jax.nn.silu(x)

def _sigmoid(x):
    return jax.nn.sigmoid(x)

def _layernorm(x, axis=-1, eps=1e-05):
    m = jnp.mean(x, axis=axis, keepdims=True)
    v = jnp.var(x, axis=axis, keepdims=True)
    return (x - m) / jnp.sqrt(v + eps)

def _scatter_add(tgt, idx, src, axis=0):
    return tgt.at[idx].add(src)

def _segment_sum(src, seg, n):
    return jax.ops.segment_sum(src, seg, n)
kernel_name = 'mk_flamingo_gated_d2_seqx_r4_c77a97'

def setup_inputs(seed: int=0):
    np.random.seed(seed)
    _w = jnp.asarray

    def _rec_inputs():
        import jax
        import jax.numpy as jnp
        _rk = jax.random.key(seed)
        x = 7.22e-05 + 1 * jax.random.normal(jax.random.fold_in(_rk, 1), (8, 256, 1024), jnp.float32)
        _lenS = 256 - jax.random.randint(jax.random.fold_in(_rk, 7), (8,), 0, max(1, 256 // 4) + 1, jnp.int32)
        _lenS2 = 256 - jax.random.randint(jax.random.fold_in(_rk, 8), (8,), 0, max(1, 256 // 4) + 1, jnp.int32)
        _ctx_4096P = jax.random.normal(jax.random.fold_in(_rk, 11), (8, 16, 1024), jnp.float32)
        _ctx_4096c = jax.random.dirichlet(jax.random.fold_in(_rk, 511), 0.3 * jnp.ones((16,), jnp.float32), (8, 256))
        _ctx_4096t = jnp.einsum('bsk,bkd->bsd', _ctx_4096c, _ctx_4096P)
        _ctx_4096t = _ctx_4096t * jax.lax.rsqrt(jnp.mean(jnp.square(_ctx_4096t)) + 1e-12) * 0.953939
        ctx_4096 = 2.81802e-05 + 1.00001 * (_ctx_4096t + 0.3 * jax.random.normal(jax.random.fold_in(_rk, 611), (8, 256, 1024), jnp.float32))
        _g = jax.random.normal(jax.random.fold_in(_rk, 9001), (2, 2), jnp.float32)
        _g = jnp.sign(_g) * jnp.maximum(jnp.abs(_g), 1.0) + (_g == 0) * 1.0
        g_xattn = _g[0]
        g_ffn = _g[1]
        return (x, ctx_4096, g_xattn, g_ffn)
    x, ctx_4096, g_xattn, g_ffn = _rec_inputs()

    def _L0_xattn_setup():
        import jax, jax.numpy as jnp
        import numpy as np
        HIDDEN = 1024
        N_HEADS = 32
        N_KV_HEADS = 8
        HEAD_DIM = HIDDEN // N_HEADS
        N_REP = N_HEADS // N_KV_HEADS
        EPS = 1e-05

        def _rmsnorm(x, w):
            xf = x.astype(jnp.float32)
            var = jnp.mean(xf * xf, axis=-1, keepdims=True)
            return (xf * jax.lax.rsqrt(var + EPS)).astype(x.dtype) * w
        key = jax.random.key(seed)
        ks = jax.random.split(key, 7)
        B, Q, K = (2, 256, 512)
        scale = 0.02
        return {'hidden_states': jax.random.normal(ks[0], (B, Q, HIDDEN), jnp.float32), 'encoder_hidden_states': jax.random.normal(ks[1], (B, K, HIDDEN), jnp.float32), 'wq': jax.random.normal(ks[2], (N_HEADS * HEAD_DIM, HIDDEN), jnp.float32) * scale, 'wk': jax.random.normal(ks[3], (N_KV_HEADS * HEAD_DIM, HIDDEN), jnp.float32) * scale, 'wv': jax.random.normal(ks[4], (N_KV_HEADS * HEAD_DIM, HIDDEN), jnp.float32) * scale, 'wo': jax.random.normal(ks[5], (HIDDEN, N_HEADS * HEAD_DIM), jnp.float32) * scale, 'ln_w': jnp.ones((HIDDEN,), jnp.float32)}
    _L0_xattn_all = _L0_xattn_setup()
    _L0_xattn_in = {k: v for k, v in _L0_xattn_all.items() if k in ('wq', 'wk', 'wv', 'wo', 'ln_w')}
    del _L0_xattn_all

    def _L0_ffn_setup():
        import math
        import jax, jax.numpy as jnp
        import numpy as np
        SCALING = 16.0 / 32.0

        def real_fourier_orthogonal_multiply(c):
            n = c.shape[-1]
            sqrt_n = math.sqrt(n)
            pair_scale = math.sqrt(n / 2.0)
            max_f = (n - 1) // 2
            work = c.astype(jnp.float32)
            dc = (work[..., 0] * sqrt_n)[..., None].astype(jnp.complex64)
            cos = work[..., 1:1 + 2 * max_f:2] * pair_scale
            sin = work[..., 2:2 + 2 * max_f:2] * pair_scale
            mid = (cos - 1j * sin).astype(jnp.complex64)
            parts = [dc, mid]
            if n % 2 == 0:
                parts.append((work[..., -1] * sqrt_n)[..., None].astype(jnp.complex64))
            spectrum = jnp.concatenate(parts, axis=-1)
            return jnp.fft.irfft(spectrum, n=n, axis=-1).astype(c.dtype)
        key = jax.random.key(seed)
        ks = jax.random.split(key, 9)
        B, S, D_in, D_out, R0, R1, E = (4, 512, 1024, 1024, 32, 8, 3)
        x = jax.random.normal(ks[0], (B, S, D_in), dtype=jnp.float32)
        W_base = jax.random.normal(ks[1], (D_out, D_in), dtype=jnp.float32) * 0.02
        b_base = jax.random.normal(ks[2], (D_out,), dtype=jnp.float32) * 0.02
        enc0 = jax.random.normal(ks[3], (R0, D_in), dtype=jnp.float32) * 0.02
        enc1 = jax.random.normal(ks[4], (R1, D_in), dtype=jnp.float32) * 0.02
        coefs0 = jax.random.normal(ks[5], (E, D_out, R0), dtype=jnp.float32) * 0.02
        coefs1 = jax.random.normal(ks[6], (E, D_out, R1), dtype=jnp.float32) * 0.02
        mask0 = jax.random.randint(ks[7], (E, D_out, R0), 0, 2).astype(bool)
        mask1 = jax.random.randint(ks[8], (E, D_out, R1), 0, 2).astype(bool)
        return dict(x=x, W_base=W_base, b_base=b_base, enc0=enc0, enc1=enc1, coefs0=coefs0, coefs1=coefs1, mask0=mask0, mask1=mask1)
    _L0_ffn_all = _L0_ffn_setup()
    _L0_ffn_in = {k: v for k, v in _L0_ffn_all.items() if k in ('W_base', 'b_base', 'enc0', 'enc1', 'coefs0', 'coefs1', 'mask0', 'mask1')}
    del _L0_ffn_all

    def _L1_xattn_setup():
        import jax, jax.numpy as jnp
        import numpy as np
        B, D, N, H, K = (4, 256, 1024, 16, 64)
        HD = D // H

        def _conv1x1(x, W, b):
            return jnp.einsum('od,bdn->bon', W, x) + b[None, :, None]
        key = jax.random.key(seed)
        ks = jax.random.split(key, 12)
        std_w = 1.0 / np.sqrt(D)
        std_p = 1.0 / np.sqrt(K)
        u = lambda k, shape, s: jax.random.uniform(k, shape, jnp.float32, -s, s)
        return {'query': jax.random.normal(ks[0], (B, D, N), jnp.float32), 'key': jax.random.normal(ks[1], (B, D, N), jnp.float32), 'value': jax.random.normal(ks[2], (B, D, N), jnp.float32), 'Wq': u(ks[3], (D, D), std_w), 'bq': u(ks[4], (D,), std_w), 'Wk': u(ks[5], (D, D), std_w), 'bk': u(ks[6], (D,), std_w), 'Wv': u(ks[7], (D, D), std_w), 'bv': u(ks[8], (D,), std_w), 'proj_k': u(ks[9], (N, K), std_p), 'proj_v': u(ks[10], (N, K), std_p), 'Wm': u(ks[11], (D, D), std_w), 'bm': u(jax.random.fold_in(key, 99), (D,), std_w)}
    _L1_xattn_all = _L1_xattn_setup()
    _L1_xattn_in = {k: v for k, v in _L1_xattn_all.items() if k in ('Wq', 'bq', 'Wk', 'bk', 'Wv', 'bv', 'proj_k', 'proj_v', 'Wm', 'bm')}
    del _L1_xattn_all

    def _L1_ffn_setup():
        import jax, jax.numpy as jnp
        import numpy as np
        FP8_MAX = 448.0
        K = 1024
        N = 1024

        def _compute_scale(t):
            amax = jnp.max(jnp.abs(t))
            return FP8_MAX / jnp.maximum(amax, 1e-12)

        def _quantize_fp8(t, scale):
            return jnp.clip(t * scale, -FP8_MAX, FP8_MAX).astype(jnp.float8_e4m3fn)
        key = jax.random.key(seed)
        kx, kw = jax.random.split(key)
        x = jax.random.normal(kx, (8, 512, K), dtype=jnp.float32)
        weight = jax.random.normal(kw, (K, N), dtype=jnp.float32) * 0.02
        return {'x': x, 'weight': weight}
    _L1_ffn_all = _L1_ffn_setup()
    _L1_ffn_in = {k: v for k, v in _L1_ffn_all.items() if k in ('weight',)}
    del _L1_ffn_all
    return {'x': x, 'ctx_4096': ctx_4096, 'g_xattn': g_xattn, 'g_ffn': g_ffn, 'L0_xattn_wq': _L0_xattn_in['wq'], 'L0_xattn_wk': _L0_xattn_in['wk'], 'L0_xattn_wv': _L0_xattn_in['wv'], 'L0_xattn_wo': _L0_xattn_in['wo'], 'L0_xattn_ln_w': _L0_xattn_in['ln_w'], 'L0_ffn_W_base': _L0_ffn_in['W_base'], 'L0_ffn_b_base': _L0_ffn_in['b_base'], 'L0_ffn_enc0': _L0_ffn_in['enc0'], 'L0_ffn_enc1': _L0_ffn_in['enc1'], 'L0_ffn_coefs0': _L0_ffn_in['coefs0'], 'L0_ffn_coefs1': _L0_ffn_in['coefs1'], 'L0_ffn_mask0': _L0_ffn_in['mask0'], 'L0_ffn_mask1': _L0_ffn_in['mask1'], 'L1_xattn_Wq': _L1_xattn_in['Wq'], 'L1_xattn_bq': _L1_xattn_in['bq'], 'L1_xattn_Wk': _L1_xattn_in['Wk'], 'L1_xattn_bk': _L1_xattn_in['bk'], 'L1_xattn_Wv': _L1_xattn_in['Wv'], 'L1_xattn_bv': _L1_xattn_in['bv'], 'L1_xattn_proj_k': _L1_xattn_in['proj_k'], 'L1_xattn_proj_v': _L1_xattn_in['proj_v'], 'L1_xattn_Wm': _L1_xattn_in['Wm'], 'L1_xattn_bm': _L1_xattn_in['bm'], 'L1_ffn_weight': _L1_ffn_in['weight']}

def reference(x, ctx_4096, g_xattn, g_ffn, L0_xattn_wq, L0_xattn_wk, L0_xattn_wv, L0_xattn_wo, L0_xattn_ln_w, L0_ffn_W_base, L0_ffn_b_base, L0_ffn_enc0, L0_ffn_enc1, L0_ffn_coefs0, L0_ffn_coefs1, L0_ffn_mask0, L0_ffn_mask1, L1_xattn_Wq, L1_xattn_bq, L1_xattn_Wk, L1_xattn_bk, L1_xattn_Wv, L1_xattn_bv, L1_xattn_proj_k, L1_xattn_proj_v, L1_xattn_Wm, L1_xattn_bm, L1_ffn_weight):
    import jax
    import jax.numpy as jnp

    def _L0_xattn_ref(hidden_states, encoder_hidden_states, wq, wk, wv, wo, ln_w):
        import jax, jax.numpy as jnp
        import numpy as np
        HIDDEN = 1024
        N_HEADS = 32
        N_KV_HEADS = 8
        HEAD_DIM = HIDDEN // N_HEADS
        N_REP = N_HEADS // N_KV_HEADS
        EPS = 1e-05

        def _rmsnorm(x, w):
            xf = x.astype(jnp.float32)
            var = jnp.mean(xf * xf, axis=-1, keepdims=True)
            return (xf * jax.lax.rsqrt(var + EPS)).astype(x.dtype) * w
        B, Qlen, _ = hidden_states.shape
        _, Klen, _ = encoder_hidden_states.shape
        x = _rmsnorm(hidden_states, ln_w)
        q = jnp.einsum('bqd,hd->bqh', x, wq).reshape(B, Qlen, N_HEADS, HEAD_DIM)
        k = jnp.einsum('bkd,hd->bkh', encoder_hidden_states, wk).reshape(B, Klen, N_KV_HEADS, HEAD_DIM)
        v = jnp.einsum('bkd,hd->bkh', encoder_hidden_states, wv).reshape(B, Klen, N_KV_HEADS, HEAD_DIM)
        q = q.transpose(0, 2, 1, 3)
        k = k.transpose(0, 2, 1, 3)
        v = v.transpose(0, 2, 1, 3)
        k = jnp.repeat(k, N_REP, axis=1)
        v = jnp.repeat(v, N_REP, axis=1)
        scores = jnp.einsum('bhqd,bhkd->bhqk', q, k) / np.sqrt(HEAD_DIM).astype(np.float32)
        attn = jax.nn.softmax(scores.astype(jnp.float32), axis=-1).astype(q.dtype)
        out = jnp.einsum('bhqk,bhkd->bhqd', attn, v)
        out = out.transpose(0, 2, 1, 3).reshape(B, Qlen, HIDDEN)
        return jnp.einsum('bqh,dh->bqd', out, wo)

    def _L0_ffn_ref(x, W_base, b_base, enc0, enc1, coefs0, coefs1, mask0, mask1):
        import math
        import jax, jax.numpy as jnp
        import numpy as np
        SCALING = 16.0 / 32.0

        def real_fourier_orthogonal_multiply(c):
            n = c.shape[-1]
            sqrt_n = math.sqrt(n)
            pair_scale = math.sqrt(n / 2.0)
            max_f = (n - 1) // 2
            work = c.astype(jnp.float32)
            dc = (work[..., 0] * sqrt_n)[..., None].astype(jnp.complex64)
            cos = work[..., 1:1 + 2 * max_f:2] * pair_scale
            sin = work[..., 2:2 + 2 * max_f:2] * pair_scale
            mid = (cos - 1j * sin).astype(jnp.complex64)
            parts = [dc, mid]
            if n % 2 == 0:
                parts.append((work[..., -1] * sqrt_n)[..., None].astype(jnp.complex64))
            spectrum = jnp.concatenate(parts, axis=-1)
            return jnp.fft.irfft(spectrum, n=n, axis=-1).astype(c.dtype)
        base = jnp.einsum('bsd,od->bso', x, W_base) + b_base
        e0 = jnp.einsum('bsd,rd->bsr', x, enc0)
        e1 = jnp.einsum('bsd,rd->bsr', x, enc1)
        w0 = coefs0 * mask0.astype(coefs0.dtype)
        w1 = coefs1 * mask1.astype(coefs1.dtype)
        decoded = jnp.einsum('bsr,eor->ebso', e0, w0) + jnp.einsum('bsr,eor->ebso', e1, w1)
        transformed = real_fourier_orthogonal_multiply(decoded)
        update = transformed.sum(axis=0)
        return base + update * SCALING

    def _L1_xattn_ref(query, key, value, Wq, bq, Wk, bk, Wv, bv, proj_k, proj_v, Wm, bm):
        import jax, jax.numpy as jnp
        import numpy as np
        B, D, N, H, K = (4, 256, 1024, 16, 64)
        HD = D // H

        def _conv1x1(x, W, b):
            return jnp.einsum('od,bdn->bon', W, x) + b[None, :, None]
        b = query.shape[0]
        q = _conv1x1(query, Wq, bq)
        k = _conv1x1(key, Wk, bk)
        v = _conv1x1(value, Wv, bv)
        k = jnp.einsum('bdn,nk->bdk', k, proj_k)
        v = jnp.einsum('bdn,nk->bdk', v, proj_v)
        q = q.reshape(b, HD, H, -1)
        k = k.reshape(b, HD, H, -1)
        v = v.reshape(b, HD, H, -1)
        scores = jnp.einsum('bdhn,bdhk->bhnk', q, k) / HD ** 0.5
        prob = jax.nn.softmax(scores, axis=-1)
        x = jnp.einsum('bhnk,bdhk->bdhn', prob, v)
        return _conv1x1(x.reshape(b, HD * H, -1), Wm, bm)

    def _L1_ffn_ref(x, weight):
        import jax, jax.numpy as jnp
        import numpy as np
        FP8_MAX = 448.0
        K = 1024
        N = 1024

        def _compute_scale(t):
            amax = jnp.max(jnp.abs(t))
            return FP8_MAX / jnp.maximum(amax, 1e-12)

        def _quantize_fp8(t, scale):
            return jnp.clip(t * scale, -FP8_MAX, FP8_MAX).astype(jnp.float8_e4m3fn)
        B, S, _ = x.shape
        x2 = x.reshape(-1, K)
        x_scale = _compute_scale(x2)
        w_scale = _compute_scale(weight)
        x_fp8 = _quantize_fp8(x2, x_scale)
        w_fp8 = _quantize_fp8(weight.T, w_scale)
        out = jnp.matmul(x_fp8.astype(jnp.float32), w_fp8.T.astype(jnp.float32))
        out = out * (1.0 / x_scale * (1.0 / w_scale))
        return out.reshape(B, S, N)
    x = x + jnp.tanh(g_xattn[0]) * _L0_xattn_ref(_layernorm(x, axis=-1), ctx_4096, L0_xattn_wq, L0_xattn_wk, L0_xattn_wv, L0_xattn_wo, L0_xattn_ln_w)
    x = x + jnp.tanh(g_ffn[0]) * _L0_ffn_ref(_layernorm(x, axis=-1), L0_ffn_W_base, L0_ffn_b_base, L0_ffn_enc0, L0_ffn_enc1, L0_ffn_coefs0, L0_ffn_coefs1, L0_ffn_mask0, L0_ffn_mask1)
    x = x + jnp.tanh(g_xattn[1]) * _L1_xattn_ref(_layernorm(x, axis=-1), ctx_4096, ctx_4096, L1_xattn_Wq, L1_xattn_bq, L1_xattn_Wk, L1_xattn_bk, L1_xattn_Wv, L1_xattn_bv, L1_xattn_proj_k, L1_xattn_proj_v, L1_xattn_Wm, L1_xattn_bm)
    x = x + jnp.tanh(g_ffn[1]) * _L1_ffn_ref(_layernorm(x, axis=-1), L1_ffn_weight)
    return x

_drawn_inputs = setup_inputs


def setup_inputs(seed=0):
    import zlib

    import numpy as np

    out = dict(_drawn_inputs(seed))
    spreads = {'g_ffn': (-1.0, 0.2), 'L0_xattn_ln_w': (1.0, 0.6)}
    factors = {'L0_ffn_b_base': 4.465,
     'L0_ffn_enc1': 4.14,
     'L0_ffn_coefs1': 4.192,
     'L1_xattn_bq': 8.0,
     'L1_xattn_bk': 8.0,
     'L1_xattn_bv': 8.0}
    for name, (base, spread) in spreads.items():
        noise = np.random.default_rng([zlib.crc32(name.encode()), seed]).standard_normal(out[name].shape)
        drawn = base * np.exp(spread * noise) if base else spread * noise
        out[name] = jnp.asarray(drawn.astype(out[name].dtype))
    for name, factor in factors.items():
        out[name] = (out[name] * factor).astype(out[name].dtype)
    return out
```

```python
from contextlib import ExitStack

import numpy as np
import concourse.bass as bass
from concourse import mybir

F32 = mybir.dt.float32
F32R = mybir.dt.float32r
BF16 = mybir.dt.bfloat16
U8 = mybir.dt.uint8
U32 = mybir.dt.uint32
ALU = mybir.AluOpType
ACT = mybir.ActivationFunctionType
AX_X = mybir.AxisListType.X
ABSMAX = bass.bass_isa.ReduceOp.absmax

P = 128
B, S, D = 8, 256, 1024
TT = S // P
KT = D // P
PAIRS = B // 2
HD0, NH0, NKV0 = 32, 32, 8
KV0 = NKV0 * HD0
HALF0 = KV0 // P
REP0 = NH0 // NKV0
JH0 = P // HD0
HD1, NH1, NK1 = 16, 16, 64
HT1 = P // HD1
CT1 = S // P
R0, R1, NE = 32, 8, 3
RR = R0 + R1
LN_EPS = 1e-5
FP8_MAX = 448.0
HALF_N = 512


def identity(nc, ident, done):
    nc.gpsimd.memset(ident[:, :], 0.0).then_inc(done, 1)
    nc.gpsimd.wait_ge(done, 1)
    nc.gpsimd.affine_select(out=ident[:, :], in_=ident[:, :], compare_op=ALU.not_equal, fill=1.0, base=0,
                            pattern=[[-1, P]], channel_multiplier=1).then_inc(done, 1)


def hold(engine, sh):
    engine.sem_inc(sh.held, 1)


class Shared:
    pass


def setup_stage(nc, ctx, g_xattn, g_ffn):
    sh = Shared()
    sh.ident = ctx.enter_context(nc.sbuf_tensor("ident", [P, P], F32))
    sh.gates = ctx.enter_context(nc.sbuf_tensor("gates", [P, 4], F32))
    sh.gate_raw = ctx.enter_context(nc.sbuf_tensor("gate_raw", [P, 4], F32))
    sh.minus_half = ctx.enter_context(nc.sbuf_tensor("minus_half", [P, 4], F32))
    sh.ident_done = ctx.enter_context(nc.semaphore("ident_done"))
    sh.held = ctx.enter_context(nc.semaphore("held"))
    sh.gates_loaded = ctx.enter_context(nc.semaphore("gates_loaded"))
    with nc.Block() as block:
        @block.sync
        def _(sp):
            sp.dma_start(sh.gate_raw[:, 0:2], g_xattn.partition_broadcast(P)).then_inc(sh.gates_loaded, 16)
            sp.dma_start(sh.gate_raw[:, 2:4], g_ffn.partition_broadcast(P)).then_inc(sh.gates_loaded, 16)

        @block.gpsimd
        def _(pool):
            identity(nc, sh.ident, sh.ident_done)
            nc.gpsimd.memset(sh.minus_half[:, :], -0.5)

        @block.scalar
        def _(act):
            act.wait_ge(sh.gates_loaded, 32)
            nc.scalar.activation(sh.gates[:, :], sh.gate_raw[:, :], ACT.Tanh)
    return sh


def context_stage(nc, sh, c, scratch):
    ident = sh.ident
    CV = KV0 + 3 * NK1
    with ExitStack() as es:
        def sb(name, shape, dt=F32):
            return es.enter_context(nc.sbuf_tensor("c_" + name, shape, dt))

        def sem(name):
            return es.enter_context(nc.semaphore("c_" + name))

        raw = sb("raw", [P, 2, D])
        raw1 = sb("raw1", [P, 2, 2, S])
        wkT = sb("wkT", [P, KT, KV0])
        wvpT = sb("wvpT", [P, KT, CV])
        w1T = sb("w1T", [P, 2, TT, S])
        rows1 = sb("rows1", [1, 2, S])
        rows1h = sb("rows1h", [1, 2, S])
        ones = sb("ones", [P, 1])
        colsum = sb("colsum", [1, 3 * NK1])
        bias_k = sb("bias_k", [P, CT1, NK1])
        bias_v = sb("bias_v", [P, S])
        nat = sb("nat", [P, 2, TT, D])
        cT = sb("cT", [P, 2, KT, S])
        k0 = sb("k0", [P, 2, HALF0, S])
        v0 = sb("v0", [P, 2, TT, KV0])
        mid = sb("mid", [P, 2, TT, 3 * NK1])
        k1 = sb("k1", [P, 2, CT1, NK1])
        v1 = sb("v1", [P, 2, NH1 // 2, 2 * HD1])
        psT = es.enter_context(nc.psum_tensor("c_psT", [P, 2, HALF_N], F32))
        psP = es.enter_context(nc.psum_tensor("c_psP", [P, 4, HALF_N], F32))
        psL = es.enter_context(nc.psum_tensor("c_psL", [P, HALF_N], F32))

        raw_loaded = [sem(f"raw_loaded{n}") for n in range(2 * HALF0)]
        raw1_loaded, small_loaded, proj_loaded = sem("raw1_loaded"), sem("small_loaded"), sem("proj_loaded")
        wT_full, wT_copied = sem("wT_full"), sem("wT_copied")
        preset = sem("preset")
        colsum_full, colsum_copied = sem("colsum_full"), sem("colsum_copied")
        bias_full, bias_copied = sem("bias_full"), sem("bias_copied")
        nat_loaded = [sem(f"nat_loaded{u}") for u in range(2)]
        psT_full = [sem(f"psT_full{p}") for p in range(2)]
        cT_dve, cT_act = sem("cT_dve"), sem("cT_act")
        psP_full, mid_ready = sem("psP_full"), sem("mid_ready")
        psL_full = sem("psL_full")
        out_act = [sem(f"out_act{u}") for u in range(2)]
        out_dve = [sem(f"out_dve{u}") for u in range(2)]
        out_stored = [sem(f"out_stored{u}") for u in range(2)]

        block = es.enter_context(nc.Block())

        blocks = [(c["wk"], n) for n in range(HALF0)] + [(c["wv"], n) for n in range(HALF0)]

        @block.sync
        def _(sp):
            def load_ctx(b, u):
                sp.dma_start(nat[:, u, :, :],
                             c["ctx"][bass.ds(b, 1)].rearrange("b (t p) d -> p (b t) d", p=P)
                             ).then_inc(nat_loaded[u], 16)

            for n, (w, rb) in enumerate(blocks):
                if n >= 2:
                    sp.wait_ge(wT_full, 2 * (n - 1))
                sp.dma_start(raw[:, n % 2, :], w[rb * P:(rb + 1) * P, :]).then_inc(raw_loaded[n], 16)
            for m, name in enumerate(("Wk1", "Wv1")):
                sp.dma_start(raw1[:, m, :, :], c[name].rearrange("(t p) d -> p t d", p=P)).then_inc(raw1_loaded, 16)
            for m, name in enumerate(("bk1", "bv1")):
                sp.dma_start(rows1[0:1, m, :], c[name].rearrange("(a d) -> a d", a=1)).then_inc(small_loaded, 16)
            for m, name in enumerate(("proj_k", "proj_v", "proj_v")):
                lo = KV0 + m * NK1
                sp.dma_start(wvpT[:, :, lo:lo + NK1],
                             c[name].rearrange("(t p) k -> p t k", p=P)).then_inc(proj_loaded, 16)
            def store(i):
                for u in range(2):
                    sp.wait_ge(out_act[u], 4 * i + 5)
                    sp.wait_ge(out_dve[u], 2 * i + 3)
                    for name, tile in (("k0", k0), ("v0", v0), ("k1", k1), ("v1", v1)):
                        sp.dma_start(scratch[name][bass.ds(2 * i + u, 1)].rearrange("b p n -> p (b n)"),
                                     tile[:, u].rearrange("p a n -> p (a n)")).then_inc(out_stored[u], 16)

            for u in range(2):
                sp.sem_inc(out_stored[u], 1)
                load_ctx(u, u)
            with sp.Fori(1, PAIRS) as i:
                for u in range(2):
                    sp.wait_ge(cT_dve, 4 * i + 2 * u - 1)
                    sp.wait_ge(cT_act, 4 * i + 2 * u - 1)
                    load_ctx(2 * i + u, u)
                store(i - 1)
            store(PAIRS - 1)
            for u in range(2):
                sp.wait_ge(out_stored[u], 64 * PAIRS + 1)

        @block.gpsimd
        def _(pool):
            nc.gpsimd.memset(ones[:, :], 1.0).then_inc(preset, 1)
            nc.gpsimd.memset(v1[:, :, :, :], 0.0).then_inc(preset, 1)

        @block.tensor
        def _(pe):
            for n in range(len(blocks)):
                pe.wait_ge(raw_loaded[n], 16)
                for half in range(2):
                    if n:
                        pe.wait_ge(wT_copied, 2 * n + half - 1)
                    for q in range(4):
                        kt = 4 * half + q
                        last = nc.tensor.transpose(psT[:, half, q * P:(q + 1) * P],
                                                   raw[:, n % 2, kt * P:(kt + 1) * P], ident[:, :])
                    last.then_inc(wT_full, 1)
            n0 = 2 * len(blocks)
            pe.wait_ge(raw1_loaded, 32)
            for m in range(2):
                pe.wait_ge(wT_copied, n0 + m - 1)
                for t in range(TT):
                    for ot in range(TT):
                        last = nc.tensor.transpose(psT[:, m, t * S + ot * P:t * S + (ot + 1) * P],
                                                   raw1[:, m, ot, t * P:(t + 1) * P], ident[:, :])
                last.then_inc(wT_full, 1)
            pe.wait_ge(preset, 1)
            pe.wait_ge(proj_loaded, 48)
            for kt in range(KT):
                last = nc.tensor.matmul(psL[0:1, 0:3 * NK1], ones[:, 0:1], wvpT[:, kt, KV0:CV],
                                        start=(kt == 0), stop=(kt == KT - 1))
            last.then_inc(colsum_full, 1)
            pe.wait_ge(colsum_copied, 1)
            for t in range(CT1):
                nc.tensor.matmul(psP[:, t, 0:NK1], rows1h[0:1, 0, t * P:(t + 1) * P], colsum[0:1, 0:NK1],
                                 start=True, stop=True)
            nc.tensor.matmul(psP[:, 2, 0:S], colsum[0:1, NK1:3 * NK1], rows1h[0:1, 1, :],
                             start=True, stop=True).then_inc(bias_full, 1)
            pe.wait_ge(bias_copied, 1)
            pe.wait_ge(wT_copied, n0 + 2)
            with pe.Fori(0, PAIRS) as i:
                for u in range(2):
                    b = 2 * i + u
                    pe.wait_ge(nat_loaded[u], 16 * i + 16)
                    for n in range(4):
                        pe.wait_ge((cT_dve, cT_act)[n % 2], 4 * i + 2 * u + n // 2 + 1)
                        for q in range(2):
                            for t in range(TT):
                                kt = 2 * n + q
                                last = nc.tensor.transpose(psT[:, n % 2, (q * TT + t) * P:(q * TT + t + 1) * P],
                                                           nat[:, u, t, kt * P:(kt + 1) * P], ident[:, :])
                        last.then_inc(psT_full[n % 2], 1)
                    pe.wait_ge(cT_dve, 4 * i + 2 * u + 3)
                    pe.wait_ge(cT_act, 4 * i + 2 * u + 3)
                    pe.wait_ge(out_act[1 - u], 4 * i + 4 * u + 1)
                    pe.wait_ge(out_dve[1 - u], 2 * i + 2 * u + 1)
                    for half in range(HALF0):
                        for kt in range(KT):
                            last = nc.tensor.matmul(psP[:, half, 0:S], wkT[:, kt, half * P:(half + 1) * P],
                                                    cT[:, u, kt, :], start=(kt == 0), stop=(kt == KT - 1))
                        last.then_inc(psP_full, 1)
                    for t in range(TT):
                        for kt in range(KT):
                            last = nc.tensor.matmul(psP[:, 2 + t, 0:CV], cT[:, u, kt, t * P:(t + 1) * P],
                                                    wvpT[:, kt, :], start=(kt == 0), stop=(kt == KT - 1))
                        last.then_inc(psP_full, 1)
                    pe.wait_ge(mid_ready, 4 * i + 2 * u + 2)
                    for ct in range(CT1):
                        for t in range(TT):
                            nc.tensor.matmul(psL[:, ct * NK1:(ct + 1) * NK1], w1T[:, 0, t, ct * P:(ct + 1) * P],
                                             mid[:, u, t, 0:NK1], start=(t == 0), stop=(t == TT - 1))
                    for t in range(TT):
                        last = nc.tensor.matmul(psL[:, P:P + S], mid[:, u, t, NK1:3 * NK1], w1T[:, 1, t, :],
                                                start=(t == 0), stop=(t == TT - 1))
                    last.then_inc(psL_full, 1)

        @block.vector
        def _(dve):
            dve.sem_inc(cT_dve, 1)
            for u in range(2):
                dve.sem_inc(out_dve[u], 1)
            for n in range(len(blocks)):
                for half in range(2):
                    dve.wait_ge(wT_full, 2 * n + half + 1)
                    dst = wkT[:, 4 * half:4 * half + 4, n * P:(n + 1) * P] if n < HALF0 else \
                        wvpT[:, 4 * half:4 * half + 4, (n - HALF0) * P:(n - HALF0 + 1) * P]
                    nc.vector.tensor_copy(dst, psT[:, half, :].rearrange("p (k n) -> p k n", k=4)).then_inc(wT_copied, 1)
            for m in range(2):
                dve.wait_ge(wT_full, 2 * len(blocks) + m + 1)
                for t in range(TT):
                    last = nc.vector.tensor_copy(w1T[:, m, t, :].rearrange("p (h c) -> p h c", h=NH1),
                                                 psT[:, m, t * S:(t + 1) * S].rearrange("p (c h) -> p h c", h=NH1))
                last.then_inc(wT_copied, 1)
            dve.wait_ge(small_loaded, 32)
            nc.vector.tensor_copy(rows1h[0:1, :, :].rearrange("p m (h c) -> p m h c", h=NH1),
                                  rows1[0:1, :, :].rearrange("p m (c h) -> p m h c", h=NH1))
            dve.wait_ge(colsum_full, 1)
            nc.vector.tensor_copy(colsum[0:1, :], psL[0:1, 0:3 * NK1]).then_inc(colsum_copied, 1)
            dve.wait_ge(bias_full, 1)
            nc.vector.tensor_copy(bias_k[:, :, :], psP[:, 0:CT1, 0:NK1])
            nc.vector.tensor_copy(bias_v[:, :], psP[:, 2, 0:S]).then_inc(bias_copied, 1)
            dve.wait_ge(bias_copied, 1)
            dve.wait_ge(preset, 2)
            with dve.Fori(0, PAIRS) as i:
                for u in range(2):
                    for n in (0, 2):
                        dve.wait_ge(psT_full[0], 4 * i + 2 * u + n // 2 + 1)
                        nc.vector.tensor_copy(cT[:, u, 2 * n:2 * n + 2, :],
                                              psT[:, 0, :].rearrange("p (k n) -> p k n", k=2)).then_inc(cT_dve, 1)
                    for t in range(TT):
                        dve.wait_ge(psP_full, 8 * i + 4 * u + 3 + t)
                        nc.vector.tensor_copy(mid[:, u, t, :], psP[:, 2 + t, KV0:CV]).then_inc(mid_ready, 1)
                    dve.wait_ge(psL_full, 2 * i + u + 1)
                    dve.wait_ge(out_stored[u], 64 * i + 1)
                    nc.vector.tensor_tensor(k1[:, u, :, :], psL[:, 0:P].rearrange("p (t n) -> p t n", t=CT1),
                                            bias_k[:, :, :], ALU.add).then_inc(out_dve[u], 1)
                    for odd in range(2):
                        lo, hi = odd * NK1, (odd + 1) * NK1

                        def heads(a):
                            return a.rearrange("p (m e c) -> p m e c", e=2, c=HD1)[:, :, odd, :]
                        last = nc.vector.tensor_tensor(v1[lo:hi, u, :, odd * HD1:(odd + 1) * HD1],
                                                       heads(psL[lo:hi, P:P + S]), heads(bias_v[lo:hi, :]), ALU.add)
                    last.then_inc(out_dve[u], 1)

        @block.scalar
        def _(act):
            act.sem_inc(cT_act, 1)
            for u in range(2):
                act.sem_inc(out_act[u], 1)
            with act.Fori(0, PAIRS) as i:
                for u in range(2):
                    for n in (1, 3):
                        act.wait_ge(psT_full[1], 4 * i + 2 * u + n // 2 + 1)
                        nc.scalar.copy(cT[:, u, 2 * n:2 * n + 2, :],
                                       psT[:, 1, :].rearrange("p (k n) -> p k n", k=2)).then_inc(cT_act, 1)
                    act.wait_ge(out_stored[u], 64 * i + 1)
                    for half in range(HALF0):
                        act.wait_ge(psP_full, 8 * i + 4 * u + 1 + half)
                        nc.scalar.mul(k0[:, u, half, :], psP[:, half, 0:S], HD0 ** -0.5).then_inc(out_act[u], 1)
                    for t in range(TT):
                        act.wait_ge(mid_ready, 4 * i + 2 * u + 1 + t)
                        nc.scalar.copy(v0[:, u, t, :], psP[:, 2 + t, 0:KV0]).then_inc(out_act[u], 1)


class Norm:

    def __init__(self, nc, es, name, sh):
        def sb(n, shape):
            return es.enter_context(nc.sbuf_tensor(f"{name}_{n}", shape, F32))

        def sem(n):
            return es.enter_context(nc.semaphore(f"{name}_{n}"))
        self.nc, self.sh = nc, sh
        self.stats = sb("stats", [P, TT, 2, 6])
        self.moments = sb("moments", [P, TT, 2])
        self.tmp = sb("tmp", [P, 4, TT])
        self.rstd = sb("rstd", [P, TT])
        self.stats_done = sem("stats_done")
        self.moments_done = sem("moments_done")
        self.rstd_steps = sem("rstd_steps")
        self.normed = sem("normed")

    def moments_of(self, dve, b, x):
        nc = self.nc
        for t in range(TT):
            for h in range(2):
                last = nc.vector.bn_stats(self.stats[:, t, h, :], x[:, t, h * HALF_N:(h + 1) * HALF_N])
        last.then_inc(self.stats_done, 1)
        dve.wait_ge(self.stats_done, b + 1)
        hold(dve, self.sh)
        for t in range(TT):
            last = nc.vector.bn_aggr(self.moments[:, t, :], self.stats[:, t, :, :])
        last.then_inc(self.moments_done, 1)

    STEPS, STEPS_RMS = 2, 6

    def rstd_of(self, pool, b, rms):
        nc, tmp = self.nc, self.tmp
        steps = self.STEPS_RMS if rms else self.STEPS
        var, half = self.moments[:, :, 1], self.sh.minus_half[:, 0:TT]
        done = [0]

        def step(instruction):
            instruction.then_inc(self.rstd_steps, 1)
            done[0] += 1
            pool.wait_ge(self.rstd_steps, steps * b + done[0])
        pool.wait_ge(self.moments_done, b + 1)
        hold(pool, self.sh)
        step(nc.gpsimd.tensor_scalar(tmp[:, 0, :], var, LN_EPS, None, ALU.add))
        if not rms:
            step(nc.gpsimd.tensor_tensor(self.rstd[:, :], tmp[:, 0, :], half, ALU.pow))
            return
        step(nc.gpsimd.tensor_tensor(tmp[:, 1, :], tmp[:, 0, :], half, ALU.pow))
        step(nc.gpsimd.tensor_tensor(tmp[:, 2, :], tmp[:, 1, :], tmp[:, 1, :], ALU.mult))
        step(nc.gpsimd.tensor_tensor(tmp[:, 3, :], tmp[:, 2, :], var, ALU.mult))
        hold(pool, self.sh)
        step(nc.gpsimd.tensor_scalar(tmp[:, 2, :], tmp[:, 3, :], LN_EPS, None, ALU.add))
        nc.gpsimd.tensor_tensor(tmp[:, 3, :], tmp[:, 2, :], tmp[:, 0, :], ALU.mult).then_inc(self.rstd_mid, 1)
        pool.wait_ge(self.rstd_mid, b + 1)
        step(nc.gpsimd.tensor_tensor(self.rstd[:, :], tmp[:, 3, :], half, ALU.pow))

    def normalise(self, dve, b, x, out, steps):
        dve.wait_ge(self.rstd_steps, steps * b + steps)
        for t in range(TT):
            last = self.nc.vector.tensor_scalar(out[:, t, :], x[:, t, :], self.moments[:, t, 0:1],
                                                self.rstd[:, t:t + 1], ALU.subtract, ALU.mult)
        last.then_inc(self.normed, 1)


def attn0_stage(nc, sh, c, scratch):
    ident = sh.ident
    UNITS = KT * TT
    T_USES = 2 + UNITS
    O_USES = (KT + KT + 2 * TT) // 2
    with ExitStack() as es:
        def sb(name, shape, dt=F32):
            return es.enter_context(nc.sbuf_tensor("a_" + name, shape, dt))

        def sem(name):
            return es.enter_context(nc.semaphore("a_" + name))

        wqT = sb("wqT", [P, KT, D])
        woT = sb("woT", [P, KT, D])
        ln_w = sb("ln_w", [P, KT])
        raw = sb("raw", [P, 2, D])
        raw_perm = sb("raw_perm", [P, 2, D])
        x = sb("x", [P, 2, TT, D])
        xn = sb("xn", [P, TT, D])
        xnT = sb("xnT", [P, KT, S])
        qT = sb("qT", [P, KT, S])
        k0 = sb("k0", [P, 2, HALF0, S])
        kpad = sb("kpad", [P, 2, HALF0, JH0, S])
        v0 = sb("v0", [P, 2, TT, KV0])
        prob = sb("prob", [P, 2, JH0, S])
        probT = sb("probT", [P, 2, TT, JH0, P])
        negmax = sb("negmax", [P, 2, JH0])
        sums = sb("sums", [P, 2, JH0])
        recip = sb("recip", [P, 2, JH0])
        oT = sb("oT", [P, KT, S])
        psS = es.enter_context(nc.psum_tensor("a_psS", [P, 2, JH0 * S], F32))
        psT = es.enter_context(nc.psum_tensor("a_psT", [P, 2, HALF_N], F32))
        psO = es.enter_context(nc.psum_tensor("a_psO", [P, 2, HALF_N], F32))
        norm = Norm(nc, es, "a_norm", sh)
        norm.rstd_mid = sem("rstd_mid")

        lnw_loaded = sem("lnw_loaded")
        raw_loaded = [sem(f"raw_loaded{u}") for u in range(2)]
        perm_done = sem("perm_done")
        w_full = [sem(f"w_full{p}") for p in range(2)]
        w_copied = [sem(f"w_copied{p}") for p in range(2)]
        x_loaded = [sem(f"x_loaded{u}") for u in range(2)]
        kv_loaded = [sem(f"kv_loaded{u}") for u in range(2)]
        x_stored = [sem(f"x_stored{u}") for u in range(2)]
        zeroed = sem("zeroed")
        kpad_ready = [sem(f"kpad_ready{u}") for u in range(2)]
        psT_full = [sem(f"psT_full{p}") for p in range(2)]
        psT_copied = [sem(f"psT_copied{p}") for p in range(2)]
        psO_full = [sem(f"psO_full{p}") for p in range(2)]
        psO_copied = [sem(f"psO_copied{p}") for p in range(2)]
        scores_full, max_ready, exp_done = sem("scores_full"), sem("max_ready"), sem("exp_done")
        recip_ready, prob_ready = sem("recip_ready"), sem("prob_ready")

        block = es.enter_context(nc.Block())
        RB = KT

        @block.sync
        def _(sp):
            sp.dma_start(ln_w[:, :], c["ln_w"].rearrange("(t p) -> p t", p=P),
                         allow_slow_non_contiguous=True).then_inc(lnw_loaded, 16)

            def load_rows(name, rb, u):
                sp.dma_start(raw[:, u, :], c[name][bass.ds(rb * P, P), :]).then_inc(raw_loaded[u], 16)

            for u in range(2):
                load_rows("wq", u, u)
            with sp.Fori(1, RB // 2) as i:
                for u in range(2):
                    sp.wait_ge(w_full[1], 2 * i + u - 1)
                    load_rows("wq", 2 * i + u, u)
            for u in range(2):
                sp.wait_ge(w_full[1], RB - 1 + u)
                load_rows("wo", u, u)
            with sp.Fori(1, RB // 2) as i:
                for u in range(2):
                    sp.wait_ge(perm_done, 2 * i + u - 1)
                    load_rows("wo", 2 * i + u, u)

            def load_batch(b, u):
                sp.dma_start(x[:, u, :, :], c["x"][bass.ds(b, 1)].rearrange("b (t p) d -> p (b t) d", p=P)
                             ).then_inc(x_loaded[u], 16)
                sp.dma_start(k0[:, u].rearrange("p a n -> p (a n)"),
                             scratch["k0"][bass.ds(b, 1)].rearrange("b p n -> p (b n)")).then_inc(kv_loaded[u], 16)
                sp.dma_start(v0[:, u].rearrange("p a n -> p (a n)"),
                             scratch["v0"][bass.ds(b, 1)].rearrange("b p n -> p (b n)")).then_inc(kv_loaded[u], 16)

            def store_batch(i, u):
                for p in range(2):
                    sp.wait_ge(psO_copied[p], O_USES * (2 * i + u + 1) + 1)
                sp.dma_start(scratch["x1"][bass.ds(2 * i + u, 1)].rearrange("b (t p) d -> p (b t) d", p=P),
                             x[:, u, :, :]).then_inc(x_stored[u], 16)

            for u in range(2):
                load_batch(u, u)
            with sp.Fori(1, PAIRS) as i:
                for u in range(2):
                    store_batch(i - 1, u)
                    sp.wait_ge(x_stored[u], 16 * i)
                    load_batch(2 * i + u, u)
            for u in range(2):
                store_batch(PAIRS - 1, u)
                sp.wait_ge(x_stored[u], 16 * PAIRS)

        @block.gpsimd
        def _(pool):
            nc.gpsimd.memset(kpad[:, :, :, :, :], 0.0).then_inc(zeroed, 1)
            pool.wait_ge(zeroed, 1)
            with pool.Fori(0, PAIRS) as i:
                for u in range(2):
                    norm.rstd_of(pool, 2 * i + u, rms=True)
                    pool.wait_ge(kv_loaded[u], 32 * i + 32)
                    for j in range(JH0):
                        rows = slice(j * HD0, (j + 1) * HD0)
                        hold(pool, sh)
                        nc.gpsimd.tensor_copy(kpad[rows, u, :, j, :], k0[rows, u, :, :]).then_inc(kpad_ready[u], 1)
                        pool.wait_ge(kpad_ready[u], JH0 * i + j + 1)

        @block.tensor
        def _(pe):
            def transpose_rows(n, u, src):
                for half in range(2):
                    pe.wait_ge(w_copied[half], n + 1)
                    for q in range(4):
                        kt = 4 * half + q
                        last = nc.tensor.transpose(psT[:, half, q * P:(q + 1) * P],
                                                   src[:, u, kt * P:(kt + 1) * P], ident[:, :])
                    last.then_inc(w_full[half], 1)

            with pe.Fori(0, RB // 2) as i:
                for u in range(2):
                    pe.wait_ge(raw_loaded[u], 16 * i + 16)
                    transpose_rows(2 * i + u, u, raw)
            with pe.Fori(0, RB // 2) as i:
                for u in range(2):
                    pe.wait_ge(perm_done, 2 * i + u + 1)
                    transpose_rows(2 * i + u + RB, u, raw_perm)
            for p in range(2):
                pe.wait_ge(w_copied[p], 2 * RB + 1)

            with pe.Fori(0, PAIRS) as i:
                for u in range(2):
                    b = 2 * i + u
                    pe.wait_ge(norm.normed, b + 1)
                    for n in range(4):
                        pe.wait_ge(psT_copied[n % 2], T_USES * b + n // 2 + 1)
                        for q in range(2):
                            for t in range(TT):
                                kt = 2 * n + q
                                last = nc.tensor.transpose(psT[:, n % 2, (q * TT + t) * P:(q * TT + t + 1) * P],
                                                           xn[:, t, kt * P:(kt + 1) * P], ident[:, :])
                        last.then_inc(psT_full[n % 2], 1)
                    for p in range(2):
                        pe.wait_ge(psT_copied[p], T_USES * b + 3)
                    for t in range(KT):
                        pe.wait_ge(psO_copied[t % 2], O_USES * b + t // 2 + 1)
                        for kt in range(KT):
                            last = nc.tensor.matmul(psO[:, t % 2, 0:S], wqT[:, kt, t * P:(t + 1) * P], xnT[:, kt, :],
                                                    start=(kt == 0), stop=(kt == KT - 1))
                        last.then_inc(psO_full[t % 2], 1)

                    def scores(n):
                        t, qb = n // TT, n % TT
                        if qb == 0:
                            pe.wait_ge(psO_copied[t % 2], O_USES * b + t // 2 + 2)
                        if n == 0:
                            pe.wait_ge(kpad_ready[u], JH0 * i + JH0)
                        for h in range(2):
                            last = nc.tensor.matmul(
                                psS[:, n % 2, h * HALF_N:(h + 1) * HALF_N], qT[:, t, qb * P:(qb + 1) * P],
                                kpad[:, u, t // REP0, 2 * h:2 * h + 2, :].rearrange("p j n -> p (j n)"),
                                start=True, stop=True)
                        last.then_inc(scores_full, 1)

                    def transposes(n):
                        pe.wait_ge(prob_ready, UNITS * b + n + 1)
                        for kt in range(TT):
                            pe.wait_ge(psT_copied[kt], T_USES * b + 2 + n + 1)
                            for j in range(JH0):
                                last = nc.tensor.transpose(psT[:, kt, j * P:(j + 1) * P],
                                                           prob[:, n % 2, j, kt * P:(kt + 1) * P], ident[:, :])
                            last.then_inc(psT_full[kt], 1)

                    def values(n):
                        t, qb = n // TT, n % TT
                        use = KT + t
                        if qb == 0:
                            pe.wait_ge(psO_copied[use % 2], O_USES * b + use // 2 + 1)
                        for kt in range(TT):
                            pe.wait_ge(psT_copied[kt], T_USES * b + 2 + n + 2)
                        for kt in range(TT):
                            for j in range(JH0):
                                head = (t // REP0) * JH0 + j
                                last = nc.tensor.matmul(
                                    psO[j * HD0:(j + 1) * HD0, use % 2, qb * P:(qb + 1) * P],
                                    v0[:, u, kt, head * HD0:(head + 1) * HD0], probT[:, n % 2, kt, j, :],
                                    start=(kt == 0), stop=(kt == TT - 1))
                        if qb == TT - 1:
                            last.then_inc(psO_full[use % 2], 1)

                    scores(0)
                    scores(1)
                    for n in range(UNITS):
                        transposes(n)
                        if n + 2 < UNITS:
                            scores(n + 2)
                        if n:
                            values(n - 1)
                    values(UNITS - 1)
                    for p in range(2):
                        pe.wait_ge(psO_copied[p], O_USES * b + KT + 1)
                    for m in range(2 * TT):
                        t, h = m // 2, m % 2
                        pe.wait_ge(psO_copied[h], O_USES * b + KT + t + 1)
                        for kt in range(KT):
                            last = nc.tensor.matmul(psO[:, h, :], oT[:, kt, t * P:(t + 1) * P],
                                                    woT[:, kt, h * HALF_N:(h + 1) * HALF_N],
                                                    start=(kt == 0), stop=(kt == KT - 1))
                        last.then_inc(psO_full[h], 1)

        @block.vector
        def _(dve):
            dve.sem_inc(w_copied[0], 1)
            dve.sem_inc(psT_copied[0], 1)
            dve.sem_inc(psO_copied[0], 1)
            dve.wait_ge(lnw_loaded, 16)
            with dve.Fori(0, HALF0) as half:
                for j in range(JH0):
                    dve.wait_ge(w_full[0], JH0 * half + j + 1)
                    for q in range(4):
                        dst = wqT[:, q, bass.ds(half * HALF_N, HALF_N)].rearrange("p (r j c) -> p r j c", r=REP0, j=JH0)
                        last = nc.vector.tensor_scalar(dst[:, :, j, :],
                                                       psT[:, 0, q * P:(q + 1) * P].rearrange("p (r c) -> p r c", r=REP0),
                                                       ln_w[:, q:q + 1], None, ALU.mult)
                    last.then_inc(w_copied[0], 1)
            with dve.Fori(0, RB) as rb:
                dve.wait_ge(w_full[0], rb + RB + 1)
                nc.vector.tensor_copy(woT[:, 0:4, bass.ds(rb * P, P)],
                                      psT[:, 0, :].rearrange("p (k n) -> p k n", k=4)).then_inc(w_copied[0], 1)

            def load_moments(b, i, u):
                dve.wait_ge(x_loaded[u], 16 * i + 16)
                norm.moments_of(dve, b, x[:, u])

            load_moments(0, 0, 0)
            norm.normalise(dve, 0, x[:, 0], xn, norm.STEPS_RMS)

            def body(i, final):
                for u in range(2):
                    b = 2 * i + u
                    for n in (0, 2):
                        dve.wait_ge(psT_full[0], T_USES * b + n // 2 + 1)
                        nc.vector.tensor_copy(xnT[:, 2 * n:2 * n + 2, :],
                                              psT[:, 0, :].rearrange("p (k n) -> p k n", k=2)).then_inc(psT_copied[0], 1)
                    for t in range(0, KT, 2):
                        dve.wait_ge(psO_full[0], O_USES * b + t // 2 + 1)
                        nc.vector.tensor_copy(qT[:, t, :], psO[:, 0, 0:S]).then_inc(psO_copied[0], 1)

                    def maximum(n):
                        dve.wait_ge(scores_full, UNITS * b + n + 1)
                        nc.vector.tensor_reduce(negmax[:, n % 2, :], psS[:, n % 2, :].rearrange("p (j k) -> p j k", j=JH0),
                                                AX_X, ALU.max, negate=True).then_inc(max_ready, 1)

                    def copy_o(t):
                        dve.wait_ge(psO_full[0], O_USES * b + (KT + t) // 2 + 1)
                        nc.vector.tensor_copy(oT[:, t, :], psO[:, 0, 0:S]).then_inc(psO_copied[0], 1)

                    maximum(0)
                    maximum(1)
                    for n in range(UNITS):
                        dve.wait_ge(exp_done, UNITS * b + n + 1)
                        nc.vector.reciprocal(recip[:, n % 2, :], sums[:, n % 2, :]).then_inc(recip_ready, 1)
                        dve.wait_ge(recip_ready, UNITS * b + n + 1)
                        for j in range(JH0):
                            last = nc.vector.tensor_scalar(prob[:, n % 2, j, :], prob[:, n % 2, j, :],
                                                           recip[:, n % 2, j:j + 1], None, ALU.mult)
                        last.then_inc(prob_ready, 1)
                        dve.wait_ge(psT_full[0], T_USES * b + 2 + n + 1)
                        nc.vector.tensor_copy(probT[:, n % 2, 0, :, :],
                                              psT[:, 0, :].rearrange("p (j q) -> p j q", j=JH0)).then_inc(psT_copied[0], 1)
                        if n + 2 < UNITS:
                            maximum(n + 2)
                        t = (n - 3) // 2
                        if n >= 3 and n % 2 and t % 2 == 0:
                            copy_o(t)
                        if n in (3, 7) and not (final and u == 1):
                            if n == 3:
                                load_moments(b + 1, i + u, 1 - u)
                            else:
                                norm.normalise(dve, b + 1, x[:, 1 - u], xn, norm.STEPS_RMS)
                    for m in range(2 * TT):
                        t, h = m // 2, m % 2
                        dve.wait_ge(psO_full[h], O_USES * b + KT + t + 1)
                        cols = slice(h * HALF_N, (h + 1) * HALF_N)
                        nc.vector.scalar_tensor_tensor(x[:, u, t, cols], psO[:, h, :], sh.gates[:, 0:1], x[:, u, t, cols],
                                                       op0=ALU.mult, op1=ALU.add).then_inc(psO_copied[h], 1)

            with dve.Fori(0, PAIRS - 1) as i:
                body(i, False)
            body(PAIRS - 1, True)

        @block.scalar
        def _(act):
            act.sem_inc(w_copied[1], 1)
            act.sem_inc(psT_copied[1], 1)
            act.sem_inc(psO_copied[1], 1)
            act.wait_ge(lnw_loaded, 16)
            with act.Fori(0, HALF0) as half:
                for j in range(JH0):
                    act.wait_ge(w_full[1], JH0 * half + j + 1)
                    for q in range(4):
                        dst = wqT[:, 4 + q, bass.ds(half * HALF_N, HALF_N)].rearrange("p (r j c) -> p r j c", r=REP0, j=JH0)
                        last = nc.scalar.mul(dst[:, :, j, :],
                                             psT[:, 1, q * P:(q + 1) * P].rearrange("p (r c) -> p r c", r=REP0),
                                             ln_w[:, 4 + q:5 + q])
                    last.then_inc(w_copied[1], 1)

            def permute(i, u):
                act.wait_ge(raw_loaded[u], 16 * i + 16 * (RB // 2) + 16)
                for half in range(HALF0):
                    cols = slice(half * HALF_N, (half + 1) * HALF_N)
                    last = nc.scalar.copy(raw_perm[:, u, cols].rearrange("p (r j c) -> p r j c", r=REP0, j=JH0),
                                          raw[:, u, cols].rearrange("p (j r c) -> p r j c", r=REP0, j=JH0))
                last.then_inc(perm_done, 1)

            with act.Fori(0, RB // 2) as i:
                for u in range(2):
                    permute(i, u)
                for u in range(2):
                    act.wait_ge(w_full[1], 2 * i + u + RB + 1)
                    nc.scalar.copy(woT[:, 4:8, bass.ds((2 * i + u) * P, P)],
                                   psT[:, 1, :].rearrange("p (k n) -> p k n", k=4)).then_inc(w_copied[1], 1)

            with act.Fori(0, PAIRS) as i:
                for u in range(2):
                    b = 2 * i + u
                    for n in (1, 3):
                        act.wait_ge(psT_full[1], T_USES * b + n // 2 + 1)
                        nc.scalar.copy(xnT[:, 2 * n:2 * n + 2, :],
                                       psT[:, 1, :].rearrange("p (k n) -> p k n", k=2)).then_inc(psT_copied[1], 1)
                    for t in range(1, KT, 2):
                        act.wait_ge(psO_full[1], O_USES * b + t // 2 + 1)
                        nc.scalar.copy(qT[:, t, :], psO[:, 1, 0:S]).then_inc(psO_copied[1], 1)

                    def exponentials(n):
                        act.wait_ge(max_ready, UNITS * b + n + 1)
                        for j in range(JH0):
                            last = nc.scalar.activation(prob[:, n % 2, j, :], psS[:, n % 2, j * S:(j + 1) * S], ACT.Exp,
                                                        bias=negmax[:, n % 2, j:j + 1], accum_out=sums[:, n % 2, j:j + 1])
                        last.then_inc(exp_done, 1)

                    def copy_o(t):
                        act.wait_ge(psO_full[1], O_USES * b + (KT + t) // 2 + 1)
                        nc.scalar.copy(oT[:, t, :], psO[:, 1, 0:S]).then_inc(psO_copied[1], 1)

                    exponentials(0)
                    exponentials(1)
                    for n in range(UNITS):
                        act.wait_ge(psT_full[1], T_USES * b + 2 + n + 1)
                        nc.scalar.copy(probT[:, n % 2, 1, :, :],
                                       psT[:, 1, :].rearrange("p (j q) -> p j q", j=JH0)).then_inc(psT_copied[1], 1)
                        if n + 2 < UNITS:
                            exponentials(n + 2)
                        t = (n - 3) // 2
                        if n >= 3 and n % 2 and t % 2 == 1:
                            copy_o(t)
                    copy_o(KT - 1)


def plain(tile):
    return tile.bitcast(F32)


def ffn0_stage(nc, sh, c, scratch):
    ident = sh.ident
    with ExitStack() as es:
        def sb(name, shape, dt=F32):
            return es.enter_context(nc.sbuf_tensor("f_" + name, shape, dt))

        def sem(name):
            return es.enter_context(nc.semaphore("f_" + name))

        coefs = sb("coefs", [P, NE, KT, RR])
        masks = sb("masks", [P, NE, KT, RR], U8)
        masked = sb("masked", [P, NE, KT, RR])
        wsum = sb("wsum", [P, KT, RR])
        table = sb("table", [P, KT, D])
        update = sb("update", [P, D])
        enc = sb("enc", [P, D])
        raw = sb("raw", [P, 2, KT, P])
        wpart = sb("wpart", [P, 2, HALF_N])
        wfull = sb("wfull", [P, 2, HALF_N])
        w_hi = sb("w_hi", [P, KT, D], F32R)
        w_lo = sb("w_lo", [P, KT, D], F32R)
        bias = sb("bias", [P, D])
        x = sb("x", [P, 2, TT, D])
        xn = sb("xn", [P, TT, D])
        xT_hi = sb("xT_hi", [P, 2, KT, S], F32R)
        xT_lo = sb("xT_lo", [P, 2, KT, S], F32R)
        y = sb("y", [P, 2, TT, D])
        psT = es.enter_context(nc.psum_tensor("f_psT", [P, 4, HALF_N], F32))
        psY = es.enter_context(nc.psum_tensor("f_psY", [P, 4, HALF_N], F32))
        norm = Norm(nc, es, "f_norm", sh)

        coefs_loaded, table_loaded, enc_loaded, bias_loaded = (
            sem("coefs_loaded"), sem("table_loaded"), sem("enc_loaded"), sem("bias_loaded"))
        zeroed, masked_done, summed, bias_gated = sem("zeroed"), sem("masked_done"), sem("summed"), sem("bias_gated")
        update_full, update_copied = sem("update_full"), sem("update_copied")
        raw_loaded = [sem(f"raw_loaded{u}") for u in range(2)]
        w_full, part_copied, full_ready, hi_ready = sem("w_full"), sem("part_copied"), sem("full_ready"), sem("hi_ready")
        lo_ready = sem("lo_ready")
        x_loaded = [sem(f"x_loaded{u}") for u in range(2)]
        y_stored = [sem(f"y_stored{u}") for u in range(2)]
        psT_full, xhi_ready, xlo_ready = sem("psT_full"), sem("xhi_ready"), sem("xlo_ready")
        biased, psY_full, y_ready = sem("biased"), sem("psY_full"), sem("y_ready")

        block = es.enter_context(nc.Block())

        @block.sync
        def _(sp):
            for name, lo, r in (("0", 0, R0), ("1", R0, R1)):
                for e in range(NE):
                    sp.dma_start(coefs[:, e, :, lo:lo + r],
                                 c["coefs" + name][e].rearrange("(t p) r -> p t r", p=P)).then_inc(coefs_loaded, 16)
                    sp.dma_start(masks[:, e, :, lo:lo + r],
                                 c["mask" + name][e].rearrange("(t p) r -> p t r", p=P)).then_inc(coefs_loaded, 16)
            sp.dma_start(table[:, :, :], c["irfft"].rearrange("(t p) o -> p t o", p=P)).then_inc(table_loaded, 16)
            sp.wait_ge(zeroed, 2)
            sp.dma_start(enc[0:R0, :], c["enc0"]).then_inc(enc_loaded, 16)
            sp.dma_start(enc[R0:RR, :], c["enc1"]).then_inc(enc_loaded, 16)
            sp.dma_start(bias[:, :], c["b_base"].partition_broadcast(P)).then_inc(bias_loaded, 16)

            def load_columns(kt, u):
                sp.dma_start(raw[:, u, :, :], c["W_base"][:, bass.ds(kt * P, P)].rearrange("(t p) d -> p t d", p=P)
                             ).then_inc(raw_loaded[u], 16)

            def load_x(b, u):
                sp.dma_start(x[:, u, :, :], scratch["x1"][bass.ds(b, 1)].rearrange("b (t p) d -> p (b t) d", p=P)
                             ).then_inc(x_loaded[u], 16)

            for u in range(2):
                load_columns(u, u)
            for u in range(2):
                load_x(u, u)
                sp.sem_inc(y_stored[u], 1)
            with sp.Fori(1, KT // 2) as i:
                for u in range(2):
                    sp.wait_ge(w_full, 4 * i + 2 * u - 2)
                    load_columns(2 * i + u, u)

            def store(i, u):
                sp.wait_ge(y_ready, 8 * i + 4 * u + 4)
                sp.dma_start(scratch["x2"][bass.ds(2 * i + u, 1)].rearrange("b (t p) d -> p (b t) d", p=P),
                             y[:, u, :, :]).then_inc(y_stored[u], 16)

            with sp.Fori(0, PAIRS - 1) as i:
                for u in range(2):
                    store(i, u)
                    load_x(2 * i + 2 + u, u)
            for u in range(2):
                store(PAIRS - 1, u)
            for u in range(2):
                sp.wait_ge(y_stored[u], 16 * PAIRS + 1)

        @block.gpsimd
        def _(pool):
            nc.gpsimd.memset(update[:, :], 0.0).then_inc(zeroed, 1)
            nc.gpsimd.memset(enc[:, :], 0.0).then_inc(zeroed, 1)
            pool.wait_ge(zeroed, 2)
            pool.sem_inc(lo_ready, 2)
            with pool.Fori(0, KT) as kt:
                for h in range(2):
                    pool.wait_ge(hi_ready, 2 * kt + h + 1)
                    dst = bass.ds(h * HALF_N, HALF_N)
                    nc.gpsimd.tensor_tensor(w_lo[:, bass.ds(kt, 1), dst].rearrange("p a n -> p (a n)"), wfull[:, h, :],
                                            plain(w_hi)[:, bass.ds(kt, 1), dst].rearrange("p a n -> p (a n)"),
                                            ALU.subtract).then_inc(lo_ready, 1)
            norm.rstd_of(pool, 0, rms=False)
            pool.wait_ge(bias_gated, 1)

            def body(i, final):
                for u in range(2):
                    b = 2 * i + u
                    pool.wait_ge(norm.normed, b + 1)
                    for t in range(TT):
                        nc.gpsimd.tensor_tensor(x[:, u, t, :], x[:, u, t, :], bias[:, :], ALU.add).then_inc(biased, 1)
                    if not (final and u == 1):
                        norm.rstd_of(pool, b + 1, rms=False)

            with pool.Fori(0, PAIRS - 1) as i:
                body(i, False)
            body(PAIRS - 1, True)

        @block.tensor
        def _(pe):
            pe.wait_ge(summed, 1)
            pe.wait_ge(table_loaded, 16)
            for h in range(2):
                for kt in range(KT):
                    last = nc.tensor.matmul(psY[0:RR, h, :], wsum[:, kt, :], table[:, kt, h * HALF_N:(h + 1) * HALF_N],
                                            start=(kt == 0), stop=(kt == KT - 1))
                last.then_inc(update_full, 1)
            pe.wait_ge(update_copied, 2)
            pe.wait_ge(enc_loaded, 32)

            def weight_tile(kt, u, enc_cols):
                for h in range(2):
                    for q in range(4):
                        nc.tensor.transpose(psT[:, h, q * P:(q + 1) * P], raw[:, u, 4 * h + q, :], ident[:, :])
                    nc.tensor.matmul(psY[:, h, :], enc_cols, update[:, h * HALF_N:(h + 1) * HALF_N],
                                     start=True, stop=True).then_inc(w_full, 1)

            for kt in range(KT):
                pe.wait_ge(raw_loaded[kt % 2], 16 * (kt // 2 + 1))
                if kt:
                    pe.wait_ge(part_copied, 2 * kt)
                    pe.wait_ge(full_ready, 2 * kt)
                weight_tile(kt, kt % 2, enc[:, kt * P:(kt + 1) * P])

            def transposes(b):
                pe.wait_ge(norm.normed, b + 1)
                if not (isinstance(b, int) and b == 0):
                    pe.wait_ge(xlo_ready, 4 * b)
                for n in range(4):
                    for q in range(2):
                        for t in range(TT):
                            last = nc.tensor.transpose(psT[:, n, (q * TT + t) * P:(q * TT + t + 1) * P],
                                                       xn[:, t, (2 * n + q) * P:(2 * n + q + 1) * P], ident[:, :])
                    last.then_inc(psT_full, 1)

            pe.wait_ge(part_copied, 2 * KT)
            transposes(0)
            pe.wait_ge(lo_ready, 2 * KT + 2)

            def body(i, final):
                for u in range(2):
                    b = 2 * i + u
                    pe.wait_ge(xlo_ready, 4 * b + 4)
                    for t in range(TT):
                        for h in range(2):
                            if not (isinstance(i, int) and i == 0 and u == 0):
                                pe.wait_ge(y_ready, 4 * b + 2 * t + h - 3)
                            for kt in range(KT):
                                rows = slice(t * P, (t + 1) * P)
                                cols = slice(h * HALF_N, (h + 1) * HALF_N)
                                for a, w in ((xT_hi, w_hi), (xT_hi, w_lo), (xT_lo, w_hi)):
                                    last = nc.tensor.matmul(psY[:, 2 * t + h, :], a[:, u, kt, rows], w[:, kt, cols],
                                                            start=(kt == 0 and a is xT_hi and w is w_hi),
                                                            stop=(kt == KT - 1 and a is xT_lo))
                            last.then_inc(psY_full, 1)
                        if t == 0 and not (final and u == 1):
                            transposes(b + 1)

            body(0, False)
            with pe.Fori(1, PAIRS - 1) as i:
                body(i, False)
            body(PAIRS - 1, True)

        @block.vector
        def _(dve):
            dve.wait_ge(coefs_loaded, 16 * 4 * NE)
            nc.vector.tensor_tensor(masked[:, :, :, :], coefs[:, :, :, :], masks[:, :, :, :], ALU.mult).then_inc(masked_done, 1)
            dve.wait_ge(masked_done, 1)
            nc.vector.tensor_tensor(wsum[:, :, :], masked[:, 0, :, :], masked[:, 1, :, :], ALU.add).then_inc(masked_done, 1)
            dve.wait_ge(masked_done, 2)
            nc.vector.tensor_tensor(wsum[:, :, :], wsum[:, :, :], masked[:, 2, :, :], ALU.add).then_inc(summed, 1)
            dve.wait_ge(bias_loaded, 16)
            nc.vector.tensor_scalar(bias[:, :], bias[:, :], sh.gates[:, 2:3], None, ALU.mult).then_inc(bias_gated, 1)
            dve.wait_ge(zeroed, 1)
            for h in range(2):
                dve.wait_ge(update_full, h + 1)
                nc.vector.tensor_scalar(update[0:RR, h * HALF_N:(h + 1) * HALF_N], psY[0:RR, h, :], 0.5, None, ALU.mult
                                        ).then_inc(update_copied, 1)
            with dve.Fori(0, KT) as kt:
                for h in range(2):
                    dve.wait_ge(lo_ready, 2 * kt + h + 1)
                    dve.wait_ge(part_copied, 2 * kt + h + 1)
                    nc.vector.tensor_tensor(wfull[:, h, :], wpart[:, h, :], psY[:, h, :], ALU.add).then_inc(full_ready, 1)

            def moments(i, u, b):
                dve.wait_ge(x_loaded[u], 16 * i + 16)
                norm.moments_of(dve, b, x[:, u])

            moments(0, 0, 0)
            norm.normalise(dve, 0, x[:, 0], xn, norm.STEPS)

            def split_low(b, u):
                for n in range(4):
                    dve.wait_ge(xhi_ready, 4 * b + n + 1)
                    cols = slice(2 * n, 2 * n + 2)
                    nc.vector.tensor_tensor(xT_lo[:, u, cols, :].rearrange("p k n -> p (k n)"), psT[:, n, :],
                                            plain(xT_hi)[:, u, cols, :].rearrange("p k n -> p (k n)"),
                                            ALU.subtract).then_inc(xlo_ready, 1)

            split_low(0, 0)

            def body(i, final):
                for u in range(2):
                    b = 2 * i + u
                    if not (final and u == 1):
                        moments(i + u, 1 - u, b + 1)
                        norm.normalise(dve, b + 1, x[:, 1 - u], xn, norm.STEPS)
                        split_low(b + 1, 1 - u)
                    dve.wait_ge(biased, 2 * b + 2)
                    dve.wait_ge(y_stored[u], 16 * i + 1)
                    for t in range(TT):
                        for h in range(2):
                            dve.wait_ge(psY_full, 4 * b + 2 * t + h + 1)
                            cols = slice(h * HALF_N, (h + 1) * HALF_N)
                            nc.vector.scalar_tensor_tensor(y[:, u, t, cols], psY[:, 2 * t + h, :], sh.gates[:, 2:3],
                                                           x[:, u, t, cols], op0=ALU.mult, op1=ALU.add
                                                           ).then_inc(y_ready, 1)

            with dve.Fori(0, PAIRS - 1) as i:
                body(i, False)
            body(PAIRS - 1, True)

        @block.scalar
        def _(act):
            def weight_part(kt, h, n):
                act.wait_ge(w_full, n + 1)
                nc.scalar.copy(wpart[:, h, :], psT[:, h, :]).then_inc(part_copied, 1)

            def weight_high(kt, h, n):
                act.wait_ge(full_ready, n + 1)
                nc.scalar.copy(w_hi[:, bass.ds(kt, 1), h * HALF_N:(h + 1) * HALF_N].rearrange("p a n -> p (a n)"),
                               wfull[:, h, :]).then_inc(hi_ready, 1)

            with act.Fori(0, KT) as kt:
                for h in range(2):
                    weight_part(kt, h, 2 * kt + h)
                for h in range(2):
                    weight_high(kt, h, 2 * kt + h)
            with act.Fori(0, PAIRS) as i:
                for u in range(2):
                    b = 2 * i + u
                    for n in range(4):
                        act.wait_ge(psT_full, 4 * b + n + 1)
                        nc.scalar.copy(xT_hi[:, u, 2 * n:2 * n + 2, :].rearrange("p k n -> p (k n)"), psT[:, n, :]
                                       ).then_inc(xhi_ready, 1)


def attn1_stage(nc, sh, c, scratch):
    ident = sh.ident
    NT = D // P
    WIDTH = NH1 * NK1
    T_USES, O_USES = NT, 8
    NQ = 2 * CT1
    with ExitStack() as es:
        def sb(name, shape, dt=F32):
            return es.enter_context(nc.sbuf_tensor("b_" + name, shape, dt))

        def sem(name):
            return es.enter_context(nc.semaphore("b_" + name))

        raw = sb("raw", [P, 2, CT1, S])
        wm_perm = sb("wm_perm", [P, CT1, S])
        wqT = sb("wqT", [P, CT1, S])
        wmT = sb("wmT", [P, CT1, S])
        bq = sb("bq", [P, CT1])
        bm = sb("bm", [P, CT1])
        mask = sb("mask", [P, HT1, NK1])
        ones2 = sb("ones2", [P, 2 * HD1])
        x = sb("x", [P, 2, CT1, D])
        xn = sb("xn", [P, CT1, D])
        q = sb("q", [P, CT1, D])
        k1 = sb("k1", [P, 2, CT1, NK1])
        kbd = sb("kbd", [P, 2, CT1, HT1, NK1])
        v1 = sb("v1", [P, 2, NH1 // 2, 2 * HD1])
        maxes = sb("maxes", [P, 2, NH1])
        prob = sb("prob", [P, 2, WIDTH])
        probT = sb("probT", [P, 2, NH1 // 2, P])
        recip = sb("recip", [P, HALF_N])
        o = sb("o", [P, CT1, D])
        psS = es.enter_context(nc.psum_tensor("b_psS", [P, 2, WIDTH], F32))
        psT = es.enter_context(nc.psum_tensor("b_psT", [P, 2, HALF_N], F32))
        psO = es.enter_context(nc.psum_tensor("b_psO", [P, 2, HALF_N], F32))
        norm = Norm(nc, es, "b_norm", sh)

        raw_loaded, bias_loaded, bm_gated = sem("raw_loaded"), sem("bias_loaded"), sem("bm_gated")
        consts_done, perm_done = sem("consts_done"), sem("perm_done")
        w_full, w_copied = sem("w_full"), sem("w_copied")
        x_loaded = [sem(f"x_loaded{u}") for u in range(2)]
        kv_loaded = [sem(f"kv_loaded{u}") for u in range(2)]
        x_stored = [sem(f"x_stored{u}") for u in range(2)]
        biased, kbd_ready = sem("biased"), sem("kbd_ready")
        psT_full = [sem(f"psT_full{p}") for p in range(2)]
        psT_copied = [sem(f"psT_copied{p}") for p in range(2)]
        psO_full = [sem(f"psO_full{p}") for p in range(2)]
        psO_copied = [sem(f"psO_copied{p}") for p in range(2)]
        scores_full, max_ready, shifted, exp_done = sem("scores_full"), sem("max_ready"), sem("shifted"), sem("exp_done")
        recip_ready = sem("recip_ready")

        block = es.enter_context(nc.Block())

        @block.sync
        def _(sp):
            for m, name in enumerate(("Wq1", "Wm1")):
                sp.dma_start(raw[:, m, :, :], c[name].rearrange("(t p) d -> p t d", p=P)).then_inc(raw_loaded, 16)
            for h in range(HT1):
                sp.dma_start(bq[h * HD1:(h + 1) * HD1, :], c["bq1"].rearrange("(c t h) -> h c t", c=HD1, t=CT1)[h],
                             allow_slow_non_contiguous=True).then_inc(bias_loaded, 16)
            sp.dma_start(bm[:, :], c["bm1"].rearrange("(t p) -> p t", p=P), allow_slow_non_contiguous=True
                         ).then_inc(bias_loaded, 16)

            def load_batch(b, u):
                sp.dma_start(x[:, u, :, :], scratch["x2"][bass.ds(b, 1)].rearrange("b (t p) d -> p (b t) d", p=P)
                             ).then_inc(x_loaded[u], 16)
                sp.dma_start(k1[:, u].rearrange("p a n -> p (a n)"),
                             scratch["k1"][bass.ds(b, 1)].rearrange("b p n -> p (b n)")).then_inc(kv_loaded[u], 16)
                sp.dma_start(v1[:, u].rearrange("p a n -> p (a n)"),
                             scratch["v1"][bass.ds(b, 1)].rearrange("b p n -> p (b n)")).then_inc(kv_loaded[u], 16)

            def store_batch(i, u):
                for p in range(2):
                    sp.wait_ge(psO_copied[p], O_USES * (2 * i + u + 1) + 1)
                sp.dma_start(scratch["x3"][bass.ds(2 * i + u, 1)].rearrange("b (t p) d -> p (b t) d", p=P),
                             x[:, u, :, :]).then_inc(x_stored[u], 16)

            for u in range(2):
                load_batch(u, u)
            with sp.Fori(1, PAIRS) as i:
                for u in range(2):
                    store_batch(i - 1, u)
                    sp.wait_ge(x_stored[u], 16 * i)
                    load_batch(2 * i + u, u)
            for u in range(2):
                store_batch(PAIRS - 1, u)
                sp.wait_ge(x_stored[u], 16 * PAIRS)

        @block.gpsimd
        def _(pool):
            nc.gpsimd.memset(mask[:, :, :], HD1 ** -0.5).then_inc(consts_done, 1)
            pool.wait_ge(consts_done, 1)
            nc.gpsimd.affine_select(out=mask[:, :, :], in_=mask[:, :, :], compare_op=ALU.is_ge, fill=0.0, base=0,
                                    pattern=[[-HD1, HT1], [0, NK1]], channel_multiplier=1).then_inc(consts_done, 1)
            pool.wait_ge(consts_done, 2)
            nc.gpsimd.affine_select(out=mask[:, :, :], in_=mask[:, :, :], compare_op=ALU.is_ge, fill=0.0, base=HD1 - 1,
                                    pattern=[[HD1, HT1], [0, NK1]], channel_multiplier=-1).then_inc(consts_done, 1)
            nc.gpsimd.memset(ones2[:, :], 0.0).then_inc(consts_done, 1)
            pool.wait_ge(consts_done, 4)
            for e in range(2):
                nc.gpsimd.memset(ones2[e * NK1:(e + 1) * NK1, e * HD1:(e + 1) * HD1], 1.0).then_inc(consts_done, 1)
                pool.wait_ge(consts_done, 5 + e)
            norm.rstd_of(pool, 0, rms=False)
            pool.wait_ge(bm_gated, 1)

            def body(i, final):
                for u in range(2):
                    b = 2 * i + u
                    pool.wait_ge(norm.normed, b + 1)
                    hold(pool, sh)
                    for t in range(CT1):
                        nc.gpsimd.tensor_scalar(x[:, u, t, :], x[:, u, t, :], bm[:, t:t + 1], None, ALU.add
                                                ).then_inc(biased, 1)
                    if not (final and u == 1):
                        norm.rstd_of(pool, b + 1, rms=False)

            with pool.Fori(0, PAIRS - 1) as i:
                body(i, False)
            body(PAIRS - 1, True)

        @block.tensor
        def _(pe):
            for m in range(2):
                if m == 0:
                    pe.wait_ge(raw_loaded, 32)
                else:
                    pe.wait_ge(perm_done, 1)
                src = (raw[:, 0], wm_perm)[m]
                for t in range(CT1):
                    for ot in range(CT1):
                        last = nc.tensor.transpose(psT[:, m, t * S + ot * P:t * S + (ot + 1) * P],
                                                   src[:, ot, t * P:(t + 1) * P], ident[:, :])
                last.then_inc(w_full, 1)
            pe.wait_ge(w_copied, 2)
            pe.wait_ge(consts_done, 6)

            with pe.Fori(0, PAIRS) as i:
                for u in range(2):
                    b = 2 * i + u
                    pe.wait_ge(norm.normed, b + 1)
                    for m in range(NQ):
                        t, h = m // 2, m % 2
                        pe.wait_ge(psO_copied[h], O_USES * b + t + 1)
                        for dt in range(CT1):
                            last = nc.tensor.matmul(psO[:, h, :], wqT[:, dt, t * P:(t + 1) * P],
                                                    xn[:, dt, h * HALF_N:(h + 1) * HALF_N],
                                                    start=(dt == 0), stop=(dt == CT1 - 1))
                        last.then_inc(psO_full[h], 1)
                    pe.wait_ge(kbd_ready, b + 1)
                    for h in range(2):
                        pe.wait_ge(psO_copied[h], O_USES * b + CT1 + 1)

                    def scores(n):
                        for t in range(CT1):
                            last = nc.tensor.matmul(psS[:, n % 2, t * HALF_N:(t + 1) * HALF_N],
                                                    q[:, t, n * P:(n + 1) * P],
                                                    kbd[:, u, t, :, :].rearrange("p h k -> p (h k)"), start=True, stop=True)
                        last.then_inc(scores_full, 1)

                    def transposes(n):
                        pe.wait_ge(exp_done, NT * b + n + 1)
                        for t in range(CT1):
                            pe.wait_ge(psT_copied[t], T_USES * b + n + 1)
                            for j in range(4):
                                last = nc.tensor.transpose(psT[:, t, j * P:(j + 1) * P],
                                                           prob[:, n % 2, (4 * t + j) * P:(4 * t + j + 1) * P], ident[:, :])
                            last.then_inc(psT_full[t], 1)

                    def values(n):
                        for t in range(CT1):
                            pe.wait_ge(psT_copied[t], T_USES * b + n + 2)
                            if n % 2 == 0:
                                pe.wait_ge(psO_copied[t], O_USES * b + CT1 + n // 2 + 1)
                        for t in range(CT1):
                            cols = slice(t * S + (n % 2) * P, t * S + (n % 2) * P + P)
                            for j in range(4):
                                rows = slice(j * 2 * HD1, (j + 1) * 2 * HD1)
                                nc.tensor.matmul(psO[rows, 0, cols], v1[:, u, 4 * t + j, :], probT[:, n % 2, 4 * t + j, :],
                                                 start=True, stop=True)
                                last = nc.tensor.matmul(psO[rows, 1, cols], ones2[:, :], probT[:, n % 2, 4 * t + j, :],
                                                        start=True, stop=True)
                        if n % 2:
                            last.then_inc(psO_full[1], 1)

                    scores(0)
                    scores(1)
                    for n in range(NT):
                        transposes(n)
                        if n + 2 < NT:
                            scores(n + 2)
                        if n:
                            values(n - 1)
                    values(NT - 1)
                    for p in range(2):
                        pe.wait_ge(psO_copied[p], O_USES * b + CT1 + NT // 2 + 1)
                    for m in range(NQ):
                        t, h = m // 2, m % 2
                        if t:
                            pe.wait_ge(psO_copied[h], O_USES * b + CT1 + NT // 2 + t + 1)
                        for dt in range(CT1):
                            last = nc.tensor.matmul(psO[:, h, :], wmT[:, dt, t * P:(t + 1) * P],
                                                    o[:, dt, h * HALF_N:(h + 1) * HALF_N],
                                                    start=(dt == 0), stop=(dt == CT1 - 1))
                        last.then_inc(psO_full[h], 1)

        FULL0, FULL1 = 2 * CT1, 2 * CT1 + NT // 2

        @block.vector
        def _(dve):
            for p in range(2):
                dve.sem_inc(psO_copied[p], 1)
                dve.sem_inc(psT_copied[p], 1)
            dve.wait_ge(raw_loaded, 32)
            nc.vector.tensor_copy(wm_perm[:, :, :].rearrange("p t (h c) -> p t h c", h=NH1),
                                  raw[:, 1, :, :].rearrange("p t (c h) -> p t h c", h=NH1)).then_inc(perm_done, 1)
            dve.wait_ge(w_full, 1)
            nc.vector.tensor_copy(wqT[:, :, :].rearrange("p t (h c) -> p t h c", h=NH1),
                                  psT[:, 0, :].rearrange("p (t c h) -> p t h c", t=CT1, h=NH1)).then_inc(w_copied, 1)
            dve.wait_ge(w_full, 2)
            nc.vector.tensor_copy(wmT[:, :, :].rearrange("p t d -> p (t d)"), psT[:, 1, :]).then_inc(w_copied, 1)
            dve.wait_ge(bias_loaded, 16 * (HT1 + 1))
            nc.vector.tensor_scalar(bm[:, :], bm[:, :], sh.gates[:, 1:2], None, ALU.mult).then_inc(bm_gated, 1)
            dve.wait_ge(consts_done, 3)

            def moments(b, i, u):
                dve.wait_ge(x_loaded[u], 16 * i + 16)
                norm.moments_of(dve, b, x[:, u])

            moments(0, 0, 0)
            norm.normalise(dve, 0, x[:, 0], xn, norm.STEPS)

            def body(i, final):
                for u in range(2):
                    b = 2 * i + u
                    dve.wait_ge(kv_loaded[u], 32 * i + 32)
                    for t in range(CT1):
                        last = nc.vector.tensor_tensor(kbd[:, u, t, :, :], mask[:, :, :],
                                                       k1[:, u, t:t + 1, :].broadcast_to([P, HT1, NK1]), ALU.mult)
                    last.then_inc(kbd_ready, 1)
                    for t in range(CT1):
                        dve.wait_ge(psO_full[0], FULL0 * b + t + 1)
                        nc.vector.tensor_scalar(q[:, t, 0:HALF_N], psO[:, 0, :], bq[:, t:t + 1], None, ALU.add
                                                ).then_inc(psO_copied[0], 1)

                    def shift(n):
                        dve.wait_ge(scores_full, NT * b + n + 1)
                        s = psS[:, n % 2, :].rearrange("p (h k) -> p h k", h=NH1)
                        nc.vector.tensor_reduce(maxes[:, n % 2, :], s, AX_X, ALU.max).then_inc(max_ready, 1)
                        dve.wait_ge(max_ready, NT * b + n + 1)
                        if n >= 2:
                            dve.wait_ge(psT_full[1], T_USES * b + n - 1)
                        nc.vector.tensor_tensor(prob[:, n % 2, :].rearrange("p (h k) -> p h k", h=NH1), s,
                                                maxes[:, n % 2, :].unsqueeze(2).broadcast_to([P, NH1, NK1]),
                                                ALU.subtract).then_inc(shifted, 1)

                    def normalise_o(pair):
                        dve.wait_ge(psO_full[1], FULL1 * b + CT1 + pair + 1)
                        nc.vector.reciprocal(recip[:, :], psO[:, 1, :]).then_inc(recip_ready, 1)
                        dve.wait_ge(recip_ready, (NT // 2) * b + pair + 1)
                        nc.vector.tensor_tensor(o[:, :, pair * S:(pair + 1) * S],
                                                psO[:, 0, :].rearrange("p (t n) -> p t n", t=CT1),
                                                recip[:, :].rearrange("p (t n) -> p t n", t=CT1), ALU.mult
                                                ).then_inc(psO_copied[0], 1)
                        dve.wait_ge(psO_copied[0], O_USES * b + CT1 + pair + 2)
                        dve.sem_inc(psO_copied[1], 1)

                    shift(0)
                    shift(1)
                    for n in range(NT):
                        if n + 2 < NT:
                            shift(n + 2)
                        if n % 2 == 0 and n:
                            normalise_o(n // 2 - 1)
                        if n in (1, 3) and not (final and u == 1):
                            if n == 1:
                                moments(b + 1, i + u, 1 - u)
                            else:
                                norm.normalise(dve, b + 1, x[:, 1 - u], xn, norm.STEPS)
                    normalise_o(NT // 2 - 1)
                    dve.wait_ge(biased, 2 * b + 2)
                    for m in range(NQ):
                        t, h = m // 2, m % 2
                        dve.wait_ge(psO_full[h], (FULL0, FULL1)[h] * b + (CT1, CT1 + NT // 2)[h] + t + 1)
                        cols = slice(h * HALF_N, (h + 1) * HALF_N)
                        nc.vector.scalar_tensor_tensor(x[:, u, t, cols], psO[:, h, :], sh.gates[:, 1:2], x[:, u, t, cols],
                                                       op0=ALU.mult, op1=ALU.add).then_inc(psO_copied[h], 1)

            with dve.Fori(0, PAIRS - 1) as i:
                body(i, False)
            body(PAIRS - 1, True)

        @block.scalar
        def _(act):
            act.wait_ge(bias_loaded, 16 * (HT1 + 1))
            with act.Fori(0, PAIRS) as i:
                for u in range(2):
                    b = 2 * i + u
                    for t in range(CT1):
                        act.wait_ge(psO_full[1], FULL1 * b + t + 1)
                        nc.scalar.activation(q[:, t, HALF_N:D], psO[:, 1, :], ACT.Identity, bias=bq[:, t:t + 1]
                                             ).then_inc(psO_copied[1], 1)

                    def exponential(n):
                        act.wait_ge(shifted, NT * b + n + 1)
                        nc.scalar.activation(prob[:, n % 2, :], prob[:, n % 2, :], ACT.Exp).then_inc(exp_done, 1)

                    exponential(0)
                    exponential(1)
                    for n in range(NT):
                        for t in range(CT1):
                            act.wait_ge(psT_full[t], T_USES * b + n + 1)
                            nc.scalar.copy(probT[:, n % 2, 4 * t:4 * t + 4, :],
                                           psT[:, t, :].rearrange("p (j q) -> p j q", j=4)).then_inc(psT_copied[t], 1)
                        if n + 2 < NT:
                            exponential(n + 2)


def ffn1_stage(nc, sh, c, scratch, out):
    EXPONENT_BITS = 0x7F800000
    SMALLEST_NORMAL = 2.0 ** -6
    MAGIC = 1.5 * 2.0 ** 20
    CHUNK = TT * D
    WCHUNKS = KT * D // CHUNK
    QSTEPS = 4
    with ExitStack() as es:
        def sb(name, shape, dt=F32):
            return es.enter_context(nc.sbuf_tensor("q_" + name, shape, dt))

        def sem(name):
            return es.enter_context(nc.semaphore("q_" + name))

        ident16 = sb("ident16", [P, P], BF16)
        w = sb("w", [P, KT, D])
        wq = sb("wq", [P, KT, D], BF16)
        x = sb("x", [P, 2, TT, D])
        xn = sb("xn", [P, B, TT, D])
        row_max = sb("row_max", [P, B, TT])
        part_max = sb("part_max", [P, 2])
        all_max = sb("all_max", [P, 2])
        scale = sb("scale", [P, 2])
        inverse = sb("inverse", [P, 2])
        out_scale = sb("out_scale", [P, 1])
        scaled = sb("scaled", [P, CHUNK])
        magic = sb("magic", [P, CHUNK])
        xq = sb("xq", [P, 2, TT, D], BF16)
        xqT = sb("xqT", [P, 2, KT, S], BF16)
        y = sb("y", [P, 2, TT, D])
        psT = es.enter_context(nc.psum_tensor("q_psT", [P, 2, 2 * HALF_N], BF16))
        psY = es.enter_context(nc.psum_tensor("q_psY", [P, 4, HALF_N], F32))
        norm = Norm(nc, es, "q_norm", sh)

        w_loaded, ident_ready = sem("w_loaded"), sem("ident_ready")
        x_loaded = [sem(f"x_loaded{u}") for u in range(2)]
        again_loaded = [sem(f"again_loaded{u}") for u in range(2)]
        max_done, part_done, all_done, scale_steps = sem("max_done"), sem("part_done"), sem("all_done"), sem("scale_steps")
        quant_steps = sem("quant_steps")
        quantised, psT_full, xqT_ready = sem("quantised"), sem("psT_full"), sem("xqT_ready")
        psY_full, y_ready = sem("psY_full"), sem("y_ready")
        y_stored = [sem(f"y_stored{u}") for u in range(2)]

        block = es.enter_context(nc.Block())

        @block.sync
        def _(sp):
            def load(b, u, loaded):
                sp.dma_start(x[:, u, :, :], scratch["x3"][bass.ds(b, 1)].rearrange("b (t p) d -> p (b t) d", p=P)
                             ).then_inc(loaded[u], 16)

            for u in range(2):
                load(u, u, x_loaded)
            sp.dma_start(w[:, :, :], c["weight"].rearrange("(t p) n -> p t n", p=P)).then_inc(w_loaded, 16)
            with sp.Fori(1, PAIRS) as i:
                for u in range(2):
                    sp.wait_ge(norm.normed, 2 * i + u - 1)
                    load(2 * i + u, u, x_loaded)
            for u in range(2):
                sp.wait_ge(norm.normed, B - 1 + u)
                load(u, u, again_loaded)

            def store(i, u):
                sp.wait_ge(y_ready, 8 * i + 4 * u + 4)
                sp.dma_start(out[bass.ds(2 * i + u, 1)].rearrange("b (t p) d -> p (b t) d", p=P), y[:, u, :, :]
                             ).then_inc(y_stored[u], 16)

            with sp.Fori(0, PAIRS - 1) as i:
                for u in range(2):
                    store(i, u)
                    load(2 * i + 2 + u, u, again_loaded)
            for u in range(2):
                store(PAIRS - 1, u)
            for u in range(2):
                sp.wait_ge(y_stored[u], 16 * PAIRS)

        @block.gpsimd
        def _(pool):
            nc.gpsimd.tensor_copy(ident16[:, :], sh.ident[:, :]).then_inc(ident_ready, 1)
            pool.wait_ge(part_done, 1)
            nc.gpsimd.partition_all_reduce(all_max[:, 1:2], part_max[:, 1:2], P, ABSMAX).then_inc(all_done, 1)
            with pool.Fori(0, B) as b:
                norm.rstd_of(pool, b, rms=False)
            pool.wait_ge(part_done, 2)
            nc.gpsimd.partition_all_reduce(all_max[:, 0:1], part_max[:, 0:1], P, ABSMAX).then_inc(all_done, 1)

        @block.tensor
        def _(pe):
            pe.wait_ge(ident_ready, 1)

            def batch(b, u, first):
                pe.wait_ge(quantised, WCHUNKS + b + 1)
                for n in range(2):
                    if not first:
                        pe.wait_ge(xqT_ready, 2 * b + n - 1)
                    for q in range(4):
                        for t in range(TT):
                            kt = 4 * n + q
                            last = nc.tensor.transpose(psT[:, n, (q * TT + t) * P:(q * TT + t + 1) * P],
                                                       xq[:, u, t, kt * P:(kt + 1) * P], ident16[:, :])
                    last.then_inc(psT_full, 1)
                pe.wait_ge(xqT_ready, 2 * b + 2)
                for t in range(TT):
                    for h in range(2):
                        if not first:
                            pe.wait_ge(y_ready, 4 * b + 2 * t + h - 3)
                        for kt in range(KT):
                            last = nc.tensor.matmul(psY[:, 2 * t + h, :], xqT[:, u, kt, t * P:(t + 1) * P],
                                                    wq[:, kt, h * HALF_N:(h + 1) * HALF_N],
                                                    start=(kt == 0), stop=(kt == KT - 1))
                        last.then_inc(psY_full, 1)

            batch(0, 0, True)
            batch(1, 1, False)
            with pe.Fori(1, PAIRS) as i:
                for u in range(2):
                    batch(2 * i + u, u, False)

        @block.vector
        def _(dve):
            def link(instruction, semaphore, value):
                instruction.then_inc(semaphore, 1)
                dve.wait_ge(semaphore, value)

            def scale_of(m, done):
                dve.wait_ge(all_done, done)
                at = 3 * (done - 1)
                link(nc.vector.tensor_scalar(all_max[:, m:m + 1], all_max[:, m:m + 1], 1e-12, None, ALU.max),
                     scale_steps, at + 1)
                link(nc.vector.reciprocal(scale[:, m:m + 1], all_max[:, m:m + 1]), scale_steps, at + 2)
                link(nc.vector.tensor_scalar(scale[:, m:m + 1], scale[:, m:m + 1], FP8_MAX, None, ALU.mult),
                     scale_steps, at + 3)
                nc.vector.reciprocal(inverse[:, m:m + 1], scale[:, m:m + 1])

            def quantise(n, src, m, dst):
                if not (isinstance(n, int) and n == 0):
                    dve.wait_ge(quantised, n)
                link(nc.vector.tensor_scalar(scaled[:, :], src, scale[:, m:m + 1], FP8_MAX, ALU.mult, ALU.min),
                     quant_steps, QSTEPS * n + 1)
                link(nc.vector.tensor_scalar(magic[:, :].bitcast(U32), scaled[:, :].bitcast(U32), EXPONENT_BITS, None,
                                             ALU.bitwise_and), quant_steps, QSTEPS * n + 2)
                link(nc.vector.tensor_scalar(magic[:, :], magic[:, :], SMALLEST_NORMAL, MAGIC, ALU.max, ALU.mult),
                     quant_steps, QSTEPS * n + 3)
                link(nc.vector.scalar_tensor_tensor(scaled[:, :], scaled[:, :], -FP8_MAX, magic[:, :],
                                                    op0=ALU.max, op1=ALU.add), quant_steps, QSTEPS * n + 4)
                nc.vector.tensor_tensor(dst, scaled[:, :], magic[:, :], ALU.subtract).then_inc(quantised, 1)

            dve.wait_ge(w_loaded, 16)
            nc.vector.tensor_reduce(part_max[:, 1:2], w[:, :, :].rearrange("p t n -> p (t n)"), AX_X, ALU.max,
                                    apply_absolute_value=True).then_inc(part_done, 1)
            scale_of(1, 1)
            for n in range(WCHUNKS):
                rows = slice(n * KT // WCHUNKS, (n + 1) * KT // WCHUNKS)
                quantise(n, w[:, rows, :].rearrange("p t n -> p (t n)"), 1, wq[:, rows, :].rearrange("p t n -> p (t n)"))

            with dve.Fori(0, PAIRS) as i:
                for u in range(2):
                    b = 2 * i + u
                    dve.wait_ge(x_loaded[u], 16 * i + 16)
                    norm.moments_of(dve, b, x[:, u])
                    mine = xn[:, bass.ds(b, 1)].rearrange("p b t d -> p (b t) d")
                    norm.normalise(dve, b, x[:, u], mine, norm.STEPS)
                    dve.wait_ge(norm.normed, b + 1)
                    nc.vector.tensor_reduce(row_max[:, bass.ds(b, 1), :].rearrange("p b t -> p (b t)"), mine, AX_X, ALU.max,
                                            apply_absolute_value=True).then_inc(max_done, 1)
            dve.wait_ge(max_done, B)
            nc.vector.tensor_reduce(part_max[:, 0:1], row_max[:, :, :].rearrange("p b t -> p (b t)"), AX_X, ALU.max
                                    ).then_inc(part_done, 1)
            scale_of(0, 2)
            dve.drain()
            link(nc.vector.tensor_tensor(out_scale[:, :], inverse[:, 0:1], inverse[:, 1:2], ALU.mult), scale_steps, 7)
            link(nc.vector.tensor_tensor(out_scale[:, :], out_scale[:, :], sh.gates[:, 3:4], ALU.mult), scale_steps, 8)

            def quantise_batch(b, u):
                quantise(WCHUNKS + b, xn[:, bass.ds(b, 1)].rearrange("p b t d -> p (b t d)"), 0,
                         xq[:, u, :, :].rearrange("p t d -> p (t d)"))

            def add_residual(b, i, u, first):
                dve.wait_ge(again_loaded[u], 16 * i + 16)
                if not first:
                    dve.wait_ge(y_stored[u], 16 * i)
                for t in range(TT):
                    for h in range(2):
                        dve.wait_ge(psY_full, 4 * b + 2 * t + h + 1)
                        cols = slice(h * HALF_N, (h + 1) * HALF_N)
                        nc.vector.scalar_tensor_tensor(y[:, u, t, cols], psY[:, 2 * t + h, :], out_scale[:, 0:1],
                                                       x[:, u, t, cols], op0=ALU.mult, op1=ALU.add).then_inc(y_ready, 1)

            quantise_batch(0, 0)
            quantise_batch(1, 1)
            add_residual(0, 0, 0, True)
            quantise_batch(2, 0)
            add_residual(1, 0, 1, True)
            quantise_batch(3, 1)
            with dve.Fori(1, PAIRS - 1) as i:
                for u in range(2):
                    add_residual(2 * i + u, i, u, False)
                    quantise_batch(2 * i + u + 2, u)
            for u in range(2):
                add_residual(B - 2 + u, PAIRS - 1, u, False)

        @block.scalar
        def _(act):
            with act.Fori(0, PAIRS) as i:
                for u in range(2):
                    b = 2 * i + u
                    for n in range(2):
                        act.wait_ge(psT_full, 2 * b + n + 1)
                        nc.scalar.copy(xqT[:, u, 4 * n:4 * n + 4, :].rearrange("p k n -> p (k n)"), psT[:, n, :]
                                       ).then_inc(xqT_ready, 1)


_NAMES = {"wk": "L0_xattn_wk", "wv": "L0_xattn_wv", "wq": "L0_xattn_wq", "wo": "L0_xattn_wo", "ln_w": "L0_xattn_ln_w",
          "x": "x", "ctx": "ctx_4096", "W_base": "L0_ffn_W_base", "b_base": "L0_ffn_b_base", "enc0": "L0_ffn_enc0",
          "enc1": "L0_ffn_enc1", "coefs0": "L0_ffn_coefs0", "coefs1": "L0_ffn_coefs1", "mask0": "L0_ffn_mask0",
          "mask1": "L0_ffn_mask1", "Wq1": "L1_xattn_Wq", "bq1": "L1_xattn_bq", "Wk1": "L1_xattn_Wk", "bk1": "L1_xattn_bk",
          "Wv1": "L1_xattn_Wv", "bv1": "L1_xattn_bv", "proj_k": "L1_xattn_proj_k", "proj_v": "L1_xattn_proj_v",
          "Wm1": "L1_xattn_Wm", "bm1": "L1_xattn_bm", "weight": "L1_ffn_weight", "g_xattn": "g_xattn", "g_ffn": "g_ffn"}


def build(nc, a, out):
    scratch = {}
    for name, width in (("k0", HALF0 * S), ("v0", TT * KV0), ("k1", CT1 * NK1), ("v1", S)):
        scratch[name] = nc.dram_tensor("scratch_" + name, [B, P, width], F32).ap()
    for name in ("x1", "x2", "x3"):
        scratch[name] = nc.dram_tensor("scratch_" + name, [B, S, D], F32).ap()
    with ExitStack() as es:
        sh = setup_stage(nc, es, a["g_xattn"], a["g_ffn"])
        context_stage(nc, sh, a, scratch)
        attn0_stage(nc, sh, a, scratch)
        ffn0_stage(nc, sh, a, scratch)
        attn1_stage(nc, sh, a, scratch)
        ffn1_stage(nc, sh, a, scratch, out)


def inverse_rfft_table():
    o = np.arange(D)
    table = np.empty((D, D), np.float64)
    table[0] = D ** -0.5
    table[D - 1] = np.where(o % 2 == 0, 1.0, -1.0) * D ** -0.5
    k = np.arange(1, D // 2)[:, None]
    angle = 2.0 * np.pi * ((k * o) % D) / D
    table[1:D - 1:2] = (2.0 / D) ** 0.5 * np.cos(angle)
    table[2:D:2][:D // 2 - 1] = (2.0 / D) ** 0.5 * np.sin(angle)
    return table.astype(np.float32)


def kernel(**inputs):
    import concourse.bacc as bacc
    from concourse.bass_utils import run_bass_kernel_spmd

    nc = bacc.Bacc("TRN2", target_bir_lowering=False, num_devices=1)
    arrays, args = {}, {}
    for short, name in _NAMES.items():
        array = np.ascontiguousarray(inputs[name])
        arrays["in_" + short] = array
        args[short] = nc.dram_tensor("in_" + short, array.shape, mybir.dt.from_np(array.dtype), kind="ExternalInput").ap()
    arrays["irfft"] = inverse_rfft_table()
    args["irfft"] = nc.dram_tensor("irfft", (D, D), F32, kind="ExternalInput").ap()
    out = nc.dram_tensor("out", (B, S, D), F32, kind="ExternalOutput").ap()
    build(nc, args, out)
    return run_bass_kernel_spmd(nc, [arrays], core_ids=[0]).results[0]["out"]
```

```python
from contextlib import ExitStack

import numpy as np
import concourse.bass as bass
from concourse import mybir

F32 = mybir.dt.float32
F32R = mybir.dt.float32r
BF16 = mybir.dt.bfloat16
U8 = mybir.dt.uint8
U32 = mybir.dt.uint32
ALU = mybir.AluOpType
ACT = mybir.ActivationFunctionType
AX_X = mybir.AxisListType.X
ABSMAX = bass.bass_isa.ReduceOp.absmax

P = 128
B, S, D = 8, 256, 1024
TT = S // P
KT = D // P
PAIRS = B // 2
HD0, NH0, NKV0 = 32, 32, 8
KV0 = NKV0 * HD0
HALF0 = KV0 // P
REP0 = NH0 // NKV0
JH0 = P // HD0
HD1, NH1, NK1 = 16, 16, 64
HT1 = P // HD1
CT1 = S // P
R0, R1, NE = 32, 8, 3
RR = R0 + R1
LN_EPS = 1e-5
FP8_MAX = 448.0
HALF_N = 512


def identity(nc, ident, done):
    nc.gpsimd.memset(ident[:, :], 0.0).then_inc(done, 1)
    nc.gpsimd.wait_ge(done, 1)
    nc.gpsimd.affine_select(out=ident[:, :], in_=ident[:, :], compare_op=ALU.not_equal, fill=1.0, base=0,
                            pattern=[[-1, P]], channel_multiplier=1).then_inc(done, 1)


def hold(engine, sh):
    engine.sem_inc(sh.held, 1)


def free_semaphores(nc, sems):
    nc.clear_and_free_semaphores(sems)
    nc.all_engine_barrier()


class Shared:
    pass


def setup_stage(nc, ctx, g_xattn, g_ffn):
    sh = Shared()
    sh.ident = ctx.enter_context(nc.sbuf_tensor("ident", [P, P], F32))
    sh.gates = ctx.enter_context(nc.sbuf_tensor("gates", [P, 4], F32))
    sh.gate_raw = ctx.enter_context(nc.sbuf_tensor("gate_raw", [P, 4], F32))
    sh.minus_half = ctx.enter_context(nc.sbuf_tensor("minus_half", [P, 4], F32))
    sh.ident_done = ctx.enter_context(nc.semaphore("ident_done"))
    sh.held = ctx.enter_context(nc.semaphore("held"))
    sh.gates_loaded = ctx.enter_context(nc.semaphore("gates_loaded"))
    with nc.Block() as block:
        @block.sync
        def _(sp):
            sp.dma_start(sh.gate_raw[:, 0:2], g_xattn.partition_broadcast(P)).then_inc(sh.gates_loaded, 16)
            sp.dma_start(sh.gate_raw[:, 2:4], g_ffn.partition_broadcast(P)).then_inc(sh.gates_loaded, 16)

        @block.gpsimd
        def _(pool):
            identity(nc, sh.ident, sh.ident_done)
            nc.gpsimd.memset(sh.minus_half[:, :], -0.5)

        @block.scalar
        def _(act):
            act.wait_ge(sh.gates_loaded, 32)
            nc.scalar.activation(sh.gates[:, :], sh.gate_raw[:, :], ACT.Tanh)
    return sh


def context_stage(nc, sh, c, scratch):
    ident = sh.ident
    STORES = 5
    CV = KV0 + 3 * NK1
    with ExitStack() as es:
        def sb(name, shape, dt=F32):
            return es.enter_context(nc.sbuf_tensor("c_" + name, shape, dt))

        sems = []
        es.callback(lambda: free_semaphores(nc, sems))

        def sem(name):
            sems.append(nc.alloc_semaphore("c_" + name))
            return sems[-1]

        raw = sb("raw", [P, 2, D])
        raw1 = sb("raw1", [P, 2, 2, S])
        wkT = sb("wkT", [P, KT, KV0])
        wvpT = sb("wvpT", [P, KT, CV])
        w1T = sb("w1T", [P, 2, TT, S])
        rows1 = sb("rows1", [1, 2, S])
        rows1h = sb("rows1h", [1, 2, S])
        ones = sb("ones", [P, 1])
        colsum = sb("colsum", [1, 3 * NK1])
        bias_k = sb("bias_k", [P, CT1, NK1])
        bias_v = sb("bias_v", [P, S])
        nat = sb("nat", [P, 2, TT, D])
        cT = sb("cT", [P, 2, KT, S])
        k0_hi = sb("k0_hi", [P, 2, HALF0, S], F32R)
        k0_lo = sb("k0_lo", [P, 2, HALF0, S], F32R)
        v0 = sb("v0", [P, 2, TT, KV0])
        mid = sb("mid", [P, 2, TT, 3 * NK1])
        k1 = sb("k1", [P, 2, CT1, NK1])
        v1 = sb("v1", [P, 2, NH1 // 2, 2 * HD1])
        psT = es.enter_context(nc.psum_tensor("c_psT", [P, 2, HALF_N], F32))
        psP = es.enter_context(nc.psum_tensor("c_psP", [P, 4, HALF_N], F32))
        psL = es.enter_context(nc.psum_tensor("c_psL", [P, HALF_N], F32))

        raw_loaded = [sem(f"raw_loaded{n}") for n in range(2 * HALF0)]
        raw1_loaded, small_loaded, proj_loaded = sem("raw1_loaded"), sem("small_loaded"), sem("proj_loaded")
        wT_full, wT_copied = sem("wT_full"), sem("wT_copied")
        preset = sem("preset")
        colsum_full, colsum_copied = sem("colsum_full"), sem("colsum_copied")
        bias_full, bias_copied = sem("bias_full"), sem("bias_copied")
        nat_loaded = [sem(f"nat_loaded{u}") for u in range(2)]
        psT_full = [sem(f"psT_full{p}") for p in range(2)]
        cT_dve, cT_act = sem("cT_dve"), sem("cT_act")
        psP_full, mid_ready = sem("psP_full"), sem("mid_ready")
        psL_full = sem("psL_full")
        out_act = [sem(f"out_act{u}") for u in range(2)]
        out_dve = [sem(f"out_dve{u}") for u in range(2)]
        out_stored = [sem(f"out_stored{u}") for u in range(2)]

        block = es.enter_context(nc.Block())

        blocks = [(c["wk"], n) for n in range(HALF0)] + [(c["wv"], n) for n in range(HALF0)]

        @block.sync
        def _(sp):
            def load_ctx(b, u):
                sp.dma_start(nat[:, u, :, :],
                             c["ctx"][bass.ds(b, 1)].rearrange("b (t p) d -> p (b t) d", p=P)
                             ).then_inc(nat_loaded[u], 16)

            for n, (w, rb) in enumerate(blocks):
                if n >= 2:
                    sp.wait_ge(wT_full, 2 * (n - 1))
                sp.dma_start(raw[:, n % 2, :], w[rb * P:(rb + 1) * P, :]).then_inc(raw_loaded[n], 16)
            for m, name in enumerate(("Wk1", "Wv1")):
                sp.dma_start(raw1[:, m, :, :], c[name].rearrange("(t p) d -> p t d", p=P)).then_inc(raw1_loaded, 16)
            for m, name in enumerate(("bk1", "bv1")):
                sp.dma_start(rows1[0:1, m, :], c[name].rearrange("(a d) -> a d", a=1)).then_inc(small_loaded, 16)
            for m, name in enumerate(("proj_k", "proj_v", "proj_v")):
                lo = KV0 + m * NK1
                sp.dma_start(wvpT[:, :, lo:lo + NK1],
                             c[name].rearrange("(t p) k -> p t k", p=P)).then_inc(proj_loaded, 16)
            def store(i):
                for u in range(2):
                    sp.wait_ge(out_act[u], 4 * i + 5)
                    sp.wait_ge(out_dve[u], 2 * i + 3)
                    for name, tile in (("k0_hi", k0_hi), ("k0_lo", k0_lo)):
                        sp.dma_start(scratch[name][bass.ds(2 * i + u, 1)].rearrange("b (a p) s -> p (b a) s", p=P),
                                     plain(tile)[:, u, :, :]).then_inc(out_stored[u], 16)
                    for name, tile in (("v0", v0), ("k1", k1), ("v1", v1)):
                        sp.dma_start(scratch[name][bass.ds(2 * i + u, 1)].rearrange("b p n -> p (b n)"),
                                     tile[:, u].rearrange("p a n -> p (a n)")).then_inc(out_stored[u], 16)

            for u in range(2):
                sp.sem_inc(out_stored[u], 1)
                load_ctx(u, u)
            with sp.Fori(1, PAIRS) as i:
                for u in range(2):
                    sp.wait_ge(cT_dve, 4 * i + 2 * u - 1)
                    sp.wait_ge(cT_act, 4 * i + 2 * u - 1)
                    load_ctx(2 * i + u, u)
                store(i - 1)
            store(PAIRS - 1)
            for u in range(2):
                sp.wait_ge(out_stored[u], 16 * STORES * PAIRS + 1)

        @block.gpsimd
        def _(pool):
            nc.gpsimd.memset(ones[:, :], 1.0).then_inc(preset, 1)
            nc.gpsimd.memset(v1[:, :, :, :], 0.0).then_inc(preset, 1)

        @block.tensor
        def _(pe):
            for n in range(len(blocks)):
                pe.wait_ge(raw_loaded[n], 16)
                for half in range(2):
                    if n:
                        pe.wait_ge(wT_copied, 2 * n + half - 1)
                    for q in range(4):
                        kt = 4 * half + q
                        last = nc.tensor.transpose(psT[:, half, q * P:(q + 1) * P],
                                                   raw[:, n % 2, kt * P:(kt + 1) * P], ident[:, :])
                    last.then_inc(wT_full, 1)
            n0 = 2 * len(blocks)
            pe.wait_ge(raw1_loaded, 32)
            for m in range(2):
                pe.wait_ge(wT_copied, n0 + m - 1)
                for t in range(TT):
                    for ot in range(TT):
                        last = nc.tensor.transpose(psT[:, m, t * S + ot * P:t * S + (ot + 1) * P],
                                                   raw1[:, m, ot, t * P:(t + 1) * P], ident[:, :])
                last.then_inc(wT_full, 1)
            pe.wait_ge(preset, 1)
            pe.wait_ge(proj_loaded, 48)
            for kt in range(KT):
                last = nc.tensor.matmul(psL[0:1, 0:3 * NK1], ones[:, 0:1], wvpT[:, kt, KV0:CV],
                                        start=(kt == 0), stop=(kt == KT - 1))
            last.then_inc(colsum_full, 1)
            pe.wait_ge(colsum_copied, 1)
            for t in range(CT1):
                nc.tensor.matmul(psP[:, t, 0:NK1], rows1h[0:1, 0, t * P:(t + 1) * P], colsum[0:1, 0:NK1],
                                 start=True, stop=True)
            nc.tensor.matmul(psP[:, 2, 0:S], colsum[0:1, NK1:3 * NK1], rows1h[0:1, 1, :],
                             start=True, stop=True).then_inc(bias_full, 1)
            pe.wait_ge(bias_copied, 1)
            pe.wait_ge(wT_copied, n0 + 2)
            with pe.Fori(0, PAIRS) as i:
                for u in range(2):
                    b = 2 * i + u
                    pe.wait_ge(nat_loaded[u], 16 * i + 16)
                    for n in range(4):
                        pe.wait_ge((cT_dve, cT_act)[n % 2], 4 * i + 2 * u + n // 2 + 1)
                        for q in range(2):
                            for t in range(TT):
                                kt = 2 * n + q
                                last = nc.tensor.transpose(psT[:, n % 2, (q * TT + t) * P:(q * TT + t + 1) * P],
                                                           nat[:, u, t, kt * P:(kt + 1) * P], ident[:, :])
                        last.then_inc(psT_full[n % 2], 1)
                    pe.wait_ge(cT_dve, 4 * i + 2 * u + 3)
                    pe.wait_ge(cT_act, 4 * i + 2 * u + 3)
                    pe.wait_ge(out_act[1 - u], 4 * i + 4 * u + 1)
                    pe.wait_ge(out_dve[1 - u], 2 * i + 2 * u + 1)
                    for half in range(HALF0):
                        for kt in range(KT):
                            last = nc.tensor.matmul(psP[:, half, 0:S], wkT[:, kt, half * P:(half + 1) * P],
                                                    cT[:, u, kt, :], start=(kt == 0), stop=(kt == KT - 1))
                        last.then_inc(psP_full, 1)
                    for t in range(TT):
                        for kt in range(KT):
                            last = nc.tensor.matmul(psP[:, 2 + t, 0:CV], cT[:, u, kt, t * P:(t + 1) * P],
                                                    wvpT[:, kt, :], start=(kt == 0), stop=(kt == KT - 1))
                        last.then_inc(psP_full, 1)
                    pe.wait_ge(mid_ready, 4 * i + 2 * u + 2)
                    for ct in range(CT1):
                        for t in range(TT):
                            nc.tensor.matmul(psL[:, ct * NK1:(ct + 1) * NK1], w1T[:, 0, t, ct * P:(ct + 1) * P],
                                             mid[:, u, t, 0:NK1], start=(t == 0), stop=(t == TT - 1))
                    for t in range(TT):
                        last = nc.tensor.matmul(psL[:, P:P + S], mid[:, u, t, NK1:3 * NK1], w1T[:, 1, t, :],
                                                start=(t == 0), stop=(t == TT - 1))
                    last.then_inc(psL_full, 1)

        @block.vector
        def _(dve):
            dve.sem_inc(cT_dve, 1)
            for u in range(2):
                dve.sem_inc(out_dve[u], 1)
            for n in range(len(blocks)):
                for half in range(2):
                    dve.wait_ge(wT_full, 2 * n + half + 1)
                    dst = wkT[:, 4 * half:4 * half + 4, n * P:(n + 1) * P] if n < HALF0 else \
                        wvpT[:, 4 * half:4 * half + 4, (n - HALF0) * P:(n - HALF0 + 1) * P]
                    nc.vector.tensor_copy(dst, psT[:, half, :].rearrange("p (k n) -> p k n", k=4)).then_inc(wT_copied, 1)
            for m in range(2):
                dve.wait_ge(wT_full, 2 * len(blocks) + m + 1)
                for t in range(TT):
                    last = nc.vector.tensor_copy(w1T[:, m, t, :].rearrange("p (h c) -> p h c", h=NH1),
                                                 psT[:, m, t * S:(t + 1) * S].rearrange("p (c h) -> p h c", h=NH1))
                last.then_inc(wT_copied, 1)
            dve.wait_ge(small_loaded, 32)
            nc.vector.tensor_copy(rows1h[0:1, :, :].rearrange("p m (h c) -> p m h c", h=NH1),
                                  rows1[0:1, :, :].rearrange("p m (c h) -> p m h c", h=NH1))
            dve.wait_ge(colsum_full, 1)
            nc.vector.tensor_copy(colsum[0:1, :], psL[0:1, 0:3 * NK1]).then_inc(colsum_copied, 1)
            dve.wait_ge(bias_full, 1)
            nc.vector.tensor_copy(bias_k[:, :, :], psP[:, 0:CT1, 0:NK1])
            nc.vector.tensor_copy(bias_v[:, :], psP[:, 2, 0:S]).then_inc(bias_copied, 1)
            dve.wait_ge(bias_copied, 1)
            dve.wait_ge(preset, 2)
            with dve.Fori(0, PAIRS) as i:
                for u in range(2):
                    for n in (0, 2):
                        dve.wait_ge(psT_full[0], 4 * i + 2 * u + n // 2 + 1)
                        nc.vector.tensor_copy(cT[:, u, 2 * n:2 * n + 2, :],
                                              psT[:, 0, :].rearrange("p (k n) -> p k n", k=2)).then_inc(cT_dve, 1)
                    dve.wait_ge(out_stored[u], 16 * STORES * i + 1)
                    for half in range(HALF0):
                        dve.wait_ge(out_act[u], 4 * i + half + 2)
                        nc.vector.scalar_tensor_tensor(k0_lo[:, u, half, :], psP[:, half, 0:S], HD0 ** -0.5,
                                                       plain(k0_hi)[:, u, half, :], op0=ALU.mult, op1=ALU.subtract)
                    for t in range(TT):
                        dve.wait_ge(psP_full, 8 * i + 4 * u + 3 + t)
                        nc.vector.tensor_copy(mid[:, u, t, :], psP[:, 2 + t, KV0:CV]).then_inc(mid_ready, 1)
                    dve.wait_ge(psL_full, 2 * i + u + 1)
                    nc.vector.tensor_tensor(k1[:, u, :, :], psL[:, 0:P].rearrange("p (t n) -> p t n", t=CT1),
                                            bias_k[:, :, :], ALU.add).then_inc(out_dve[u], 1)
                    for odd in range(2):
                        lo, hi = odd * NK1, (odd + 1) * NK1

                        def heads(a):
                            return a.rearrange("p (m e c) -> p m e c", e=2, c=HD1)[:, :, odd, :]
                        last = nc.vector.tensor_tensor(v1[lo:hi, u, :, odd * HD1:(odd + 1) * HD1],
                                                       heads(psL[lo:hi, P:P + S]), heads(bias_v[lo:hi, :]), ALU.add)
                    last.then_inc(out_dve[u], 1)

        @block.scalar
        def _(act):
            act.sem_inc(cT_act, 1)
            for u in range(2):
                act.sem_inc(out_act[u], 1)
            with act.Fori(0, PAIRS) as i:
                for u in range(2):
                    for n in (1, 3):
                        act.wait_ge(psT_full[1], 4 * i + 2 * u + n // 2 + 1)
                        nc.scalar.copy(cT[:, u, 2 * n:2 * n + 2, :],
                                       psT[:, 1, :].rearrange("p (k n) -> p k n", k=2)).then_inc(cT_act, 1)
                    act.wait_ge(out_stored[u], 16 * STORES * i + 1)
                    for half in range(HALF0):
                        act.wait_ge(psP_full, 8 * i + 4 * u + 1 + half)
                        nc.scalar.mul(k0_hi[:, u, half, :], psP[:, half, 0:S], HD0 ** -0.5).then_inc(out_act[u], 1)
                    for t in range(TT):
                        act.wait_ge(mid_ready, 4 * i + 2 * u + 1 + t)
                        nc.scalar.copy(v0[:, u, t, :], psP[:, 2 + t, 0:KV0]).then_inc(out_act[u], 1)


class Norm:

    def __init__(self, nc, es, name, sh):
        def sb(n, shape):
            return es.enter_context(nc.sbuf_tensor(f"{name}_{n}", shape, F32))

        def sem(n):
            return es.enter_context(nc.semaphore(f"{name}_{n}"))
        self.nc, self.sh = nc, sh
        self.stats = sb("stats", [P, TT, 2, 6])
        self.moments = sb("moments", [P, TT, 2])
        self.tmp = sb("tmp", [P, 4, TT])
        self.rstd = sb("rstd", [P, TT])
        self.stats_done = sem("stats_done")
        self.moments_done = sem("moments_done")
        self.rstd_steps = sem("rstd_steps")
        self.normed = sem("normed")

    def moments_of(self, dve, b, x):
        nc = self.nc
        for t in range(TT):
            for h in range(2):
                last = nc.vector.bn_stats(self.stats[:, t, h, :], x[:, t, h * HALF_N:(h + 1) * HALF_N])
        last.then_inc(self.stats_done, 1)
        dve.wait_ge(self.stats_done, b + 1)
        hold(dve, self.sh)
        for t in range(TT):
            last = nc.vector.bn_aggr(self.moments[:, t, :], self.stats[:, t, :, :])
        last.then_inc(self.moments_done, 1)

    STEPS, STEPS_RMS = 2, 6

    def rstd_of(self, pool, b, rms):
        nc, tmp = self.nc, self.tmp
        steps = self.STEPS_RMS if rms else self.STEPS
        var, half = self.moments[:, :, 1], self.sh.minus_half[:, 0:TT]
        done = [0]

        def step(instruction):
            instruction.then_inc(self.rstd_steps, 1)
            done[0] += 1
            pool.wait_ge(self.rstd_steps, steps * b + done[0])
        pool.wait_ge(self.moments_done, b + 1)
        hold(pool, self.sh)
        step(nc.gpsimd.tensor_scalar(tmp[:, 0, :], var, LN_EPS, None, ALU.add))
        if not rms:
            step(nc.gpsimd.tensor_tensor(self.rstd[:, :], tmp[:, 0, :], half, ALU.pow))
            return
        step(nc.gpsimd.tensor_tensor(tmp[:, 1, :], tmp[:, 0, :], half, ALU.pow))
        step(nc.gpsimd.tensor_tensor(tmp[:, 2, :], tmp[:, 1, :], tmp[:, 1, :], ALU.mult))
        step(nc.gpsimd.tensor_tensor(tmp[:, 3, :], tmp[:, 2, :], var, ALU.mult))
        hold(pool, self.sh)
        step(nc.gpsimd.tensor_scalar(tmp[:, 2, :], tmp[:, 3, :], LN_EPS, None, ALU.add))
        nc.gpsimd.tensor_tensor(tmp[:, 3, :], tmp[:, 2, :], tmp[:, 0, :], ALU.mult).then_inc(self.rstd_mid, 1)
        pool.wait_ge(self.rstd_mid, b + 1)
        step(nc.gpsimd.tensor_tensor(self.rstd[:, :], tmp[:, 3, :], half, ALU.pow))

    def normalise(self, dve, b, x, out, steps):
        dve.wait_ge(self.rstd_steps, steps * b + steps)
        for t in range(TT):
            last = self.nc.vector.tensor_scalar(out[:, t, :], x[:, t, :], self.moments[:, t, 0:1],
                                                self.rstd[:, t:t + 1], ALU.subtract, ALU.mult)
        last.then_inc(self.normed, 1)


def plain(tile):
    return tile.bitcast(F32)


def attn0_stage(nc, sh, c, scratch):
    ident = sh.ident
    UNITS = KT * TT
    XFILLS = KT // 2
    Q_USES = XFILLS + KT
    QUAD = KT // 2
    BANK0_DVE = {0} | set(range(1, UNITS, 2))
    QUAD_DMAS = JH0 * 4
    COPY_STEP = {f + 1: f for f in range(XFILLS)}
    for t in range(KT - 1):
        COPY_STEP[XFILLS + 1 + 3 * (t // 2) + 2 * (t % 2)] = XFILLS + t
    with ExitStack() as es:
        def sb(name, shape, dt=F32):
            return es.enter_context(nc.sbuf_tensor("a_" + name, shape, dt))

        def sem(name):
            return es.enter_context(nc.semaphore("a_" + name))

        w_hi = sb("w_hi", [P, KT, D], F32R)
        w_lo = sb("w_lo", [P, KT, D], F32R)
        ln_w = sb("ln_w", [P, D])
        raw = sb("raw", [P, 2, D])
        x = sb("x", [P, 2, TT, D])
        xT_hi = sb("xT_hi", [P, KT, S], F32R)
        xT_lo = sb("xT_lo", [P, KT, S], F32R)
        q_hi = sb("q_hi", [P, KT, S], F32R)
        q_lo = sb("q_lo", [P, KT, S], F32R)
        q_stack = sb("q_stack", [P, KT, JH0, S], F32R)
        k_stack = sb("k_stack", [P, 2, NKV0, S], F32R)
        v0 = sb("v0", [P, 2, TT, KV0])
        prob = sb("prob", [P, 2, JH0, S])
        probT = sb("probT", [P, 2, TT, JH0, P])
        negmax = sb("negmax", [P, 2, JH0])
        sums = sb("sums", [P, 2, TT, JH0])
        recip_head = sb("recip_head", [P, 2, TT, JH0])
        recip = sb("recip", [P, 2, TT, JH0, HD0])
        recipT = sb("recipT", [P, S])
        oT = sb("oT", [P, KT, S])
        psS = es.enter_context(nc.psum_tensor("a_psS", [P, 4, HALF_N], F32))
        psT = es.enter_context(nc.psum_tensor("a_psT", [P, 2, HALF_N], F32))
        psO = es.enter_context(nc.psum_tensor("a_psO", [P, 2, S], F32))
        psQ = es.enter_context(nc.psum_tensor("a_psQ", [P, HALF_N], F32))
        norm = Norm(nc, es, "a_norm", sh)
        norm.rstd_mid = sem("rstd_mid")

        lnw_loaded = sem("lnw_loaded")
        raw_loaded = [sem(f"raw_loaded{u}") for u in range(2)]
        raw_scaled, whi_ready = sem("raw_scaled"), sem("whi_ready")
        w_full = sem("w_full")
        wlo_ready = sem("wlo_ready")
        x_loaded = [sem(f"x_loaded{u}") for u in range(2)]
        kv_loaded = [sem(f"kv_loaded{u}") for u in range(2)]
        psQ_full, psQ_hi = sem("psQ_full"), sem("psQ_hi")
        psQ_lo = sem("psQ_lo")
        q_stacked = [sem(f"q_stacked{h}") for h in range(2)]
        scores_full, max_ready, exp_done = sem("scores_full"), sem("max_ready"), sem("exp_done")
        psT_full = [sem(f"psT_full{p}") for p in range(2)]
        psT_copied = [sem(f"psT_copied{p}") for p in range(2)]
        head_ready, recip_ready = sem("head_ready"), sem("recip_ready")
        psO_full, recipT_ready = sem("psO_full"), sem("recipT_ready")
        o_ready = sem("o_ready")
        o_stored = [sem(f"o_stored{h}") for h in range(2)]

        block = es.enter_context(nc.Block())

        @block.sync
        def _(sp):
            sp.dma_start(ln_w[:, :], c["ln_w"].partition_broadcast(P)).then_inc(lnw_loaded, 16)
            for h in range(2):
                sp.sem_inc(q_stacked[h], 1)
                sp.sem_inc(o_stored[h], 1)

            def load_rows(half, r):
                rows = c["wq"].rearrange("(h j r c) d -> h j r c d", h=HALF0, j=JH0, r=REP0)
                for j in range(JH0):
                    sp.dma_start(raw[j * HD0:(j + 1) * HD0, r % 2, :],
                                 rows[bass.ds(half, 1), j, r].rearrange("h c d -> c (h d)")
                                 ).then_inc(raw_loaded[r % 2], 16)

            def load_x(b, u):
                sp.dma_start(x[:, u, :, :], c["x"][bass.ds(b, 1)].rearrange("b (t p) d -> p (b t) d", p=P)
                             ).then_inc(x_loaded[u], 16)

            def load_kv(b, u):
                for part, name in enumerate(("k0_hi", "k0_lo", "k0_hi", "k0_lo")):
                    sp.dma_start(plain(k_stack)[part * HD0:(part + 1) * HD0, u, :, :],
                                 scratch[name][bass.ds(b, 1)].rearrange("b (g c) s -> c (b g) s", c=HD0)
                                 ).then_inc(kv_loaded[u], 16)
                sp.dma_start(v0[:, u].rearrange("p a n -> p (a n)"),
                             scratch["v0"][bass.ds(b, 1)].rearrange("b p n -> p (b n)")).then_inc(kv_loaded[u], 16)

            def stack_quad(b, h):
                sp.wait_ge(psQ_lo, Q_USES * b + XFILLS + QUAD * (h + 1) + 1)
                tiles = slice(QUAD * h, QUAD * (h + 1))
                for part, src in enumerate((q_hi, q_hi, q_lo, q_lo)):
                    for j in range(JH0):
                        sp.dma_start(plain(q_stack)[part * HD0:(part + 1) * HD0, tiles, j, :],
                                     plain(src)[j * HD0:(j + 1) * HD0, tiles, :]).then_inc(q_stacked[h], 16)

            def store_quad(b, h):
                sp.wait_ge(o_ready, KT * b + QUAD * (h + 1) + 1)
                rows = scratch["o"].rearrange("b (h j r c) s -> b h j c r s", h=HALF0, j=JH0, r=REP0)
                for j in range(JH0):
                    sp.dma_start(rows[bass.ds(b, 1), h, j].rearrange("b c r s -> c (b r) s"),
                                 oT[j * HD0:(j + 1) * HD0, QUAD * h:QUAD * (h + 1), :]).then_inc(o_stored[h], 16)

            for u in range(2):
                load_x(u, u)
            with sp.Fori(0, HALF0) as half:
                for r in range(REP0):
                    sp.wait_ge(w_full, 2 * REP0 * half + 2 * r + 2)
                    load_rows(half, r)
            load_kv(0, 0)
            stack_quad(0, 0)

            def body(i, final):
                for u in range(2):
                    b = 2 * i + u
                    stack_quad(b, 1)
                    if not final:
                        sp.wait_ge(psQ_full, Q_USES * b + XFILLS)
                        load_x(b + 2, u)
                    if not (final and u == 1):
                        sp.wait_ge(o_ready, KT * b + 1)
                        load_kv(b + 1, 1 - u)
                    store_quad(b, 0)
                    if not (final and u == 1):
                        stack_quad(b + 1, 0)
                    store_quad(b, 1)

            with sp.Fori(0, PAIRS - 1) as i:
                body(i, False)
            body(PAIRS - 1, True)
            for h in range(2):
                sp.wait_ge(o_stored[h], 16 * JH0 * B + 1)

        @block.gpsimd
        def _(pool):
            for b in range(2):
                norm.rstd_of(pool, b, rms=True)
            pool.wait_ge(lnw_loaded, 16)
            with pool.Fori(0, KT // 2) as i:
                for u in range(2):
                    pool.wait_ge(raw_loaded[u], 16 * JH0 * i + 16 * JH0)
                    nc.gpsimd.tensor_tensor(raw[:, u, :], raw[:, u, :], ln_w[:, :], ALU.mult).then_inc(raw_scaled, 1)

            def spread_reciprocals(b, t):
                pool.wait_ge(head_ready, KT * b + t + 1)
                hold(pool, sh)
                nc.gpsimd.tensor_copy(recip[:, t % 2], recip_head[:, t % 2].unsqueeze(3).broadcast_to([P, TT, JH0, HD0])
                                      ).then_inc(recip_ready, 1)

            def body(i, final):
                for u in range(2):
                    b = 2 * i + u
                    for t in range(KT):
                        spread_reciprocals(b, t)
                        if t == 3 and not final:
                            norm.rstd_of(pool, b + 2, rms=True)

            with pool.Fori(0, PAIRS - 1) as i:
                body(i, False)
            body(PAIRS - 1, True)

        @block.tensor
        def _(pe):
            pe.sem_inc(w_full, 4)
            with pe.Fori(0, KT // 2) as i:
                for u in range(2):
                    pe.wait_ge(raw_scaled, 2 * i + u + 1)
                    for half in range(2):
                        bank = 2 * u + half
                        pe.wait_ge(wlo_ready, 4 * i + bank + 1)
                        for q in range(4):
                            kt = 4 * half + q
                            last = nc.tensor.transpose(psS[:, bank, q * P:(q + 1) * P],
                                                       raw[:, u, kt * P:(kt + 1) * P], ident[:, :])
                        last.then_inc(w_full, 1)
            pe.wait_ge(wlo_ready, 2 * KT + 4)

            def transposed_x(b, u, f):
                if f == 0:
                    pe.wait_ge(norm.normed, b + 1)
                pe.wait_ge(psQ_lo, Q_USES * b + f + 1)
                for q in range(2):
                    for t in range(TT):
                        kt = 2 * f + q
                        last = nc.tensor.transpose(psQ[:, (q * TT + t) * P:(q * TT + t + 1) * P],
                                                   x[:, u, t, kt * P:(kt + 1) * P], ident[:, :])
                last.then_inc(psQ_full, 1)

            def query(b, t, tiles):
                if tiles[0] == 0:
                    pe.wait_ge(psQ_lo, Q_USES * b + XFILLS + t + 1)
                for kt in tiles:
                    for w, a in ((w_hi, xT_hi), (w_lo, xT_hi), (w_hi, xT_lo)):
                        last = nc.tensor.matmul(psQ[:, 0:S], w[:, kt, t * P:(t + 1) * P], a[:, kt, :],
                                                start=(kt == 0 and w is w_hi and a is xT_hi),
                                                stop=(kt == KT - 1 and a is xT_lo))
                if tiles[-1] == KT - 1:
                    last.then_inc(psQ_full, 1)

            def query_step(b, u, n):
                if n < XFILLS:
                    transposed_x(b, u, n)
                    return
                three, part = (n - XFILLS) // 3, (n - XFILLS) % 3
                if part == 0:
                    query(b, 2 * three, range(KT))
                else:
                    query(b, 2 * three + 1, range((part - 1) * KT // 2, part * KT // 2))

            def scores(b, i, u, n):
                t, qb = n // TT, n % TT
                if n % (UNITS // 2) == 0:
                    pe.wait_ge(q_stacked[t // QUAD], 16 * QUAD_DMAS * (b + 1) + 1)
                if n == 0:
                    pe.wait_ge(kv_loaded[u], 16 * 5 * (i + 1))
                for j in range(JH0):
                    last = nc.tensor.matmul(psS[:, 2 * (n % 2) + j // 2, (j % 2) * S:(j % 2 + 1) * S],
                                            q_stack[:, t, j, qb * P:(qb + 1) * P],
                                            k_stack[:, u, (t // REP0) * JH0 + j, :], start=True, stop=True)
                last.then_inc(scores_full, 1)

            def transposes(b, n):
                pe.wait_ge(exp_done, UNITS * b + n + 1)
                for kt in range(TT):
                    pe.wait_ge(psT_copied[kt], UNITS * b + n + 1)
                    for j in range(JH0):
                        last = nc.tensor.transpose(psT[:, kt, j * P:(j + 1) * P],
                                                   prob[:, n % 2, j, kt * P:(kt + 1) * P], ident[:, :])
                    last.then_inc(psT_full[kt], 1)

            def values(b, u, n):
                t, qb = n // TT, n % TT
                if qb == 0:
                    pe.wait_ge(o_ready, KT * b + t + 1)
                for kt in range(TT):
                    pe.wait_ge(psT_copied[kt], UNITS * b + n + 2)
                for kt in range(TT):
                    for j in range(JH0):
                        head = (t // REP0) * JH0 + j
                        nc.tensor.matmul(psO[j * HD0:(j + 1) * HD0, 0, qb * P:(qb + 1) * P],
                                         v0[:, u, kt, head * HD0:(head + 1) * HD0], probT[:, n % 2, kt, j, :],
                                         start=(kt == 0), stop=(kt == TT - 1))
                if qb == TT - 1:
                    pe.wait_ge(recip_ready, KT * b + t + 1)
                    for s in range(TT):
                        last = nc.tensor.transpose(psO[:, 1, s * P:(s + 1) * P],
                                                   recip[:, t % 2, s, :, :].rearrange("p j c -> p (j c)"), ident[:, :])
                    last.then_inc(psO_full, 1)

            for f in range(XFILLS):
                transposed_x(0, 0, f)
            for t in range(KT):
                query(0, t, range(KT))
            scores(0, 0, 0, 0)
            scores(0, 0, 0, 1)

            def body(i, final):
                for u in range(2):
                    b = 2 * i + u
                    more = not (final and u == 1)
                    for n in range(UNITS):
                        transposes(b, n)
                        if n + 2 < UNITS:
                            scores(b, i, u, n + 2)
                        elif more:
                            scores(b + 1, i + u, 1 - u, n + 2 - UNITS)
                        if n:
                            values(b, u, n - 1)
                        if more:
                            query_step(b + 1, 1 - u, n)
                    values(b, u, UNITS - 1)

            with pe.Fori(0, PAIRS - 1) as i:
                body(i, False)
            body(PAIRS - 1, True)

        @block.vector
        def _(dve):
            dve.sem_inc(wlo_ready, 4)
            dve.sem_inc(psT_copied[0], 1)
            dve.sem_inc(psQ_lo, 1)
            dve.sem_inc(o_ready, 1)
            for b in range(2):
                dve.wait_ge(x_loaded[b], 16)
                norm.moments_of(dve, b, x[:, b])
                norm.normalise(dve, b, x[:, b], x[:, b], norm.STEPS_RMS)
            with dve.Fori(0, KT // 2) as i:
                for u in range(2):
                    for half in range(2):
                        bank = 2 * u + half
                        dve.wait_ge(whi_ready, 4 * i + bank + 1)
                        cols = bass.ds((2 * i + u) * P, P)
                        nc.vector.tensor_tensor(w_lo[:, 4 * half:4 * half + 4, cols],
                                                psS[:, bank, :].rearrange("p (k n) -> p k n", k=4),
                                                plain(w_hi)[:, 4 * half:4 * half + 4, cols],
                                                ALU.subtract).then_inc(wlo_ready, 1)

            def split(b, use):
                dve.wait_ge(psQ_full, Q_USES * b + use + 1)
                if use < XFILLS:
                    cols = slice(2 * use, 2 * use + 2)
                    hi, lo, src = xT_hi[:, cols, :], xT_lo[:, cols, :], psQ[:, :].rearrange("p (k n) -> p k n", k=2)
                    high = plain(xT_hi)[:, cols, :]
                else:
                    t = use - XFILLS
                    if t % QUAD == 0:
                        dve.wait_ge(q_stacked[t // QUAD], 16 * QUAD_DMAS * b + 1)
                    hi, lo, src, high = q_hi[:, t, :], q_lo[:, t, :], psQ[:, 0:S], plain(q_hi)[:, t, :]
                nc.vector.tensor_copy(hi, src).then_inc(psQ_hi, 1)
                dve.wait_ge(psQ_hi, Q_USES * b + use + 1)
                nc.vector.tensor_tensor(lo, src, high, ALU.subtract).then_inc(psQ_lo, 1)

            def maximum(b, n):
                dve.wait_ge(scores_full, UNITS * b + n + 1)
                bank = 2 * (n % 2)
                nc.vector.tensor_reduce(negmax[:, n % 2, :], psS[:, bank:bank + 2, :].rearrange("p a (j k) -> p (a j) k", k=S),
                                        AX_X, ALU.max, negate=True).then_inc(max_ready, 1)

            def normalise_o(b, t):
                if t % QUAD == 0:
                    dve.wait_ge(o_stored[t // QUAD], 16 * JH0 * b + 1)
                dve.wait_ge(psO_full, KT * b + t + 1)
                nc.vector.tensor_copy(recipT[:, :], psO[:, 1, :]).then_inc(recipT_ready, 1)
                dve.wait_ge(recipT_ready, KT * b + t + 1)
                nc.vector.tensor_tensor(oT[:, t, :], psO[:, 0, :], recipT[:, :], ALU.mult).then_inc(o_ready, 1)

            for use in range(Q_USES - 1):
                split(0, use)
            maximum(0, 0)
            maximum(0, 1)

            def body(i, final):
                for u in range(2):
                    b = 2 * i + u
                    more = not (final and u == 1)
                    for n in range(UNITS):
                        if n == 0:
                            split(b, Q_USES - 1)
                        elif n in COPY_STEP and more:
                            split(b + 1, COPY_STEP[n])
                        if n in BANK0_DVE:
                            dve.wait_ge(psT_full[0], UNITS * b + n + 1)
                            nc.vector.tensor_copy(probT[:, n % 2, 0, :, :],
                                                  psT[:, 0, :].rearrange("p (j q) -> p j q", j=JH0)).then_inc(psT_copied[0], 1)
                        if n % 2:
                            t = n // 2
                            dve.wait_ge(exp_done, UNITS * b + n + 1)
                            nc.vector.reciprocal(recip_head[:, t % 2], sums[:, t % 2]).then_inc(head_ready, 1)
                        if n + 2 < UNITS:
                            maximum(b, n + 2)
                        elif more:
                            maximum(b + 1, n + 2 - UNITS)
                        if n and n % 2 == 0:
                            normalise_o(b, n // 2 - 1)
                        if n == 6 and not final:
                            dve.wait_ge(x_loaded[u], 16 * i + 32)
                            norm.moments_of(dve, b + 2, x[:, u])
                        if n == 12 and not final:
                            norm.normalise(dve, b + 2, x[:, u], x[:, u], norm.STEPS_RMS)
                    normalise_o(b, KT - 1)

            with dve.Fori(0, PAIRS - 1) as i:
                body(i, False)
            body(PAIRS - 1, True)

        @block.scalar
        def _(act):
            act.sem_inc(psT_copied[1], 1)
            with act.Fori(0, KT // 2) as i:
                for u in range(2):
                    for half in range(2):
                        bank = 2 * u + half
                        act.wait_ge(w_full, 4 * i + bank + 5)
                        nc.scalar.copy(w_hi[:, 4 * half:4 * half + 4, bass.ds((2 * i + u) * P, P)],
                                       psS[:, bank, :].rearrange("p (k n) -> p k n", k=4)).then_inc(whi_ready, 1)

            def exponentials(b, n):
                act.wait_ge(max_ready, UNITS * b + n + 1)
                t, qb = n // TT, n % TT
                for j in range(JH0):
                    last = nc.scalar.activation(prob[:, n % 2, j, :],
                                                psS[:, 2 * (n % 2) + j // 2, (j % 2) * S:(j % 2 + 1) * S], ACT.Exp,
                                                bias=negmax[:, n % 2, j:j + 1], accum_out=sums[:, t % 2, qb, j:j + 1])
                last.then_inc(exp_done, 1)

            exponentials(0, 0)
            exponentials(0, 1)

            def body(i, final):
                for u in range(2):
                    b = 2 * i + u
                    more = not (final and u == 1)
                    for n in range(UNITS):
                        for kt in range(TT):
                            if kt == 0 and n in BANK0_DVE:
                                continue
                            act.wait_ge(psT_full[kt], UNITS * b + n + 1)
                            nc.scalar.copy(probT[:, n % 2, kt, :, :],
                                           psT[:, kt, :].rearrange("p (j q) -> p j q", j=JH0)).then_inc(psT_copied[kt], 1)
                        if n + 2 < UNITS:
                            exponentials(b, n + 2)
                        elif more:
                            exponentials(b + 1, n + 2 - UNITS)

            with act.Fori(0, PAIRS - 1) as i:
                body(i, False)
            body(PAIRS - 1, True)


def proj0_stage(nc, sh, c, scratch):
    ident = sh.ident
    with ExitStack() as es:
        def sb(name, shape, dt=F32):
            return es.enter_context(nc.sbuf_tensor("p_" + name, shape, dt))

        def sem(name):
            return es.enter_context(nc.semaphore("p_" + name))

        w_hi = sb("w_hi", [P, KT, D], F32R)
        w_lo = sb("w_lo", [P, KT, D], F32R)
        raw = sb("raw", [P, 2, D])
        oT = sb("oT", [P, 2, KT, S])
        o_hi = sb("o_hi", [P, KT, S], F32R)
        o_lo = sb("o_lo", [P, KT, S], F32R)
        x = sb("x", [P, 2, TT, D])
        psW = es.enter_context(nc.psum_tensor("p_psW", [P, 4, HALF_N], F32))
        psY = es.enter_context(nc.psum_tensor("p_psY", [P, 4, HALF_N], F32))

        raw_loaded = [sem(f"raw_loaded{u}") for u in range(2)]
        w_full, whi_ready = sem("w_full"), sem("whi_ready")
        wlo_ready = sem("wlo_ready")
        o_loaded = [sem(f"o_loaded{u}") for u in range(2)]
        x_loaded = [sem(f"x_loaded{u}") for u in range(2)]
        ohi_ready, olo_ready, psY_full = sem("ohi_ready"), sem("olo_ready"), sem("psY_full")
        x1_ready = sem("x1_ready")
        x1_stored = [sem(f"x1_stored{u}") for u in range(2)]

        block = es.enter_context(nc.Block())

        @block.sync
        def _(sp):
            def load_rows(rb, u):
                sp.dma_start(raw[:, u, :], c["wo"][bass.ds(rb * P, P), :]).then_inc(raw_loaded[u], 16)

            def load_batch(b, u):
                sp.dma_start(oT[:, u, :, :], scratch["o"][bass.ds(b, 1)].rearrange("b (k p) s -> p (b k) s", p=P)
                             ).then_inc(o_loaded[u], 16)
                sp.dma_start(x[:, u, :, :], c["x"][bass.ds(b, 1)].rearrange("b (t p) d -> p (b t) d", p=P)
                             ).then_inc(x_loaded[u], 16)

            def store_batch(i, u):
                sp.wait_ge(x1_ready, 4 * (2 * i + u) + 8)
                sp.dma_start(scratch["x1"][bass.ds(2 * i + u, 1)].rearrange("b (t p) d -> p (b t) d", p=P),
                             x[:, u, :, :]).then_inc(x1_stored[u], 16)

            for u in range(2):
                load_rows(u, u)
            with sp.Fori(1, KT // 2) as i:
                for u in range(2):
                    sp.wait_ge(w_full, 4 * i + 2 * u - 2)
                    load_rows(2 * i + u, u)
            for u in range(2):
                load_batch(u, u)
            with sp.Fori(0, PAIRS - 1) as i:
                for u in range(2):
                    store_batch(i, u)
                    sp.wait_ge(x1_stored[u], 16 * i + 16)
                    load_batch(2 * i + u + 2, u)
            for u in range(2):
                store_batch(PAIRS - 1, u)
            for u in range(2):
                sp.wait_ge(x1_stored[u], 16 * PAIRS)

        @block.tensor
        def _(pe):
            with pe.Fori(0, KT // 2) as i:
                for u in range(2):
                    pe.wait_ge(raw_loaded[u], 16 * i + 16)
                    for half in range(2):
                        bank = 2 * u + half
                        pe.wait_ge(wlo_ready, 4 * i + bank + 1)
                        for q in range(4):
                            kt = 4 * half + q
                            last = nc.tensor.transpose(psW[:, bank, q * P:(q + 1) * P],
                                                       raw[:, u, kt * P:(kt + 1) * P], ident[:, :])
                        last.then_inc(w_full, 1)
            pe.wait_ge(wlo_ready, 2 * KT + 4)
            with pe.Fori(0, B) as b:
                for t in range(TT):
                    for h in range(2):
                        pe.wait_ge(x1_ready, 4 * b + 2 * t + h + 1)
                        for kt in range(KT):
                            if t == 0 and h == 0 and kt % 2 == 0:
                                pe.wait_ge(olo_ready, 4 * b + kt // 2 + 1)
                            for a, w in ((o_hi, w_hi), (o_hi, w_lo), (o_lo, w_hi)):
                                last = nc.tensor.matmul(psY[:, 2 * t + h, :], a[:, kt, t * P:(t + 1) * P],
                                                        w[:, kt, h * HALF_N:(h + 1) * HALF_N],
                                                        start=(kt == 0 and a is o_hi and w is w_hi),
                                                        stop=(kt == KT - 1 and a is o_lo))
                        last.then_inc(psY_full, 1)

        @block.vector
        def _(dve):
            dve.sem_inc(wlo_ready, 4)
            dve.sem_inc(x1_ready, 4)
            with dve.Fori(0, KT // 2) as i:
                for u in range(2):
                    for half in range(2):
                        bank = 2 * u + half
                        dve.wait_ge(whi_ready, 4 * i + bank + 1)
                        cols = bass.ds((2 * i + u) * P, P)
                        nc.vector.tensor_tensor(w_lo[:, 4 * half:4 * half + 4, cols],
                                                psW[:, bank, :].rearrange("p (k n) -> p k n", k=4),
                                                plain(w_hi)[:, 4 * half:4 * half + 4, cols],
                                                ALU.subtract).then_inc(wlo_ready, 1)
            with dve.Fori(0, PAIRS) as i:
                for u in range(2):
                    b = 2 * i + u
                    for n in range(4):
                        dve.wait_ge(ohi_ready, 4 * b + n + 1)
                        cols = slice(2 * n, 2 * n + 2)
                        nc.vector.tensor_tensor(o_lo[:, cols, :], oT[:, u, cols, :], plain(o_hi)[:, cols, :],
                                                ALU.subtract).then_inc(olo_ready, 1)
                    dve.wait_ge(x_loaded[u], 16 * i + 16)
                    for t in range(TT):
                        for h in range(2):
                            dve.wait_ge(psY_full, 4 * b + 2 * t + h + 1)
                            cols = slice(h * HALF_N, (h + 1) * HALF_N)
                            nc.vector.scalar_tensor_tensor(x[:, u, t, cols], psY[:, 2 * t + h, :], sh.gates[:, 0:1],
                                                           x[:, u, t, cols], op0=ALU.mult, op1=ALU.add
                                                           ).then_inc(x1_ready, 1)

        @block.scalar
        def _(act):
            with act.Fori(0, KT // 2) as i:
                for u in range(2):
                    for half in range(2):
                        bank = 2 * u + half
                        act.wait_ge(w_full, 4 * i + bank + 1)
                        nc.scalar.copy(w_hi[:, 4 * half:4 * half + 4, bass.ds((2 * i + u) * P, P)],
                                       psW[:, bank, :].rearrange("p (k n) -> p k n", k=4)).then_inc(whi_ready, 1)

            def high_parts(i, u, b, first):
                act.wait_ge(o_loaded[u], 16 * i + 16)
                if not first:
                    act.wait_ge(psY_full, 4 * b)
                for n in range(4):
                    cols = slice(2 * n, 2 * n + 2)
                    nc.scalar.copy(o_hi[:, cols, :], oT[:, u, cols, :]).then_inc(ohi_ready, 1)

            high_parts(0, 0, 0, True)
            high_parts(0, 1, 1, False)
            with act.Fori(1, PAIRS) as i:
                for u in range(2):
                    high_parts(i, u, 2 * i + u, False)


def ffn0_stage(nc, sh, c, scratch):
    ident = sh.ident
    with ExitStack() as es:
        def sb(name, shape, dt=F32):
            return es.enter_context(nc.sbuf_tensor("f_" + name, shape, dt))

        def sem(name):
            return es.enter_context(nc.semaphore("f_" + name))

        coefs = sb("coefs", [P, NE, KT, RR])
        masks = sb("masks", [P, NE, KT, RR], U8)
        masked = sb("masked", [P, NE, KT, RR])
        wsum = sb("wsum", [P, KT, RR])
        table = sb("table", [P, KT, D])
        update = sb("update", [P, D])
        enc = sb("enc", [P, D])
        raw = sb("raw", [P, 2, KT, P])
        wpart = sb("wpart", [P, 2, HALF_N])
        wfull = sb("wfull", [P, 2, HALF_N])
        w_hi = sb("w_hi", [P, KT, D], F32R)
        w_lo = sb("w_lo", [P, KT, D], F32R)
        bias = sb("bias", [P, D])
        x = sb("x", [P, 2, TT, D])
        xn = sb("xn", [P, TT, D])
        xT_hi = sb("xT_hi", [P, 2, KT, S], F32R)
        xT_lo = sb("xT_lo", [P, 2, KT, S], F32R)
        y = sb("y", [P, 2, TT, D])
        psT = es.enter_context(nc.psum_tensor("f_psT", [P, 4, HALF_N], F32))
        psY = es.enter_context(nc.psum_tensor("f_psY", [P, 4, HALF_N], F32))
        norm = Norm(nc, es, "f_norm", sh)

        coefs_loaded, table_loaded, enc_loaded, bias_loaded = (
            sem("coefs_loaded"), sem("table_loaded"), sem("enc_loaded"), sem("bias_loaded"))
        zeroed, masked_done, summed, bias_gated = sem("zeroed"), sem("masked_done"), sem("summed"), sem("bias_gated")
        update_full, update_copied = sem("update_full"), sem("update_copied")
        raw_loaded = [sem(f"raw_loaded{u}") for u in range(2)]
        w_full, part_copied, full_ready, hi_ready = sem("w_full"), sem("part_copied"), sem("full_ready"), sem("hi_ready")
        lo_ready = sem("lo_ready")
        x_loaded = [sem(f"x_loaded{u}") for u in range(2)]
        y_stored = [sem(f"y_stored{u}") for u in range(2)]
        psT_full, xhi_ready, xlo_ready = sem("psT_full"), sem("xhi_ready"), sem("xlo_ready")
        biased, psY_full, y_ready = sem("biased"), sem("psY_full"), sem("y_ready")

        block = es.enter_context(nc.Block())

        @block.sync
        def _(sp):
            for name, lo, r in (("0", 0, R0), ("1", R0, R1)):
                for e in range(NE):
                    sp.dma_start(coefs[:, e, :, lo:lo + r],
                                 c["coefs" + name][e].rearrange("(t p) r -> p t r", p=P)).then_inc(coefs_loaded, 16)
                    sp.dma_start(masks[:, e, :, lo:lo + r],
                                 c["mask" + name][e].rearrange("(t p) r -> p t r", p=P)).then_inc(coefs_loaded, 16)
            sp.dma_start(table[:, :, :], c["irfft"].rearrange("(t p) o -> p t o", p=P)).then_inc(table_loaded, 16)
            sp.wait_ge(zeroed, 2)
            sp.dma_start(enc[0:R0, :], c["enc0"]).then_inc(enc_loaded, 16)
            sp.dma_start(enc[R0:RR, :], c["enc1"]).then_inc(enc_loaded, 16)
            sp.dma_start(bias[:, :], c["b_base"].partition_broadcast(P)).then_inc(bias_loaded, 16)

            def load_columns(kt, u):
                sp.dma_start(raw[:, u, :, :], c["W_base"][:, bass.ds(kt * P, P)].rearrange("(t p) d -> p t d", p=P)
                             ).then_inc(raw_loaded[u], 16)

            def load_x(b, u):
                sp.dma_start(x[:, u, :, :], scratch["x1"][bass.ds(b, 1)].rearrange("b (t p) d -> p (b t) d", p=P)
                             ).then_inc(x_loaded[u], 16)

            for u in range(2):
                load_columns(u, u)
            for u in range(2):
                load_x(u, u)
                sp.sem_inc(y_stored[u], 1)
            with sp.Fori(1, KT // 2) as i:
                for u in range(2):
                    sp.wait_ge(w_full, 4 * i + 2 * u - 2)
                    load_columns(2 * i + u, u)

            def store(i, u):
                sp.wait_ge(y_ready, 8 * i + 4 * u + 4)
                sp.dma_start(scratch["x2"][bass.ds(2 * i + u, 1)].rearrange("b (t p) d -> p (b t) d", p=P),
                             y[:, u, :, :]).then_inc(y_stored[u], 16)

            with sp.Fori(0, PAIRS - 1) as i:
                for u in range(2):
                    store(i, u)
                    load_x(2 * i + 2 + u, u)
            for u in range(2):
                store(PAIRS - 1, u)
            for u in range(2):
                sp.wait_ge(y_stored[u], 16 * PAIRS + 1)

        @block.gpsimd
        def _(pool):
            nc.gpsimd.memset(update[:, :], 0.0).then_inc(zeroed, 1)
            nc.gpsimd.memset(enc[:, :], 0.0).then_inc(zeroed, 1)
            pool.wait_ge(zeroed, 2)
            pool.sem_inc(lo_ready, 2)
            with pool.Fori(0, KT) as kt:
                for h in range(2):
                    pool.wait_ge(hi_ready, 2 * kt + h + 1)
                    dst = bass.ds(h * HALF_N, HALF_N)
                    nc.gpsimd.tensor_tensor(w_lo[:, bass.ds(kt, 1), dst].rearrange("p a n -> p (a n)"), wfull[:, h, :],
                                            plain(w_hi)[:, bass.ds(kt, 1), dst].rearrange("p a n -> p (a n)"),
                                            ALU.subtract).then_inc(lo_ready, 1)
            norm.rstd_of(pool, 0, rms=False)
            pool.wait_ge(bias_gated, 1)

            def body(i, final):
                for u in range(2):
                    b = 2 * i + u
                    pool.wait_ge(norm.normed, b + 1)
                    for t in range(TT):
                        nc.gpsimd.tensor_tensor(x[:, u, t, :], x[:, u, t, :], bias[:, :], ALU.add).then_inc(biased, 1)
                    if not (final and u == 1):
                        norm.rstd_of(pool, b + 1, rms=False)

            with pool.Fori(0, PAIRS - 1) as i:
                body(i, False)
            body(PAIRS - 1, True)

        @block.tensor
        def _(pe):
            pe.wait_ge(summed, 1)
            pe.wait_ge(table_loaded, 16)
            for h in range(2):
                for kt in range(KT):
                    last = nc.tensor.matmul(psY[0:RR, h, :], wsum[:, kt, :], table[:, kt, h * HALF_N:(h + 1) * HALF_N],
                                            start=(kt == 0), stop=(kt == KT - 1))
                last.then_inc(update_full, 1)
            pe.wait_ge(update_copied, 2)
            pe.wait_ge(enc_loaded, 32)

            def weight_tile(kt, u, enc_cols):
                for h in range(2):
                    for q in range(4):
                        nc.tensor.transpose(psT[:, h, q * P:(q + 1) * P], raw[:, u, 4 * h + q, :], ident[:, :])
                    nc.tensor.matmul(psY[:, h, :], enc_cols, update[:, h * HALF_N:(h + 1) * HALF_N],
                                     start=True, stop=True).then_inc(w_full, 1)

            for kt in range(KT):
                pe.wait_ge(raw_loaded[kt % 2], 16 * (kt // 2 + 1))
                if kt:
                    pe.wait_ge(part_copied, 2 * kt)
                    pe.wait_ge(full_ready, 2 * kt)
                weight_tile(kt, kt % 2, enc[:, kt * P:(kt + 1) * P])

            def transposes(b):
                pe.wait_ge(norm.normed, b + 1)
                if not (isinstance(b, int) and b == 0):
                    pe.wait_ge(xlo_ready, 4 * b)
                for n in range(4):
                    for q in range(2):
                        for t in range(TT):
                            last = nc.tensor.transpose(psT[:, n, (q * TT + t) * P:(q * TT + t + 1) * P],
                                                       xn[:, t, (2 * n + q) * P:(2 * n + q + 1) * P], ident[:, :])
                    last.then_inc(psT_full, 1)

            pe.wait_ge(part_copied, 2 * KT)
            transposes(0)
            pe.wait_ge(lo_ready, 2 * KT + 2)

            def body(i, final):
                for u in range(2):
                    b = 2 * i + u
                    pe.wait_ge(xlo_ready, 4 * b + 4)
                    for t in range(TT):
                        for h in range(2):
                            if not (isinstance(i, int) and i == 0 and u == 0):
                                pe.wait_ge(y_ready, 4 * b + 2 * t + h - 3)
                            for kt in range(KT):
                                rows = slice(t * P, (t + 1) * P)
                                cols = slice(h * HALF_N, (h + 1) * HALF_N)
                                for a, w in ((xT_hi, w_hi), (xT_hi, w_lo), (xT_lo, w_hi)):
                                    last = nc.tensor.matmul(psY[:, 2 * t + h, :], a[:, u, kt, rows], w[:, kt, cols],
                                                            start=(kt == 0 and a is xT_hi and w is w_hi),
                                                            stop=(kt == KT - 1 and a is xT_lo))
                            last.then_inc(psY_full, 1)
                        if t == 0 and not (final and u == 1):
                            transposes(b + 1)

            body(0, False)
            with pe.Fori(1, PAIRS - 1) as i:
                body(i, False)
            body(PAIRS - 1, True)

        @block.vector
        def _(dve):
            dve.wait_ge(coefs_loaded, 16 * 4 * NE)
            nc.vector.tensor_tensor(masked[:, :, :, :], coefs[:, :, :, :], masks[:, :, :, :], ALU.mult).then_inc(masked_done, 1)
            dve.wait_ge(masked_done, 1)
            nc.vector.tensor_tensor(wsum[:, :, :], masked[:, 0, :, :], masked[:, 1, :, :], ALU.add).then_inc(masked_done, 1)
            dve.wait_ge(masked_done, 2)
            nc.vector.tensor_tensor(wsum[:, :, :], wsum[:, :, :], masked[:, 2, :, :], ALU.add).then_inc(summed, 1)
            dve.wait_ge(bias_loaded, 16)
            nc.vector.tensor_scalar(bias[:, :], bias[:, :], sh.gates[:, 2:3], None, ALU.mult).then_inc(bias_gated, 1)
            dve.wait_ge(zeroed, 1)
            for h in range(2):
                dve.wait_ge(update_full, h + 1)
                nc.vector.tensor_scalar(update[0:RR, h * HALF_N:(h + 1) * HALF_N], psY[0:RR, h, :], 0.5, None, ALU.mult
                                        ).then_inc(update_copied, 1)
            with dve.Fori(0, KT) as kt:
                for h in range(2):
                    dve.wait_ge(lo_ready, 2 * kt + h + 1)
                    dve.wait_ge(part_copied, 2 * kt + h + 1)
                    nc.vector.tensor_tensor(wfull[:, h, :], wpart[:, h, :], psY[:, h, :], ALU.add).then_inc(full_ready, 1)

            def moments(i, u, b):
                dve.wait_ge(x_loaded[u], 16 * i + 16)
                norm.moments_of(dve, b, x[:, u])

            moments(0, 0, 0)
            norm.normalise(dve, 0, x[:, 0], xn, norm.STEPS)

            def split_low(b, u):
                for n in range(4):
                    dve.wait_ge(xhi_ready, 4 * b + n + 1)
                    cols = slice(2 * n, 2 * n + 2)
                    nc.vector.tensor_tensor(xT_lo[:, u, cols, :].rearrange("p k n -> p (k n)"), psT[:, n, :],
                                            plain(xT_hi)[:, u, cols, :].rearrange("p k n -> p (k n)"),
                                            ALU.subtract).then_inc(xlo_ready, 1)

            split_low(0, 0)

            def body(i, final):
                for u in range(2):
                    b = 2 * i + u
                    if not (final and u == 1):
                        moments(i + u, 1 - u, b + 1)
                        norm.normalise(dve, b + 1, x[:, 1 - u], xn, norm.STEPS)
                        split_low(b + 1, 1 - u)
                    dve.wait_ge(biased, 2 * b + 2)
                    dve.wait_ge(y_stored[u], 16 * i + 1)
                    for t in range(TT):
                        for h in range(2):
                            dve.wait_ge(psY_full, 4 * b + 2 * t + h + 1)
                            cols = slice(h * HALF_N, (h + 1) * HALF_N)
                            nc.vector.scalar_tensor_tensor(y[:, u, t, cols], psY[:, 2 * t + h, :], sh.gates[:, 2:3],
                                                           x[:, u, t, cols], op0=ALU.mult, op1=ALU.add
                                                           ).then_inc(y_ready, 1)

            with dve.Fori(0, PAIRS - 1) as i:
                body(i, False)
            body(PAIRS - 1, True)

        @block.scalar
        def _(act):
            def weight_part(kt, h, n):
                act.wait_ge(w_full, n + 1)
                nc.scalar.copy(wpart[:, h, :], psT[:, h, :]).then_inc(part_copied, 1)

            def weight_high(kt, h, n):
                act.wait_ge(full_ready, n + 1)
                nc.scalar.copy(w_hi[:, bass.ds(kt, 1), h * HALF_N:(h + 1) * HALF_N].rearrange("p a n -> p (a n)"),
                               wfull[:, h, :]).then_inc(hi_ready, 1)

            with act.Fori(0, KT) as kt:
                for h in range(2):
                    weight_part(kt, h, 2 * kt + h)
                for h in range(2):
                    weight_high(kt, h, 2 * kt + h)
            with act.Fori(0, PAIRS) as i:
                for u in range(2):
                    b = 2 * i + u
                    for n in range(4):
                        act.wait_ge(psT_full, 4 * b + n + 1)
                        nc.scalar.copy(xT_hi[:, u, 2 * n:2 * n + 2, :].rearrange("p k n -> p (k n)"), psT[:, n, :]
                                       ).then_inc(xhi_ready, 1)


def attn1_stage(nc, sh, c, scratch):
    ident = sh.ident
    NT = D // P
    WIDTH = NH1 * NK1
    T_USES, O_USES = NT, 8
    NQ = 2 * CT1
    with ExitStack() as es:
        def sb(name, shape, dt=F32):
            return es.enter_context(nc.sbuf_tensor("b_" + name, shape, dt))

        def sem(name):
            return es.enter_context(nc.semaphore("b_" + name))

        raw = sb("raw", [P, 2, CT1, S])
        wm_perm = sb("wm_perm", [P, CT1, S])
        wqT = sb("wqT", [P, CT1, S])
        wmT = sb("wmT", [P, CT1, S])
        bq = sb("bq", [P, CT1])
        bm = sb("bm", [P, CT1])
        mask = sb("mask", [P, HT1, NK1])
        ones2 = sb("ones2", [P, 2 * HD1])
        x = sb("x", [P, 2, CT1, D])
        xn = sb("xn", [P, CT1, D])
        q = sb("q", [P, CT1, D])
        k1 = sb("k1", [P, 2, CT1, NK1])
        kbd = sb("kbd", [P, 2, CT1, HT1, NK1])
        v1 = sb("v1", [P, 2, NH1 // 2, 2 * HD1])
        maxes = sb("maxes", [P, 2, NH1])
        prob = sb("prob", [P, 2, WIDTH])
        probT = sb("probT", [P, 2, NH1 // 2, P])
        recip = sb("recip", [P, HALF_N])
        o = sb("o", [P, CT1, D])
        psS = es.enter_context(nc.psum_tensor("b_psS", [P, 2, WIDTH], F32))
        psT = es.enter_context(nc.psum_tensor("b_psT", [P, 2, HALF_N], F32))
        psO = es.enter_context(nc.psum_tensor("b_psO", [P, 2, HALF_N], F32))
        norm = Norm(nc, es, "b_norm", sh)

        raw_loaded, bias_loaded, bm_gated = sem("raw_loaded"), sem("bias_loaded"), sem("bm_gated")
        consts_done, perm_done = sem("consts_done"), sem("perm_done")
        w_full, w_copied = sem("w_full"), sem("w_copied")
        x_loaded = [sem(f"x_loaded{u}") for u in range(2)]
        kv_loaded = [sem(f"kv_loaded{u}") for u in range(2)]
        x_stored = [sem(f"x_stored{u}") for u in range(2)]
        biased, kbd_ready = sem("biased"), sem("kbd_ready")
        psT_full = [sem(f"psT_full{p}") for p in range(2)]
        psT_copied = [sem(f"psT_copied{p}") for p in range(2)]
        psO_full = [sem(f"psO_full{p}") for p in range(2)]
        psO_copied = [sem(f"psO_copied{p}") for p in range(2)]
        scores_full, max_ready, shifted, exp_done = sem("scores_full"), sem("max_ready"), sem("shifted"), sem("exp_done")
        recip_ready = sem("recip_ready")

        block = es.enter_context(nc.Block())

        @block.sync
        def _(sp):
            for m, name in enumerate(("Wq1", "Wm1")):
                sp.dma_start(raw[:, m, :, :], c[name].rearrange("(t p) d -> p t d", p=P)).then_inc(raw_loaded, 16)
            for h in range(HT1):
                sp.dma_start(bq[h * HD1:(h + 1) * HD1, :], c["bq1"].rearrange("(c t h) -> h c t", c=HD1, t=CT1)[h],
                             allow_slow_non_contiguous=True).then_inc(bias_loaded, 16)
            sp.dma_start(bm[:, :], c["bm1"].rearrange("(t p) -> p t", p=P), allow_slow_non_contiguous=True
                         ).then_inc(bias_loaded, 16)

            def load_batch(b, u):
                sp.dma_start(x[:, u, :, :], scratch["x2"][bass.ds(b, 1)].rearrange("b (t p) d -> p (b t) d", p=P)
                             ).then_inc(x_loaded[u], 16)
                sp.dma_start(k1[:, u].rearrange("p a n -> p (a n)"),
                             scratch["k1"][bass.ds(b, 1)].rearrange("b p n -> p (b n)")).then_inc(kv_loaded[u], 16)
                sp.dma_start(v1[:, u].rearrange("p a n -> p (a n)"),
                             scratch["v1"][bass.ds(b, 1)].rearrange("b p n -> p (b n)")).then_inc(kv_loaded[u], 16)

            def store_batch(i, u):
                for p in range(2):
                    sp.wait_ge(psO_copied[p], O_USES * (2 * i + u + 1) + 1)
                sp.dma_start(scratch["x3"][bass.ds(2 * i + u, 1)].rearrange("b (t p) d -> p (b t) d", p=P),
                             x[:, u, :, :]).then_inc(x_stored[u], 16)

            for u in range(2):
                load_batch(u, u)
            with sp.Fori(1, PAIRS) as i:
                for u in range(2):
                    store_batch(i - 1, u)
                    sp.wait_ge(x_stored[u], 16 * i)
                    load_batch(2 * i + u, u)
            for u in range(2):
                store_batch(PAIRS - 1, u)
                sp.wait_ge(x_stored[u], 16 * PAIRS)

        @block.gpsimd
        def _(pool):
            nc.gpsimd.memset(mask[:, :, :], HD1 ** -0.5).then_inc(consts_done, 1)
            pool.wait_ge(consts_done, 1)
            nc.gpsimd.affine_select(out=mask[:, :, :], in_=mask[:, :, :], compare_op=ALU.is_ge, fill=0.0, base=0,
                                    pattern=[[-HD1, HT1], [0, NK1]], channel_multiplier=1).then_inc(consts_done, 1)
            pool.wait_ge(consts_done, 2)
            nc.gpsimd.affine_select(out=mask[:, :, :], in_=mask[:, :, :], compare_op=ALU.is_ge, fill=0.0, base=HD1 - 1,
                                    pattern=[[HD1, HT1], [0, NK1]], channel_multiplier=-1).then_inc(consts_done, 1)
            nc.gpsimd.memset(ones2[:, :], 0.0).then_inc(consts_done, 1)
            pool.wait_ge(consts_done, 4)
            for e in range(2):
                nc.gpsimd.memset(ones2[e * NK1:(e + 1) * NK1, e * HD1:(e + 1) * HD1], 1.0).then_inc(consts_done, 1)
                pool.wait_ge(consts_done, 5 + e)
            norm.rstd_of(pool, 0, rms=False)
            pool.wait_ge(bm_gated, 1)

            def body(i, final):
                for u in range(2):
                    b = 2 * i + u
                    pool.wait_ge(norm.normed, b + 1)
                    hold(pool, sh)
                    for t in range(CT1):
                        nc.gpsimd.tensor_scalar(x[:, u, t, :], x[:, u, t, :], bm[:, t:t + 1], None, ALU.add
                                                ).then_inc(biased, 1)
                    if not (final and u == 1):
                        norm.rstd_of(pool, b + 1, rms=False)

            with pool.Fori(0, PAIRS - 1) as i:
                body(i, False)
            body(PAIRS - 1, True)

        @block.tensor
        def _(pe):
            for m in range(2):
                if m == 0:
                    pe.wait_ge(raw_loaded, 32)
                else:
                    pe.wait_ge(perm_done, 1)
                src = (raw[:, 0], wm_perm)[m]
                for t in range(CT1):
                    for ot in range(CT1):
                        last = nc.tensor.transpose(psT[:, m, t * S + ot * P:t * S + (ot + 1) * P],
                                                   src[:, ot, t * P:(t + 1) * P], ident[:, :])
                last.then_inc(w_full, 1)
            pe.wait_ge(w_copied, 2)
            pe.wait_ge(consts_done, 6)

            with pe.Fori(0, PAIRS) as i:
                for u in range(2):
                    b = 2 * i + u
                    pe.wait_ge(norm.normed, b + 1)
                    for m in range(NQ):
                        t, h = m // 2, m % 2
                        pe.wait_ge(psO_copied[h], O_USES * b + t + 1)
                        for dt in range(CT1):
                            last = nc.tensor.matmul(psO[:, h, :], wqT[:, dt, t * P:(t + 1) * P],
                                                    xn[:, dt, h * HALF_N:(h + 1) * HALF_N],
                                                    start=(dt == 0), stop=(dt == CT1 - 1))
                        last.then_inc(psO_full[h], 1)
                    pe.wait_ge(kbd_ready, b + 1)
                    for h in range(2):
                        pe.wait_ge(psO_copied[h], O_USES * b + CT1 + 1)

                    def scores(n):
                        for t in range(CT1):
                            last = nc.tensor.matmul(psS[:, n % 2, t * HALF_N:(t + 1) * HALF_N],
                                                    q[:, t, n * P:(n + 1) * P],
                                                    kbd[:, u, t, :, :].rearrange("p h k -> p (h k)"), start=True, stop=True)
                        last.then_inc(scores_full, 1)

                    def transposes(n):
                        pe.wait_ge(exp_done, NT * b + n + 1)
                        for t in range(CT1):
                            pe.wait_ge(psT_copied[t], T_USES * b + n + 1)
                            for j in range(4):
                                last = nc.tensor.transpose(psT[:, t, j * P:(j + 1) * P],
                                                           prob[:, n % 2, (4 * t + j) * P:(4 * t + j + 1) * P], ident[:, :])
                            last.then_inc(psT_full[t], 1)

                    def values(n):
                        for t in range(CT1):
                            pe.wait_ge(psT_copied[t], T_USES * b + n + 2)
                            if n % 2 == 0:
                                pe.wait_ge(psO_copied[t], O_USES * b + CT1 + n // 2 + 1)
                        for t in range(CT1):
                            cols = slice(t * S + (n % 2) * P, t * S + (n % 2) * P + P)
                            for j in range(4):
                                rows = slice(j * 2 * HD1, (j + 1) * 2 * HD1)
                                nc.tensor.matmul(psO[rows, 0, cols], v1[:, u, 4 * t + j, :], probT[:, n % 2, 4 * t + j, :],
                                                 start=True, stop=True)
                                last = nc.tensor.matmul(psO[rows, 1, cols], ones2[:, :], probT[:, n % 2, 4 * t + j, :],
                                                        start=True, stop=True)
                        if n % 2:
                            last.then_inc(psO_full[1], 1)

                    scores(0)
                    scores(1)
                    for n in range(NT):
                        transposes(n)
                        if n + 2 < NT:
                            scores(n + 2)
                        if n:
                            values(n - 1)
                    values(NT - 1)
                    for p in range(2):
                        pe.wait_ge(psO_copied[p], O_USES * b + CT1 + NT // 2 + 1)
                    for m in range(NQ):
                        t, h = m // 2, m % 2
                        if t:
                            pe.wait_ge(psO_copied[h], O_USES * b + CT1 + NT // 2 + t + 1)
                        for dt in range(CT1):
                            last = nc.tensor.matmul(psO[:, h, :], wmT[:, dt, t * P:(t + 1) * P],
                                                    o[:, dt, h * HALF_N:(h + 1) * HALF_N],
                                                    start=(dt == 0), stop=(dt == CT1 - 1))
                        last.then_inc(psO_full[h], 1)

        FULL0, FULL1 = 2 * CT1, 2 * CT1 + NT // 2

        @block.vector
        def _(dve):
            for p in range(2):
                dve.sem_inc(psO_copied[p], 1)
                dve.sem_inc(psT_copied[p], 1)
            dve.wait_ge(raw_loaded, 32)
            nc.vector.tensor_copy(wm_perm[:, :, :].rearrange("p t (h c) -> p t h c", h=NH1),
                                  raw[:, 1, :, :].rearrange("p t (c h) -> p t h c", h=NH1)).then_inc(perm_done, 1)
            dve.wait_ge(w_full, 1)
            nc.vector.tensor_copy(wqT[:, :, :].rearrange("p t (h c) -> p t h c", h=NH1),
                                  psT[:, 0, :].rearrange("p (t c h) -> p t h c", t=CT1, h=NH1)).then_inc(w_copied, 1)
            dve.wait_ge(w_full, 2)
            nc.vector.tensor_copy(wmT[:, :, :].rearrange("p t d -> p (t d)"), psT[:, 1, :]).then_inc(w_copied, 1)
            dve.wait_ge(bias_loaded, 16 * (HT1 + 1))
            nc.vector.tensor_scalar(bm[:, :], bm[:, :], sh.gates[:, 1:2], None, ALU.mult).then_inc(bm_gated, 1)
            dve.wait_ge(consts_done, 3)

            def moments(b, i, u):
                dve.wait_ge(x_loaded[u], 16 * i + 16)
                norm.moments_of(dve, b, x[:, u])

            moments(0, 0, 0)
            norm.normalise(dve, 0, x[:, 0], xn, norm.STEPS)

            def body(i, final):
                for u in range(2):
                    b = 2 * i + u
                    dve.wait_ge(kv_loaded[u], 32 * i + 32)
                    for t in range(CT1):
                        last = nc.vector.tensor_tensor(kbd[:, u, t, :, :], mask[:, :, :],
                                                       k1[:, u, t:t + 1, :].broadcast_to([P, HT1, NK1]), ALU.mult)
                    last.then_inc(kbd_ready, 1)
                    for t in range(CT1):
                        dve.wait_ge(psO_full[0], FULL0 * b + t + 1)
                        nc.vector.tensor_scalar(q[:, t, 0:HALF_N], psO[:, 0, :], bq[:, t:t + 1], None, ALU.add
                                                ).then_inc(psO_copied[0], 1)

                    def shift(n):
                        dve.wait_ge(scores_full, NT * b + n + 1)
                        s = psS[:, n % 2, :].rearrange("p (h k) -> p h k", h=NH1)
                        nc.vector.tensor_reduce(maxes[:, n % 2, :], s, AX_X, ALU.max).then_inc(max_ready, 1)
                        dve.wait_ge(max_ready, NT * b + n + 1)
                        if n >= 2:
                            dve.wait_ge(psT_full[1], T_USES * b + n - 1)
                        nc.vector.tensor_tensor(prob[:, n % 2, :].rearrange("p (h k) -> p h k", h=NH1), s,
                                                maxes[:, n % 2, :].unsqueeze(2).broadcast_to([P, NH1, NK1]),
                                                ALU.subtract).then_inc(shifted, 1)

                    def normalise_o(pair):
                        dve.wait_ge(psO_full[1], FULL1 * b + CT1 + pair + 1)
                        nc.vector.reciprocal(recip[:, :], psO[:, 1, :]).then_inc(recip_ready, 1)
                        dve.wait_ge(recip_ready, (NT // 2) * b + pair + 1)
                        nc.vector.tensor_tensor(o[:, :, pair * S:(pair + 1) * S],
                                                psO[:, 0, :].rearrange("p (t n) -> p t n", t=CT1),
                                                recip[:, :].rearrange("p (t n) -> p t n", t=CT1), ALU.mult
                                                ).then_inc(psO_copied[0], 1)
                        dve.wait_ge(psO_copied[0], O_USES * b + CT1 + pair + 2)
                        dve.sem_inc(psO_copied[1], 1)

                    shift(0)
                    shift(1)
                    for n in range(NT):
                        if n + 2 < NT:
                            shift(n + 2)
                        if n % 2 == 0 and n:
                            normalise_o(n // 2 - 1)
                        if n in (1, 3) and not (final and u == 1):
                            if n == 1:
                                moments(b + 1, i + u, 1 - u)
                            else:
                                norm.normalise(dve, b + 1, x[:, 1 - u], xn, norm.STEPS)
                    normalise_o(NT // 2 - 1)
                    dve.wait_ge(biased, 2 * b + 2)
                    for m in range(NQ):
                        t, h = m // 2, m % 2
                        dve.wait_ge(psO_full[h], (FULL0, FULL1)[h] * b + (CT1, CT1 + NT // 2)[h] + t + 1)
                        cols = slice(h * HALF_N, (h + 1) * HALF_N)
                        nc.vector.scalar_tensor_tensor(x[:, u, t, cols], psO[:, h, :], sh.gates[:, 1:2], x[:, u, t, cols],
                                                       op0=ALU.mult, op1=ALU.add).then_inc(psO_copied[h], 1)

            with dve.Fori(0, PAIRS - 1) as i:
                body(i, False)
            body(PAIRS - 1, True)

        @block.scalar
        def _(act):
            act.wait_ge(bias_loaded, 16 * (HT1 + 1))
            with act.Fori(0, PAIRS) as i:
                for u in range(2):
                    b = 2 * i + u
                    for t in range(CT1):
                        act.wait_ge(psO_full[1], FULL1 * b + t + 1)
                        nc.scalar.activation(q[:, t, HALF_N:D], psO[:, 1, :], ACT.Identity, bias=bq[:, t:t + 1]
                                             ).then_inc(psO_copied[1], 1)

                    def exponential(n):
                        act.wait_ge(shifted, NT * b + n + 1)
                        nc.scalar.activation(prob[:, n % 2, :], prob[:, n % 2, :], ACT.Exp).then_inc(exp_done, 1)

                    exponential(0)
                    exponential(1)
                    for n in range(NT):
                        for t in range(CT1):
                            act.wait_ge(psT_full[t], T_USES * b + n + 1)
                            nc.scalar.copy(probT[:, n % 2, 4 * t:4 * t + 4, :],
                                           psT[:, t, :].rearrange("p (j q) -> p j q", j=4)).then_inc(psT_copied[t], 1)
                        if n + 2 < NT:
                            exponential(n + 2)


def ffn1_stage(nc, sh, c, scratch, out):
    EXPONENT_BITS = 0x7F800000
    SMALLEST_NORMAL = 2.0 ** -6
    MAGIC = 1.5 * 2.0 ** 20
    CHUNK = TT * D
    WCHUNKS = KT * D // CHUNK
    QSTEPS = 4
    with ExitStack() as es:
        def sb(name, shape, dt=F32):
            return es.enter_context(nc.sbuf_tensor("q_" + name, shape, dt))

        def sem(name):
            return es.enter_context(nc.semaphore("q_" + name))

        ident16 = sb("ident16", [P, P], BF16)
        w = sb("w", [P, KT, D])
        wq = sb("wq", [P, KT, D], BF16)
        x = sb("x", [P, 2, TT, D])
        xn = sb("xn", [P, B, TT, D])
        row_max = sb("row_max", [P, B, TT])
        part_max = sb("part_max", [P, 2])
        all_max = sb("all_max", [P, 2])
        scale = sb("scale", [P, 2])
        inverse = sb("inverse", [P, 2])
        out_scale = sb("out_scale", [P, 1])
        scaled = sb("scaled", [P, CHUNK])
        magic = sb("magic", [P, CHUNK])
        xq = sb("xq", [P, 2, TT, D], BF16)
        xqT = sb("xqT", [P, 2, KT, S], BF16)
        y = sb("y", [P, 2, TT, D])
        psT = es.enter_context(nc.psum_tensor("q_psT", [P, 2, 2 * HALF_N], BF16))
        psY = es.enter_context(nc.psum_tensor("q_psY", [P, 4, HALF_N], F32))
        norm = Norm(nc, es, "q_norm", sh)

        w_loaded, ident_ready = sem("w_loaded"), sem("ident_ready")
        x_loaded = [sem(f"x_loaded{u}") for u in range(2)]
        again_loaded = [sem(f"again_loaded{u}") for u in range(2)]
        max_done, part_done, all_done, scale_steps = sem("max_done"), sem("part_done"), sem("all_done"), sem("scale_steps")
        quant_steps = sem("quant_steps")
        quantised, psT_full, xqT_ready = sem("quantised"), sem("psT_full"), sem("xqT_ready")
        psY_full, y_ready = sem("psY_full"), sem("y_ready")
        y_stored = [sem(f"y_stored{u}") for u in range(2)]

        block = es.enter_context(nc.Block())

        @block.sync
        def _(sp):
            def load(b, u, loaded):
                sp.dma_start(x[:, u, :, :], scratch["x3"][bass.ds(b, 1)].rearrange("b (t p) d -> p (b t) d", p=P)
                             ).then_inc(loaded[u], 16)

            for u in range(2):
                load(u, u, x_loaded)
            sp.dma_start(w[:, :, :], c["weight"].rearrange("(t p) n -> p t n", p=P)).then_inc(w_loaded, 16)
            with sp.Fori(1, PAIRS) as i:
                for u in range(2):
                    sp.wait_ge(norm.normed, 2 * i + u - 1)
                    load(2 * i + u, u, x_loaded)
            for u in range(2):
                sp.wait_ge(norm.normed, B - 1 + u)
                load(u, u, again_loaded)

            def store(i, u):
                sp.wait_ge(y_ready, 8 * i + 4 * u + 4)
                sp.dma_start(out[bass.ds(2 * i + u, 1)].rearrange("b (t p) d -> p (b t) d", p=P), y[:, u, :, :]
                             ).then_inc(y_stored[u], 16)

            with sp.Fori(0, PAIRS - 1) as i:
                for u in range(2):
                    store(i, u)
                    load(2 * i + 2 + u, u, again_loaded)
            for u in range(2):
                store(PAIRS - 1, u)
            for u in range(2):
                sp.wait_ge(y_stored[u], 16 * PAIRS)

        @block.gpsimd
        def _(pool):
            nc.gpsimd.tensor_copy(ident16[:, :], sh.ident[:, :]).then_inc(ident_ready, 1)
            pool.wait_ge(part_done, 1)
            nc.gpsimd.partition_all_reduce(all_max[:, 1:2], part_max[:, 1:2], P, ABSMAX).then_inc(all_done, 1)
            with pool.Fori(0, B) as b:
                norm.rstd_of(pool, b, rms=False)
            pool.wait_ge(part_done, 2)
            nc.gpsimd.partition_all_reduce(all_max[:, 0:1], part_max[:, 0:1], P, ABSMAX).then_inc(all_done, 1)

        @block.tensor
        def _(pe):
            pe.wait_ge(ident_ready, 1)

            def batch(b, u, first):
                pe.wait_ge(quantised, WCHUNKS + b + 1)
                for n in range(2):
                    if not first:
                        pe.wait_ge(xqT_ready, 2 * b + n - 1)
                    for q in range(4):
                        for t in range(TT):
                            kt = 4 * n + q
                            last = nc.tensor.transpose(psT[:, n, (q * TT + t) * P:(q * TT + t + 1) * P],
                                                       xq[:, u, t, kt * P:(kt + 1) * P], ident16[:, :])
                    last.then_inc(psT_full, 1)
                pe.wait_ge(xqT_ready, 2 * b + 2)
                for t in range(TT):
                    for h in range(2):
                        if not first:
                            pe.wait_ge(y_ready, 4 * b + 2 * t + h - 3)
                        for kt in range(KT):
                            last = nc.tensor.matmul(psY[:, 2 * t + h, :], xqT[:, u, kt, t * P:(t + 1) * P],
                                                    wq[:, kt, h * HALF_N:(h + 1) * HALF_N],
                                                    start=(kt == 0), stop=(kt == KT - 1))
                        last.then_inc(psY_full, 1)

            batch(0, 0, True)
            batch(1, 1, False)
            with pe.Fori(1, PAIRS) as i:
                for u in range(2):
                    batch(2 * i + u, u, False)

        @block.vector
        def _(dve):
            def link(instruction, semaphore, value):
                instruction.then_inc(semaphore, 1)
                dve.wait_ge(semaphore, value)

            def scale_of(m, done):
                dve.wait_ge(all_done, done)
                at = 3 * (done - 1)
                link(nc.vector.tensor_scalar(all_max[:, m:m + 1], all_max[:, m:m + 1], 1e-12, None, ALU.max),
                     scale_steps, at + 1)
                link(nc.vector.reciprocal(scale[:, m:m + 1], all_max[:, m:m + 1]), scale_steps, at + 2)
                link(nc.vector.tensor_scalar(scale[:, m:m + 1], scale[:, m:m + 1], FP8_MAX, None, ALU.mult),
                     scale_steps, at + 3)
                nc.vector.reciprocal(inverse[:, m:m + 1], scale[:, m:m + 1])

            def quantise(n, src, m, dst):
                if not (isinstance(n, int) and n == 0):
                    dve.wait_ge(quantised, n)
                link(nc.vector.tensor_scalar(scaled[:, :], src, scale[:, m:m + 1], FP8_MAX, ALU.mult, ALU.min),
                     quant_steps, QSTEPS * n + 1)
                link(nc.vector.tensor_scalar(magic[:, :].bitcast(U32), scaled[:, :].bitcast(U32), EXPONENT_BITS, None,
                                             ALU.bitwise_and), quant_steps, QSTEPS * n + 2)
                link(nc.vector.tensor_scalar(magic[:, :], magic[:, :], SMALLEST_NORMAL, MAGIC, ALU.max, ALU.mult),
                     quant_steps, QSTEPS * n + 3)
                link(nc.vector.scalar_tensor_tensor(scaled[:, :], scaled[:, :], -FP8_MAX, magic[:, :],
                                                    op0=ALU.max, op1=ALU.add), quant_steps, QSTEPS * n + 4)
                nc.vector.tensor_tensor(dst, scaled[:, :], magic[:, :], ALU.subtract).then_inc(quantised, 1)

            dve.wait_ge(w_loaded, 16)
            nc.vector.tensor_reduce(part_max[:, 1:2], w[:, :, :].rearrange("p t n -> p (t n)"), AX_X, ALU.max,
                                    apply_absolute_value=True).then_inc(part_done, 1)
            scale_of(1, 1)
            for n in range(WCHUNKS):
                rows = slice(n * KT // WCHUNKS, (n + 1) * KT // WCHUNKS)
                quantise(n, w[:, rows, :].rearrange("p t n -> p (t n)"), 1, wq[:, rows, :].rearrange("p t n -> p (t n)"))

            with dve.Fori(0, PAIRS) as i:
                for u in range(2):
                    b = 2 * i + u
                    dve.wait_ge(x_loaded[u], 16 * i + 16)
                    norm.moments_of(dve, b, x[:, u])
                    mine = xn[:, bass.ds(b, 1)].rearrange("p b t d -> p (b t) d")
                    norm.normalise(dve, b, x[:, u], mine, norm.STEPS)
                    dve.wait_ge(norm.normed, b + 1)
                    nc.vector.tensor_reduce(row_max[:, bass.ds(b, 1), :].rearrange("p b t -> p (b t)"), mine, AX_X, ALU.max,
                                            apply_absolute_value=True).then_inc(max_done, 1)
            dve.wait_ge(max_done, B)
            nc.vector.tensor_reduce(part_max[:, 0:1], row_max[:, :, :].rearrange("p b t -> p (b t)"), AX_X, ALU.max
                                    ).then_inc(part_done, 1)
            scale_of(0, 2)
            dve.drain()
            link(nc.vector.tensor_tensor(out_scale[:, :], inverse[:, 0:1], inverse[:, 1:2], ALU.mult), scale_steps, 7)
            link(nc.vector.tensor_tensor(out_scale[:, :], out_scale[:, :], sh.gates[:, 3:4], ALU.mult), scale_steps, 8)

            def quantise_batch(b, u):
                quantise(WCHUNKS + b, xn[:, bass.ds(b, 1)].rearrange("p b t d -> p (b t d)"), 0,
                         xq[:, u, :, :].rearrange("p t d -> p (t d)"))

            def add_residual(b, i, u, first):
                dve.wait_ge(again_loaded[u], 16 * i + 16)
                if not first:
                    dve.wait_ge(y_stored[u], 16 * i)
                for t in range(TT):
                    for h in range(2):
                        dve.wait_ge(psY_full, 4 * b + 2 * t + h + 1)
                        cols = slice(h * HALF_N, (h + 1) * HALF_N)
                        nc.vector.scalar_tensor_tensor(y[:, u, t, cols], psY[:, 2 * t + h, :], out_scale[:, 0:1],
                                                       x[:, u, t, cols], op0=ALU.mult, op1=ALU.add).then_inc(y_ready, 1)

            quantise_batch(0, 0)
            quantise_batch(1, 1)
            add_residual(0, 0, 0, True)
            quantise_batch(2, 0)
            add_residual(1, 0, 1, True)
            quantise_batch(3, 1)
            with dve.Fori(1, PAIRS - 1) as i:
                for u in range(2):
                    add_residual(2 * i + u, i, u, False)
                    quantise_batch(2 * i + u + 2, u)
            for u in range(2):
                add_residual(B - 2 + u, PAIRS - 1, u, False)

        @block.scalar
        def _(act):
            with act.Fori(0, PAIRS) as i:
                for u in range(2):
                    b = 2 * i + u
                    for n in range(2):
                        act.wait_ge(psT_full, 2 * b + n + 1)
                        nc.scalar.copy(xqT[:, u, 4 * n:4 * n + 4, :].rearrange("p k n -> p (k n)"), psT[:, n, :]
                                       ).then_inc(xqT_ready, 1)


_NAMES = {"wk": "L0_xattn_wk", "wv": "L0_xattn_wv", "wq": "L0_xattn_wq", "wo": "L0_xattn_wo", "ln_w": "L0_xattn_ln_w",
          "x": "x", "ctx": "ctx_4096", "W_base": "L0_ffn_W_base", "b_base": "L0_ffn_b_base", "enc0": "L0_ffn_enc0",
          "enc1": "L0_ffn_enc1", "coefs0": "L0_ffn_coefs0", "coefs1": "L0_ffn_coefs1", "mask0": "L0_ffn_mask0",
          "mask1": "L0_ffn_mask1", "Wq1": "L1_xattn_Wq", "bq1": "L1_xattn_bq", "Wk1": "L1_xattn_Wk", "bk1": "L1_xattn_bk",
          "Wv1": "L1_xattn_Wv", "bv1": "L1_xattn_bv", "proj_k": "L1_xattn_proj_k", "proj_v": "L1_xattn_proj_v",
          "Wm1": "L1_xattn_Wm", "bm1": "L1_xattn_bm", "weight": "L1_ffn_weight", "g_xattn": "g_xattn", "g_ffn": "g_ffn"}


def build(nc, a, out):
    scratch = {}
    for name in ("k0_hi", "k0_lo"):
        scratch[name] = nc.dram_tensor("scratch_" + name, [B, KV0, S], F32).ap()
    scratch["o"] = nc.dram_tensor("scratch_o", [B, D, S], F32).ap()
    for name, width in (("v0", TT * KV0), ("k1", CT1 * NK1), ("v1", S)):
        scratch[name] = nc.dram_tensor("scratch_" + name, [B, P, width], F32).ap()
    for name in ("x1", "x2", "x3"):
        scratch[name] = nc.dram_tensor("scratch_" + name, [B, S, D], F32).ap()
    with ExitStack() as es:
        sh = setup_stage(nc, es, a["g_xattn"], a["g_ffn"])
        context_stage(nc, sh, a, scratch)
        attn0_stage(nc, sh, a, scratch)
        proj0_stage(nc, sh, a, scratch)
        ffn0_stage(nc, sh, a, scratch)
        attn1_stage(nc, sh, a, scratch)
        ffn1_stage(nc, sh, a, scratch, out)


def inverse_rfft_table():
    o = np.arange(D)
    table = np.empty((D, D), np.float64)
    table[0] = D ** -0.5
    table[D - 1] = np.where(o % 2 == 0, 1.0, -1.0) * D ** -0.5
    k = np.arange(1, D // 2)[:, None]
    angle = 2.0 * np.pi * ((k * o) % D) / D
    table[1:D - 1:2] = (2.0 / D) ** 0.5 * np.cos(angle)
    table[2:D:2][:D // 2 - 1] = (2.0 / D) ** 0.5 * np.sin(angle)
    return table.astype(np.float32)


def kernel(**inputs):
    import concourse.bacc as bacc
    from concourse.bass_utils import run_bass_kernel_spmd

    nc = bacc.Bacc("TRN2", target_bir_lowering=False, num_devices=1)
    arrays, args = {}, {}
    for short, name in _NAMES.items():
        array = np.ascontiguousarray(inputs[name])
        arrays["in_" + short] = array
        args[short] = nc.dram_tensor("in_" + short, array.shape, mybir.dt.from_np(array.dtype), kind="ExternalInput").ap()
    arrays["irfft"] = inverse_rfft_table()
    args["irfft"] = nc.dram_tensor("irfft", (D, D), F32, kind="ExternalInput").ap()
    out = nc.dram_tensor("out", (B, S, D), F32, kind="ExternalOutput").ap()
    build(nc, args, out)
    return run_bass_kernel_spmd(nc, [arrays], core_ids=[0]).results[0]["out"]
```

```python
from contextlib import ExitStack

import numpy as np
import concourse.bass as bass
from concourse import mybir

F32 = mybir.dt.float32
F32R = mybir.dt.float32r
BF16 = mybir.dt.bfloat16
U8 = mybir.dt.uint8
U32 = mybir.dt.uint32
ALU = mybir.AluOpType
ACT = mybir.ActivationFunctionType
AX_X = mybir.AxisListType.X
ABSMAX = bass.bass_isa.ReduceOp.absmax

P = 128
B, S, D = 8, 256, 1024
TT = S // P
KT = D // P
PAIRS = B // 2
HD0, NH0, NKV0 = 32, 32, 8
KV0 = NKV0 * HD0
HALF0 = KV0 // P
REP0 = NH0 // NKV0
JH0 = P // HD0
HD1, NH1, NK1 = 16, 16, 64
HT1 = P // HD1
CT1 = S // P
R0, R1, NE = 32, 8, 3
RR = R0 + R1
LN_EPS = 1e-5
FP8_MAX = 448.0
HALF_N = 512


def batch_of(stream, b):
    return stream[:, bass.ds(b, 1)].rearrange("p b t d -> p (b t) d")


def identity(nc, ident, done):
    nc.gpsimd.memset(ident[:, :], 0.0).then_inc(done, 1)
    nc.gpsimd.wait_ge(done, 1)
    nc.gpsimd.affine_select(out=ident[:, :], in_=ident[:, :], compare_op=ALU.not_equal, fill=1.0, base=0,
                            pattern=[[-1, P]], channel_multiplier=1).then_inc(done, 1)


def hold(engine, sh):
    engine.sem_inc(sh.held, 1)


FP8_SHIFT = 2.0 ** 20
FP8_LEAST_MAGIC = 1.5 * FP8_SHIFT * 2.0 ** -6
EXPONENT_BITS, HALF_BIT = 0x7F800000, 0x00400000


class Quant:

    def __init__(self, nc, es):
        def sb(name, shape, dt=F32):
            return es.enter_context(nc.sbuf_tensor("z_" + name, shape, dt))
        self.w_max = sb("w_max", [P, KT])
        self.part_max = sb("part_max", [P, 2])
        self.all_max = sb("all_max", [P, 2])
        self.scale = sb("scale", [P, 2])
        self.inverse = sb("inverse", [P, 2])
        self.row_max = sb("row_max", [P, B, TT])
        self.mean = sb("mean", [P, B, TT])
        self.rstd = sb("rstd", [P, B, TT])
        self.steps = es.enter_context(nc.semaphore("z_steps"))
        self.all_done = es.enter_context(nc.semaphore("z_all_done"))
        self.part_done = es.enter_context(nc.semaphore("z_part_done"))
        self.w_shift = sb("w_shift", [P, 1])
        self.sb = sb

    def scale_of(self, nc, dve, m, done):
        dve.wait_ge(self.all_done, done)
        at = 3 * (done - 1)
        nc.vector.tensor_scalar(self.all_max[:, m:m + 1], self.all_max[:, m:m + 1], 1e-12, None, ALU.max
                                ).then_inc(self.steps, 1)
        dve.wait_ge(self.steps, at + 1)
        nc.vector.reciprocal(self.scale[:, m:m + 1], self.all_max[:, m:m + 1]).then_inc(self.steps, 1)
        dve.wait_ge(self.steps, at + 2)
        nc.vector.tensor_scalar(self.scale[:, m:m + 1], self.scale[:, m:m + 1], FP8_MAX, None, ALU.mult
                                ).then_inc(self.steps, 1)
        dve.wait_ge(self.steps, at + 3)
        return nc.vector.reciprocal(self.inverse[:, m:m + 1], self.scale[:, m:m + 1])


def fp8_magic(nc, magic, shifted):
    return nc.vector.tensor_scalar(magic.bitcast(U32), shifted.bitcast(U32), EXPONENT_BITS, HALF_BIT,
                                   ALU.bitwise_and, ALU.bitwise_or)


def fp8_add_magic(nc, total, magic, scaled):
    return nc.vector.scalar_tensor_tensor(total, magic, FP8_LEAST_MAGIC, scaled, op0=ALU.max, op1=ALU.add)


def fp8_minus_rounded(nc, rounded, magic, total):
    return nc.vector.scalar_tensor_tensor(rounded, magic, FP8_LEAST_MAGIC, total, op0=ALU.max, op1=ALU.subtract)


def fp8_clip(nc, rounded):
    return nc.vector.tensor_scalar(rounded, rounded, FP8_MAX, -FP8_MAX, ALU.min, ALU.max)


def free_semaphores(nc, sems):
    nc.clear_and_free_semaphores(sems)
    nc.all_engine_barrier()


class Shared:
    pass


def setup_stage(nc, ctx, g_xattn, g_ffn):
    sh = Shared()
    sh.ident = ctx.enter_context(nc.sbuf_tensor("ident", [P, P], F32))
    sh.gates = ctx.enter_context(nc.sbuf_tensor("gates", [P, 4], F32))
    sh.gate_raw = ctx.enter_context(nc.sbuf_tensor("gate_raw", [P, 4], F32))
    sh.minus_half = ctx.enter_context(nc.sbuf_tensor("minus_half", [P, 4], F32))
    sh.ident_done = ctx.enter_context(nc.semaphore("ident_done"))
    sh.held = ctx.enter_context(nc.semaphore("held"))
    sh.gates_loaded = ctx.enter_context(nc.semaphore("gates_loaded"))
    with nc.Block() as block:
        @block.sync
        def _(sp):
            sp.dma_start(sh.gate_raw[:, 0:2], g_xattn.partition_broadcast(P)).then_inc(sh.gates_loaded, 16)
            sp.dma_start(sh.gate_raw[:, 2:4], g_ffn.partition_broadcast(P)).then_inc(sh.gates_loaded, 16)

        @block.gpsimd
        def _(pool):
            identity(nc, sh.ident, sh.ident_done)
            nc.gpsimd.memset(sh.minus_half[:, :], -0.5)

        @block.scalar
        def _(act):
            act.wait_ge(sh.gates_loaded, 32)
            nc.scalar.activation(sh.gates[:, :], sh.gate_raw[:, :], ACT.Tanh)
    return sh


class SplitWeight:

    def __init__(self, nc, es, name, side=None):
        self.hi = es.enter_context(nc.sbuf_tensor(name + "_hi", [P, KT, D], F32R, side=side))
        self.lo = es.enter_context(nc.sbuf_tensor(name + "_lo", [P, KT, D], F32R, side=side))


class Rows:

    def __init__(self, nc, es):
        self.batches = es.enter_context(nc.sbuf_tensor("rows", [P, 2, TT, D], F32))
        self.blocks = [self.batches[:, u, t, :] for u in range(2) for t in range(TT)]
        self.wo_loaded = es.enter_context(nc.semaphore("rows_wo_loaded"))


def context_stage(nc, sh, c, scratch, wq, first_x, first_norm):
    ident = sh.ident
    STORES = 5
    CV = KV0 + 3 * NK1
    FILLS = KT // 2
    with ExitStack() as es:
        sems = []
        es.callback(lambda: free_semaphores(nc, sems))

        def sb(name, shape, dt=F32):
            return es.enter_context(nc.sbuf_tensor("c_" + name, shape, dt))

        def sem(name):
            sems.append(nc.alloc_semaphore("c_" + name))
            return sems[-1]

        raw = sb("raw", [P, 2, D])
        raw1 = sb("raw1", [P, 2, 2, S])
        projs = sb("projs", [P, KT, 2 * NK1])
        wk_hi = sb("wk_hi", [P, KT, KV0], F32R)
        wk_lo = sb("wk_lo", [P, KT, KV0], F32R)
        wvp_hi = sb("wvp_hi", [P, KT, CV], F32R)
        wvp_lo = sb("wvp_lo", [P, KT, CV], F32R)
        w1T = sb("w1T", [P, 2, TT, S])
        rows1 = sb("rows1", [1, 2, S])
        rows1h = sb("rows1h", [1, 2, S])
        ones = sb("ones", [P, 1])
        colsum = sb("colsum", [1, 2 * NK1])
        colsum_v = sb("colsum_v", [1, 2 * NK1])
        bias_k = sb("bias_k", [P, CT1, NK1])
        bias_v = sb("bias_v", [P, S])
        nat = sb("nat", [P, 2, TT, D])
        cT_hi = sb("cT_hi", [P, KT, S], F32R)
        cT_lo = sb("cT_lo", [P, KT, S], F32R)
        k0_hi = sb("k0_hi", [P, 2, HALF0, S], F32R)
        k0_lo = sb("k0_lo", [P, 2, HALF0, S], F32R)
        v0 = sb("v0", [P, 2, TT, KV0])
        mid = sb("mid", [P, 2, TT, 3 * NK1])
        k1 = sb("k1", [P, 2, CT1, NK1])
        v1 = sb("v1", [P, 2, NH1 // 2, 2 * HD1])
        ln_w = sb("ln_w", [P, D])
        psT = es.enter_context(nc.psum_tensor("c_psT", [P, 2, HALF_N], F32))
        psW = es.enter_context(nc.psum_tensor("c_psW", [P, HALF_N], F32))
        psP = es.enter_context(nc.psum_tensor("c_psP", [P, 4, HALF_N], F32))
        psL = es.enter_context(nc.psum_tensor("c_psL", [P, HALF_N], F32))

        raw_loaded = [sem(f"raw_loaded{n}") for n in range(2 * HALF0)]
        raw1_loaded, small_loaded, proj_loaded = sem("raw1_loaded"), sem("small_loaded"), sem("proj_loaded")
        wT_full, wT_hi, wT_copied, w1_copied = sem("wT_full"), sem("wT_hi"), sem("wT_copied"), sem("w1_copied")
        proj_hi, proj_split = sem("proj_hi"), sem("proj_split")
        preset = sem("preset")
        colsum_full, colsum_copied = sem("colsum_full"), sem("colsum_copied")
        bias_full, bias_copied = sem("bias_full"), sem("bias_copied")
        nat_loaded = [sem(f"nat_loaded{u}") for u in range(2)]
        psT_full, cT_high = sem("psT_full"), sem("cT_high")
        cT_low = sem("cT_low")
        psP_full, mid_ready, k_low = sem("psP_full"), sem("mid_ready"), sem("k_low")
        psL_full = sem("psL_full")
        out_act = [sem(f"out_act{u}") for u in range(2)]
        out_dve = [sem(f"out_dve{u}") for u in range(2)]
        out_stored = [sem(f"out_stored{u}") for u in range(2)]
        lnw_loaded, wq_scaled, wq_full, wq_hi = sem("lnw_loaded"), sem("wq_scaled"), sem("wq_full"), sem("wq_hi")
        wq_lo = sem("wq_lo")
        wq_loaded = [sem(f"wq_loaded{u}") for u in range(2)]
        x_loaded = [sem(f"x_loaded{u}") for u in range(2)]

        block = es.enter_context(nc.Block())

        blocks = [(c["wk"], n) for n in range(HALF0)] + [(c["wv"], n) for n in range(HALF0)]
        FIRST = 2 * len(blocks)

        @block.sync
        def _(sp):
            def load_ctx(b, u):
                sp.dma_start(nat[:, u, :, :],
                             c["ctx"][bass.ds(b, 1)].rearrange("b (t p) d -> p (b t) d", p=P)
                             ).then_inc(nat_loaded[u], 16)

            for n, (w, rb) in enumerate(blocks):
                if n >= 2:
                    sp.wait_ge(wT_full, 2 * (n - 1))
                sp.dma_start(raw[:, n % 2, :], w[rb * P:(rb + 1) * P, :]).then_inc(raw_loaded[n], 16)
            for m, name in enumerate(("Wk1", "Wv1")):
                sp.dma_start(raw1[:, m, :, :], c[name].rearrange("(t p) d -> p t d", p=P)).then_inc(raw1_loaded, 16)
            for m, name in enumerate(("bk1", "bv1")):
                sp.dma_start(rows1[0:1, m, :], c[name].rearrange("(a d) -> a d", a=1)).then_inc(small_loaded, 16)
            for m, name in enumerate(("proj_k", "proj_v")):
                sp.dma_start(projs[:, :, m * NK1:(m + 1) * NK1],
                             c[name].rearrange("(t p) k -> p t k", p=P)).then_inc(proj_loaded, 16)

            def store(i, u):
                sp.wait_ge(out_act[u], 4 * i + 5)
                sp.wait_ge(out_dve[u], 2 * i + 3)
                for name, tile in (("k0_hi", k0_hi), ("k0_lo", k0_lo)):
                    sp.dma_start(scratch[name][bass.ds(2 * i + u, 1)].rearrange("b (a p) s -> p (b a) s", p=P),
                                 plain(tile)[:, u, :, :]).then_inc(out_stored[u], 16)
                for name, tile in (("v0", v0), ("k1", k1), ("v1", v1)):
                    sp.dma_start(scratch[name][bass.ds(2 * i + u, 1)].rearrange("b p n -> p (b n)"),
                                 tile[:, u].rearrange("p a n -> p (a n)")).then_inc(out_stored[u], 16)

            def load_wq(i, u):
                rows = c["wq"].rearrange("(h j r c) d -> h j r c d", h=HALF0, j=JH0, r=REP0)
                for j in range(JH0):
                    sp.dma_start(raw[j * HD0:(j + 1) * HD0, u, :], rows[u, j, bass.ds(i, 1)].rearrange("r c d -> c (r d)")
                                 ).then_inc(wq_loaded[u], 16)

            for u in range(2):
                sp.sem_inc(out_stored[u], 1)
                load_ctx(u, u)
            sp.dma_start(ln_w[:, :], c["ln_w"].partition_broadcast(P)).then_inc(lnw_loaded, 16)
            for u in range(2):
                sp.wait_ge(wT_full, 2 * (len(blocks) - 1 + u))
                load_wq(0, u)
            for u in range(2):
                sp.dma_start(first_x[:, u, :, :], c["x"][u].rearrange("(t p) d -> p t d", p=P)).then_inc(x_loaded[u], 16)
            with sp.Fori(1, PAIRS) as i:
                for u in range(2):
                    sp.wait_ge(psT_full, FILLS * (2 * i + u - 1))
                    load_ctx(2 * i + u, u)
                    sp.wait_ge(wq_full, 4 * i + 2 * u - 2)
                    load_wq(i, u)
                    store(i - 1, u)
            for u in range(2):
                store(PAIRS - 1, u)
            for u in range(2):
                sp.wait_ge(out_stored[u], 16 * STORES * PAIRS + 1)

        @block.gpsimd
        def _(pool):
            nc.gpsimd.memset(ones[:, :], 1.0).then_inc(preset, 1)
            nc.gpsimd.memset(v1[:, :, :, :], 0.0).then_inc(preset, 1)
            pool.wait_ge(lnw_loaded, 16)
            with pool.Fori(0, PAIRS) as i:
                for u in range(2):
                    pool.wait_ge(wq_loaded[u], 16 * JH0 * i + 16 * JH0)
                    nc.gpsimd.tensor_tensor(raw[:, u, :], raw[:, u, :], ln_w[:, :], ALU.mult).then_inc(wq_scaled, 1)
            for b in range(2):
                first_norm.rstd_of(pool, b, rms=True)

        @block.tensor
        def _(pe):
            for n in range(len(blocks)):
                pe.wait_ge(raw_loaded[n], 16)
                for half in range(2):
                    if n:
                        pe.wait_ge(wT_copied, 2 * n + half - 1)
                    for q in range(4):
                        kt = 4 * half + q
                        last = nc.tensor.transpose(psT[:, half, q * P:(q + 1) * P],
                                                   raw[:, n % 2, kt * P:(kt + 1) * P], ident[:, :])
                    last.then_inc(wT_full, 1)
            pe.wait_ge(raw1_loaded, 32)
            for m in range(2):
                pe.wait_ge(wT_copied, FIRST + m - 1)
                for t in range(TT):
                    for ot in range(TT):
                        last = nc.tensor.transpose(psT[:, m, t * S + ot * P:t * S + (ot + 1) * P],
                                                   raw1[:, m, ot, t * P:(t + 1) * P], ident[:, :])
                last.then_inc(wT_full, 1)
            pe.wait_ge(preset, 1)
            pe.wait_ge(proj_loaded, 32)
            for kt in range(KT):
                last = nc.tensor.matmul(psL[0:1, 0:2 * NK1], ones[:, 0:1], projs[:, kt, :],
                                        start=(kt == 0), stop=(kt == KT - 1))
            last.then_inc(colsum_full, 1)
            pe.wait_ge(colsum_copied, 3)
            for t in range(CT1):
                nc.tensor.matmul(psP[:, t, 0:NK1], rows1h[0:1, 0, t * P:(t + 1) * P], colsum[0:1, 0:NK1],
                                 start=True, stop=True)
            nc.tensor.matmul(psP[:, 2, 0:S], colsum_v[0:1, :], rows1h[0:1, 1, :],
                             start=True, stop=True).then_inc(bias_full, 1)
            pe.wait_ge(bias_copied, 1)
            pe.wait_ge(w1_copied, 2)
            pe.wait_ge(proj_split, 1)

            def transpose_ctx(b, i, u, fills):
                pe.wait_ge(nat_loaded[u], 16 * i + 16)
                for n in fills:
                    pe.wait_ge(cT_low, FILLS * b + n + 1)
                    for q in range(2):
                        for t in range(TT):
                            kt = 2 * n + q
                            last = nc.tensor.transpose(psT[:, n % 2, (q * TT + t) * P:(q * TT + t + 1) * P],
                                                       nat[:, u, t, kt * P:(kt + 1) * P], ident[:, :])
                    last.then_inc(psT_full, 1)

            def transpose_wq(b, u, half):
                if half == 0:
                    pe.wait_ge(wq_scaled, b + 1)
                pe.wait_ge(wq_lo, 2 * b + half + 1)
                for q in range(4):
                    kt = 4 * half + q
                    last = nc.tensor.transpose(psW[:, q * P:(q + 1) * P], raw[:, u, kt * P:(kt + 1) * P], ident[:, :])
                last.then_inc(wq_full, 1)

            def parts(kt, out, stationary, moving):
                (s_hi, s_lo), (m_hi, m_lo) = stationary, moving
                nc.tensor.matmul(out, s_hi, m_hi, start=(kt == 0), stop=False)
                nc.tensor.matmul(out, s_hi, m_lo, start=False, stop=False)
                return nc.tensor.matmul(out, s_lo, m_hi, start=False, stop=(kt == KT - 1))

            transpose_ctx(0, 0, 0, range(FILLS))

            def body(i, final):
                for u in range(2):
                    b = 2 * i + u
                    pe.wait_ge(out_act[1 - u], 4 * i + 4 * u + 1)
                    pe.wait_ge(k_low, 2 * b + 1)
                    for half in range(HALF0):
                        cols = slice(half * P, (half + 1) * P)
                        for kt in range(KT):
                            if half == 0 and kt % 2 == 0:
                                pe.wait_ge(cT_low, FILLS * b + kt // 2 + 3)
                            last = parts(kt, psP[:, half, 0:S], (wk_hi[:, kt, cols], wk_lo[:, kt, cols]),
                                         (cT_hi[:, kt, :], cT_lo[:, kt, :]))
                        last.then_inc(psP_full, 1)
                    transpose_wq(b, u, 0)
                    for t in range(TT):
                        rows = slice(t * P, (t + 1) * P)
                        for kt in range(KT):
                            last = parts(kt, psP[:, 2 + t, 0:CV], (cT_hi[:, kt, rows], cT_lo[:, kt, rows]),
                                         (wvp_hi[:, kt, :], wvp_lo[:, kt, :]))
                        last.then_inc(psP_full, 1)
                    transpose_wq(b, u, 1)
                    if not (final and u == 1):
                        transpose_ctx(b + 1, i + u, 1 - u, range(2))
                    pe.wait_ge(mid_ready, 2 * b + 2)
                    pe.wait_ge(out_dve[1 - u], 2 * i + 2 * u + 1)
                    for ct in range(CT1):
                        for t in range(TT):
                            nc.tensor.matmul(psL[:, ct * NK1:(ct + 1) * NK1], w1T[:, 0, t, ct * P:(ct + 1) * P],
                                             mid[:, u, t, 0:NK1], start=(t == 0), stop=(t == TT - 1))
                    for t in range(TT):
                        last = nc.tensor.matmul(psL[:, P:P + S], mid[:, u, t, NK1:3 * NK1], w1T[:, 1, t, :],
                                                start=(t == 0), stop=(t == TT - 1))
                    last.then_inc(psL_full, 1)
                    if not (final and u == 1):
                        transpose_ctx(b + 1, i + u, 1 - u, range(2, FILLS))

            with pe.Fori(0, PAIRS - 1) as i:
                body(i, False)
            body(PAIRS - 1, True)

        def weight_parts(n, half):
            kts, cols = slice(4 * half, 4 * half + 4), slice((n % HALF0) * P, (n % HALF0 + 1) * P)
            hi, lo = (wk_hi, wk_lo) if n < HALF0 else (wvp_hi, wvp_lo)
            return hi[:, kts, cols], lo[:, kts, cols], plain(hi)[:, kts, cols]

        @block.vector
        def _(dve):
            dve.sem_inc(cT_low, 2)
            dve.sem_inc(wq_lo, 1)
            dve.sem_inc(k_low, 1)
            for u in range(2):
                dve.sem_inc(out_dve[u], 1)
            for n in range(len(blocks)):
                for half in range(2):
                    dve.wait_ge(wT_hi, 2 * n + half + 1)
                    _, lo, hi = weight_parts(n, half)
                    nc.vector.tensor_tensor(lo, psT[:, half, :].rearrange("p (k n) -> p k n", k=4), hi, ALU.subtract
                                            ).then_inc(wT_copied, 1)
            for m in range(2):
                dve.wait_ge(wT_full, FIRST + m + 1)
                for t in range(TT):
                    last = nc.vector.tensor_copy(w1T[:, m, t, :].rearrange("p (h c) -> p h c", h=NH1),
                                                 psT[:, m, t * S:(t + 1) * S].rearrange("p (c h) -> p h c", h=NH1))
                last.then_inc(w1_copied, 1)
            dve.wait_ge(small_loaded, 32)
            nc.vector.tensor_copy(rows1h[0:1, :, :].rearrange("p m (h c) -> p m h c", h=NH1),
                                  rows1[0:1, :, :].rearrange("p m (c h) -> p m h c", h=NH1))
            dve.wait_ge(colsum_full, 1)
            nc.vector.tensor_copy(colsum[0:1, :], psL[0:1, 0:2 * NK1]).then_inc(colsum_copied, 1)
            for e in range(2):
                nc.vector.tensor_copy(colsum_v[0:1, e * NK1:(e + 1) * NK1], psL[0:1, NK1:2 * NK1]).then_inc(colsum_copied, 1)
            dve.wait_ge(proj_hi, 1)
            for m, e in enumerate((0, 1, 1)):
                cols = slice(KV0 + m * NK1, KV0 + (m + 1) * NK1)
                last = nc.vector.tensor_tensor(wvp_lo[:, :, cols], projs[:, :, e * NK1:(e + 1) * NK1],
                                               plain(wvp_hi)[:, :, cols], ALU.subtract)
            last.then_inc(proj_split, 1)
            dve.wait_ge(bias_full, 1)
            nc.vector.tensor_copy(bias_k[:, :, :], psP[:, 0:CT1, 0:NK1])
            nc.vector.tensor_copy(bias_v[:, :], psP[:, 2, 0:S]).then_inc(bias_copied, 1)
            dve.wait_ge(bias_copied, 1)
            dve.wait_ge(preset, 2)

            def low_ctx(b):
                for n in range(FILLS):
                    dve.wait_ge(cT_high, FILLS * b + n + 1)
                    cols = slice(2 * n, 2 * n + 2)
                    nc.vector.tensor_tensor(cT_lo[:, cols, :], psT[:, n % 2, :].rearrange("p (k n) -> p k n", k=2),
                                            plain(cT_hi)[:, cols, :], ALU.subtract).then_inc(cT_low, 1)

            def low_wq(b, i, u, half):
                dve.wait_ge(wq_hi, 2 * b + half + 1)
                cols = bass.ds((REP0 * u + i) * P, P)
                nc.vector.tensor_tensor(wq.lo[:, 4 * half:4 * half + 4, cols], psW[:, :].rearrange("p (k n) -> p k n", k=4),
                                        plain(wq.hi)[:, 4 * half:4 * half + 4, cols], ALU.subtract).then_inc(wq_lo, 1)

            low_ctx(0)

            def body(i, final):
                for u in range(2):
                    b = 2 * i + u
                    dve.wait_ge(out_stored[u], 16 * STORES * i + 1)
                    for half in range(HALF0):
                        dve.wait_ge(out_act[u], 4 * i + half + 2)
                        nc.vector.scalar_tensor_tensor(k0_lo[:, u, half, :], psP[:, half, 0:S], HD0 ** -0.5,
                                                       plain(k0_hi)[:, u, half, :], op0=ALU.mult, op1=ALU.subtract
                                                       ).then_inc(k_low, 1)
                    low_wq(b, i, u, 0)
                    if final:
                        dve.wait_ge(x_loaded[u], 16)
                        first_norm.moments_of(dve, u, first_x[:, u])
                    for t in range(TT):
                        dve.wait_ge(psP_full, 4 * b + 3 + t)
                        nc.vector.tensor_copy(mid[:, u, t, :], psP[:, 2 + t, KV0:CV]).then_inc(mid_ready, 1)
                    low_wq(b, i, u, 1)
                    if not (final and u == 1):
                        low_ctx(b + 1)
                    dve.wait_ge(psL_full, b + 1)
                    nc.vector.tensor_tensor(k1[:, u, :, :], psL[:, 0:P].rearrange("p (t n) -> p t n", t=CT1),
                                            bias_k[:, :, :], ALU.add).then_inc(out_dve[u], 1)
                    for odd in range(2):
                        lo, hi = odd * NK1, (odd + 1) * NK1

                        def heads(a):
                            return a.rearrange("p (m e c) -> p m e c", e=2, c=HD1)[:, :, odd, :]
                        last = nc.vector.tensor_tensor(v1[lo:hi, u, :, odd * HD1:(odd + 1) * HD1],
                                                       heads(psL[lo:hi, P:P + S]), heads(bias_v[lo:hi, :]), ALU.add)
                    last.then_inc(out_dve[u], 1)
                    if final:
                        first_norm.normalise(dve, u, first_x[:, u], first_x[:, u], first_norm.STEPS_RMS)

            with dve.Fori(0, PAIRS - 1) as i:
                body(i, False)
            body(PAIRS - 1, True)

        @block.scalar
        def _(act):
            for u in range(2):
                act.sem_inc(out_act[u], 1)
            for n in range(len(blocks)):
                for half in range(2):
                    act.wait_ge(wT_full, 2 * n + half + 1)
                    nc.scalar.copy(weight_parts(n, half)[0], psT[:, half, :].rearrange("p (k n) -> p k n", k=4)
                                   ).then_inc(wT_hi, 1)
            act.wait_ge(proj_loaded, 32)
            for m, e in enumerate((0, 1, 1)):
                last = nc.scalar.copy(wvp_hi[:, :, KV0 + m * NK1:KV0 + (m + 1) * NK1], projs[:, :, e * NK1:(e + 1) * NK1])
            last.then_inc(proj_hi, 1)

            def high_ctx(b):
                for n in range(FILLS):
                    act.wait_ge(psT_full, FILLS * b + n + 1)
                    nc.scalar.copy(cT_hi[:, 2 * n:2 * n + 2, :], psT[:, n % 2, :].rearrange("p (k n) -> p k n", k=2)
                                   ).then_inc(cT_high, 1)

            def high_wq(b, i, u, half):
                act.wait_ge(wq_full, 2 * b + half + 1)
                nc.scalar.copy(wq.hi[:, 4 * half:4 * half + 4, bass.ds((REP0 * u + i) * P, P)],
                               psW[:, :].rearrange("p (k n) -> p k n", k=4)).then_inc(wq_hi, 1)

            high_ctx(0)

            def body(i, final):
                for u in range(2):
                    b = 2 * i + u
                    act.wait_ge(out_stored[u], 16 * STORES * i + 1)
                    for half in range(HALF0):
                        act.wait_ge(psP_full, 4 * b + 1 + half)
                        nc.scalar.mul(k0_hi[:, u, half, :], psP[:, half, 0:S], HD0 ** -0.5).then_inc(out_act[u], 1)
                    high_wq(b, i, u, 0)
                    for t in range(TT):
                        act.wait_ge(mid_ready, 2 * b + 1 + t)
                        nc.scalar.copy(v0[:, u, t, :], psP[:, 2 + t, 0:KV0]).then_inc(out_act[u], 1)
                    high_wq(b, i, u, 1)
                    if not (final and u == 1):
                        high_ctx(b + 1)

            with act.Fori(0, PAIRS - 1) as i:
                body(i, False)
            body(PAIRS - 1, True)


class Norm:

    def __init__(self, nc, es, name, sh):
        def sb(n, shape):
            return es.enter_context(nc.sbuf_tensor(f"{name}_{n}", shape, F32))

        def sem(n):
            return es.enter_context(nc.semaphore(f"{name}_{n}"))
        self.nc, self.sh = nc, sh
        self.stats = sb("stats", [P, TT, 2, 6])
        self.moments = sb("moments", [P, TT, 2])
        self.tmp = sb("tmp", [P, 4, TT])
        self.rstd = sb("rstd", [P, TT])
        self.stats_done = sem("stats_done")
        self.moments_done = sem("moments_done")
        self.rstd_steps = sem("rstd_steps")
        self.normed = sem("normed")

    def stats_of(self, x, t):
        for h in range(2):
            last = self.nc.vector.bn_stats(self.stats[:, t, h, :], x[:, t, h * HALF_N:(h + 1) * HALF_N])
        return last

    def moments_of(self, dve, b, x, last_tile_only=False):
        nc = self.nc
        for t in range(TT - 1 if last_tile_only else 0, TT):
            last = self.stats_of(x, t)
        last.then_inc(self.stats_done, 1)
        self.aggregate(dve, b)

    def aggregate(self, dve, b):
        nc = self.nc
        dve.wait_ge(self.stats_done, b + 1)
        hold(dve, self.sh)
        for t in range(TT):
            last = nc.vector.bn_aggr(self.moments[:, t, :], self.stats[:, t, :, :])
        last.then_inc(self.moments_done, 1)

    STEPS, STEPS_RMS = 2, 6

    def rstd_of(self, pool, b, rms):
        nc, tmp = self.nc, self.tmp
        steps = self.STEPS_RMS if rms else self.STEPS
        var, half = self.moments[:, :, 1], self.sh.minus_half[:, 0:TT]
        done = [0]

        def step(instruction):
            instruction.then_inc(self.rstd_steps, 1)
            done[0] += 1
            pool.wait_ge(self.rstd_steps, steps * b + done[0])
        pool.wait_ge(self.moments_done, b + 1)
        hold(pool, self.sh)
        step(nc.gpsimd.tensor_scalar(tmp[:, 0, :], var, LN_EPS, None, ALU.add))
        if not rms:
            step(nc.gpsimd.tensor_tensor(self.rstd[:, :], tmp[:, 0, :], half, ALU.pow))
            return
        step(nc.gpsimd.tensor_tensor(tmp[:, 1, :], tmp[:, 0, :], half, ALU.pow))
        step(nc.gpsimd.tensor_tensor(tmp[:, 2, :], tmp[:, 1, :], tmp[:, 1, :], ALU.mult))
        step(nc.gpsimd.tensor_tensor(tmp[:, 3, :], tmp[:, 2, :], var, ALU.mult))
        hold(pool, self.sh)
        step(nc.gpsimd.tensor_scalar(tmp[:, 2, :], tmp[:, 3, :], LN_EPS, None, ALU.add))
        nc.gpsimd.tensor_tensor(tmp[:, 3, :], tmp[:, 2, :], tmp[:, 0, :], ALU.mult).then_inc(self.rstd_mid, 1)
        pool.wait_ge(self.rstd_mid, b + 1)
        step(nc.gpsimd.tensor_tensor(self.rstd[:, :], tmp[:, 3, :], half, ALU.pow))

    def normalise(self, dve, b, x, out, steps):
        dve.wait_ge(self.rstd_steps, steps * b + steps)
        for t in range(TT):
            last = self.nc.vector.tensor_scalar(out[:, t, :], x[:, t, :], self.moments[:, t, 0:1],
                                                self.rstd[:, t:t + 1], ALU.subtract, ALU.mult)
        last.then_inc(self.normed, 1)


class StreamNorm(Norm):

    def __init__(self, nc, es, name, sh):
        super().__init__(nc, es, name, sh)
        self.mean = es.enter_context(nc.sbuf_tensor(f"{name}_mean", [P, B, TT], F32))
        self.var = es.enter_context(nc.sbuf_tensor(f"{name}_var", [P, B, TT], F32))
        self.rstds = es.enter_context(nc.sbuf_tensor(f"{name}_rstds", [P, B, TT], F32))
        self.eps = es.enter_context(nc.sbuf_tensor(f"{name}_eps", [P, TT], F32))
        self.eps_filled = es.enter_context(nc.semaphore(f"{name}_eps_filled"))
        self.kept = es.enter_context(nc.semaphore(f"{name}_kept"))

    def keep(self, dve, b):
        nc, at = self.nc, bass.ds(b, 1)
        dve.wait_ge(self.moments_done, b + 1)
        hold(dve, self.sh)
        nc.vector.tensor_copy(self.mean[:, at, :].rearrange("p b t -> p (b t)"), self.moments[:, :, 0])
        nc.vector.tensor_copy(self.var[:, at, :].rearrange("p b t -> p (b t)"), self.moments[:, :, 1]).then_inc(self.kept, 1)

    def rstd_of_batch(self, pool, b):
        nc, rstd = self.nc, self.rstds[:, bass.ds(b, 1), :].rearrange("p b t -> p (b t)")
        pool.wait_ge(self.kept, b + 1)
        hold(pool, self.sh)
        nc.gpsimd.tensor_tensor(self.tmp[:, 0, :], self.var[:, bass.ds(b, 1), :].rearrange("p b t -> p (b t)"),
                                self.eps[:, :], ALU.add).then_inc(self.rstd_steps, 1)
        pool.wait_ge(self.rstd_steps, 2 * b + 1)
        nc.gpsimd.tensor_tensor(rstd, self.tmp[:, 0, :], self.sh.minus_half[:, 0:TT], ALU.pow).then_inc(self.rstd_steps, 1)

    def normalise_tile(self, b, t, x, out):
        at = bass.ds(b, 1)
        self.nc.vector.tensor_scalar(out[:, t, :], x[:, t, :], self.mean[:, at, t], self.rstds[:, at, t],
                                     ALU.subtract, ALU.mult).then_inc(self.normed, 1)


def plain(tile):
    return tile.bitcast(F32)


def attn0_stage(nc, sh, c, scratch, wq, rows, norm):
    ident = sh.ident
    UNITS = KT * TT
    XFILLS = KT // 2
    Q_USES = XFILLS + KT
    QUAD = KT // 2
    BANK0_DVE = set(range(XFILLS + 1, UNITS, 2))
    QUAD_DMAS = JH0 * 4
    COPY_STEP = {f + 1: f for f in range(XFILLS)}
    for t in range(KT - 1):
        COPY_STEP[XFILLS + 1 + 3 * (t // 2) + 2 * (t % 2)] = XFILLS + t
    with ExitStack() as es:
        def sb(name, shape, dt=F32):
            return es.enter_context(nc.sbuf_tensor("a_" + name, shape, dt))

        def sem(name):
            return es.enter_context(nc.semaphore("a_" + name))

        x = rows.batches
        xT_hi = sb("xT_hi", [P, KT, S], F32R)
        xT_lo = sb("xT_lo", [P, KT, S], F32R)
        q_hi = sb("q_hi", [P, KT, S], F32R)
        q_lo = sb("q_lo", [P, KT, S], F32R)
        q_stack = sb("q_stack", [P, KT, JH0, S], F32R)
        k_stack = sb("k_stack", [P, 2, NKV0, S], F32R)
        v0 = sb("v0", [P, 2, TT, KV0])
        prob = sb("prob", [P, 2, JH0, S])
        probT = sb("probT", [P, 2, TT, JH0, P])
        negmax = sb("negmax", [P, 2, JH0])
        sums = sb("sums", [P, 2, TT, JH0])
        recip_head = sb("recip_head", [P, 2, TT, JH0])
        recip = sb("recip", [P, 2, TT, JH0, HD0])
        recipT = sb("recipT", [P, S])
        oT = sb("oT", [P, KT, S])
        psS = es.enter_context(nc.psum_tensor("a_psS", [P, 4, HALF_N], F32))
        psT = es.enter_context(nc.psum_tensor("a_psT", [P, 2, HALF_N], F32))
        psO = es.enter_context(nc.psum_tensor("a_psO", [P, 2, S], F32))
        psQ = es.enter_context(nc.psum_tensor("a_psQ", [P, HALF_N], F32))
        coefs = sb("coefs", [P, NE, KT, RR])
        masks = sb("masks", [P, NE, KT, RR], U8)
        wsum = sb("wsum", [P, KT, RR])
        update = sb("update", [RR, D])
        QUARTER, UPDATE_STEP = D // 4, UNITS - 3 * 4
        def table(quarter, part):
            return plain((q_hi, q_lo)[part])[:, quarter % 2 * QUAD:(quarter % 2 + 1) * QUAD, :]

        x_loaded = [sem(f"x_loaded{u}") for u in range(2)]
        kv_loaded = [sem(f"kv_loaded{u}") for u in range(2)]
        psQ_full, psQ_hi = sem("psQ_full"), sem("psQ_hi")
        psQ_lo = sem("psQ_lo")
        q_stacked = [sem(f"q_stacked{h}") for h in range(2)]
        scores_full, max_ready, exp_done = sem("scores_full"), sem("max_ready"), sem("exp_done")
        psT_full = [sem(f"psT_full{p}") for p in range(2)]
        psT_copied = [sem(f"psT_copied{p}") for p in range(2)]
        head_ready, recip_ready = sem("head_ready"), sem("recip_ready")
        psO_full, recipT_ready = sem("psO_full"), sem("recipT_ready")
        o_ready = sem("o_ready")
        o_stored = [sem(f"o_stored{h}") for h in range(2)]
        coefs_loaded = sem("coefs_loaded")
        table_loaded = [sem(f"table_loaded{u}") for u in range(2)]
        masked_done, summed = sem("masked_done"), sem("summed")
        update_full, update_copied, update_stored = sem("update_full"), sem("update_copied"), sem("update_stored")

        block = es.enter_context(nc.Block())

        @block.sync
        def _(sp):
            for h in range(2):
                sp.sem_inc(q_stacked[h], 1)
                sp.sem_inc(o_stored[h], 1)

            def load_x(b, u):
                sp.dma_start(x[:, u, :, :], c["x"][bass.ds(b, 1)].rearrange("b (t p) d -> p (b t) d", p=P)
                             ).then_inc(x_loaded[u], 16)

            def load_kv(b, u):
                for part, name in enumerate(("k0_hi", "k0_lo", "k0_hi", "k0_lo")):
                    sp.dma_start(plain(k_stack)[part * HD0:(part + 1) * HD0, u, :, :],
                                 scratch[name][bass.ds(b, 1)].rearrange("b (g c) s -> c (b g) s", c=HD0)
                                 ).then_inc(kv_loaded[u], 16)
                sp.dma_start(v0[:, u].rearrange("p a n -> p (a n)"),
                             scratch["v0"][bass.ds(b, 1)].rearrange("b p n -> p (b n)")).then_inc(kv_loaded[u], 16)

            def stack_quad(b, h):
                sp.wait_ge(psQ_lo, Q_USES * b + XFILLS + QUAD * (h + 1) + 1)
                tiles = slice(QUAD * h, QUAD * (h + 1))
                for part, src in enumerate((q_hi, q_hi, q_lo, q_lo)):
                    for j in range(JH0):
                        sp.dma_start(plain(q_stack)[part * HD0:(part + 1) * HD0, tiles, j, :],
                                     plain(src)[j * HD0:(j + 1) * HD0, tiles, :]).then_inc(q_stacked[h], 16)

            def store_quad(b, h):
                sp.wait_ge(o_ready, KT * b + QUAD * (h + 1) + 1)
                o_rows = scratch["o"].rearrange("b (h j r c) s -> b h j c r s", h=HALF0, j=JH0, r=REP0)
                for j in range(JH0):
                    sp.dma_start(o_rows[bass.ds(b, 1), h, j].rearrange("b c r s -> c (b r) s"),
                                 oT[j * HD0:(j + 1) * HD0, QUAD * h:QUAD * (h + 1), :]).then_inc(o_stored[h], 16)

            load_kv(0, 0)
            stack_quad(0, 0)
            for name, lo, ranks in (("0", 0, R0), ("1", R0, R1)):
                for e in range(NE):
                    sp.dma_start(coefs[:, e, :, lo:lo + ranks],
                                 c["coefs" + name][e].rearrange("(t p) r -> p t r", p=P)).then_inc(coefs_loaded, 16)
                    sp.dma_start(masks[:, e, :, lo:lo + ranks],
                                 c["mask" + name][e].rearrange("(t p) r -> p t r", p=P)).then_inc(coefs_loaded, 16)

            def load_table(quarter):
                rows_of_table = c["irfft"].rearrange("(h t p) o -> h p t o", h=2, p=P)
                for part in range(2):
                    sp.dma_start(table(quarter, part), rows_of_table[part, :, :, quarter * QUARTER:(quarter + 1) * QUARTER]
                                 ).then_inc(table_loaded[quarter % 2], 16)

            def body(i, final):
                for u in range(2):
                    b = 2 * i + u
                    if final and u == 1:
                        sp.wait_ge(q_stacked[0], 16 * QUAD_DMAS * B + 1)
                        load_table(0)
                    stack_quad(b, 1)
                    if final and u == 1:
                        sp.wait_ge(q_stacked[1], 16 * QUAD_DMAS * B + 1)
                        load_table(1)
                        for n, block in enumerate(rows.blocks):
                            sp.dma_start(block, c["wo"][n * P:(n + 1) * P, :]).then_inc(rows.wo_loaded, 16)
                        for quarter in range(2, 4):
                            sp.wait_ge(update_full, quarter - 1)
                            load_table(quarter)
                    if not final:
                        sp.wait_ge(psQ_full, Q_USES * b + XFILLS)
                        load_x(b + 2, u)
                    if not (final and u == 1):
                        sp.wait_ge(o_ready, KT * b + 1)
                        load_kv(b + 1, 1 - u)
                    store_quad(b, 0)
                    if not (final and u == 1):
                        stack_quad(b + 1, 0)
                    store_quad(b, 1)

            with sp.Fori(0, PAIRS - 1) as i:
                body(i, False)
            body(PAIRS - 1, True)
            sp.wait_ge(update_copied, 4)
            sp.dma_start(scratch["update"], update[:, :]).then_inc(update_stored, 16)
            sp.wait_ge(update_stored, 16)
            for h in range(2):
                sp.wait_ge(o_stored[h], 16 * JH0 * B + 1)

        @block.gpsimd
        def _(pool):
            def spread_reciprocals(b, t):
                pool.wait_ge(head_ready, KT * b + t + 1)
                hold(pool, sh)
                nc.gpsimd.tensor_copy(recip[:, t % 2], recip_head[:, t % 2].unsqueeze(3).broadcast_to([P, TT, JH0, HD0])
                                      ).then_inc(recip_ready, 1)

            def body(i, final):
                for u in range(2):
                    b = 2 * i + u
                    for t in range(KT):
                        spread_reciprocals(b, t)
                        if t == 5 and not final:
                            norm.rstd_of(pool, b + 2, rms=True)

            with pool.Fori(0, PAIRS - 1) as i:
                body(i, False)
            body(PAIRS - 1, True)

        @block.tensor
        def _(pe):
            def bank_of(use, prologue):
                return psS[:, use % 4, :] if prologue and use < Q_USES - 1 else psQ[:, :]

            def transposed_x(b, u, f, prologue=False):
                bank = bank_of(f, prologue)
                if f == 0 and not prologue:
                    pe.wait_ge(norm.normed, b + 1)
                if not prologue:
                    pe.wait_ge(psQ_lo, Q_USES * b + f + 1)
                for q in range(2):
                    for t in range(TT):
                        kt = 2 * f + q
                        last = nc.tensor.transpose(bank[:, (q * TT + t) * P:(q * TT + t + 1) * P],
                                                   x[:, u, t, kt * P:(kt + 1) * P], ident[:, :])
                last.then_inc(psQ_full, 1)

            def query(b, t, tiles, prologue=False):
                use = XFILLS + t
                bank = bank_of(use, prologue)
                if not prologue:
                    if tiles[0] == 0:
                        pe.wait_ge(psQ_lo, Q_USES * b + use + 1)
                elif use < Q_USES - 1:
                    pe.wait_ge(psQ_lo, XFILLS + 1 if t == 0 else use - 2)
                for kt in tiles:
                    for w, a in ((wq.hi, xT_hi), (wq.lo, xT_hi), (wq.hi, xT_lo)):
                        last = nc.tensor.matmul(bank[:, 0:S], w[:, kt, t * P:(t + 1) * P], a[:, kt, :],
                                                start=(kt == 0 and w is wq.hi and a is xT_hi),
                                                stop=(kt == KT - 1 and a is xT_lo))
                if tiles[-1] == KT - 1:
                    last.then_inc(psQ_full, 1)

            def query_step(b, u, n):
                if n < XFILLS:
                    transposed_x(b, u, n)
                    return
                three, part = (n - XFILLS) // 3, (n - XFILLS) % 3
                if part == 0:
                    query(b, 2 * three, range(KT))
                else:
                    query(b, 2 * three + 1, range((part - 1) * KT // 2, part * KT // 2))

            def scores(b, i, u, n):
                t, qb = n // TT, n % TT
                if n % (UNITS // 2) == 0:
                    pe.wait_ge(q_stacked[t // QUAD], 16 * QUAD_DMAS * (b + 1) + 1)
                if n == 0:
                    pe.wait_ge(kv_loaded[u], 16 * 5 * (i + 1))
                for j in range(JH0):
                    last = nc.tensor.matmul(psS[:, 2 * (n % 2) + j // 2, (j % 2) * S:(j % 2 + 1) * S],
                                            q_stack[:, t, j, qb * P:(qb + 1) * P],
                                            k_stack[:, u, (t // REP0) * JH0 + j, :], start=True, stop=True)
                last.then_inc(scores_full, 1)

            def transposes(b, n):
                pe.wait_ge(exp_done, UNITS * b + n + 1)
                for kt in range(TT):
                    pe.wait_ge(psT_copied[kt], UNITS * b + n + 1)
                    for j in range(JH0):
                        last = nc.tensor.transpose(psT[:, kt, j * P:(j + 1) * P],
                                                   prob[:, n % 2, j, kt * P:(kt + 1) * P], ident[:, :])
                    last.then_inc(psT_full[kt], 1)

            def values(b, u, n):
                t, qb = n // TT, n % TT
                if qb == 0:
                    pe.wait_ge(o_ready, KT * b + t + 1)
                for kt in range(TT):
                    pe.wait_ge(psT_copied[kt], UNITS * b + n + 2)
                for kt in range(TT):
                    for j in range(JH0):
                        head = (t // REP0) * JH0 + j
                        nc.tensor.matmul(psO[j * HD0:(j + 1) * HD0, 0, qb * P:(qb + 1) * P],
                                         v0[:, u, kt, head * HD0:(head + 1) * HD0], probT[:, n % 2, kt, j, :],
                                         start=(kt == 0), stop=(kt == TT - 1))
                if qb == TT - 1:
                    pe.wait_ge(recip_ready, KT * b + t + 1)
                    for s in range(TT):
                        last = nc.tensor.transpose(psO[:, 1, s * P:(s + 1) * P],
                                                   recip[:, t % 2, s, :, :].rearrange("p j c -> p (j c)"), ident[:, :])
                    last.then_inc(psO_full, 1)

            for f in range(XFILLS):
                transposed_x(0, 0, f, True)
            for t in range(KT):
                query(0, t, range(KT), True)
            pe.wait_ge(psQ_lo, Q_USES)
            scores(0, 0, 0, 0)
            scores(0, 0, 0, 1)

            def update_part(quarter, kt):
                if kt == 0:
                    if quarter == 0:
                        pe.wait_ge(summed, 1)
                        pe.wait_ge(psQ_lo, Q_USES * B + 1)
                    else:
                        pe.wait_ge(update_copied, quarter)
                    pe.wait_ge(table_loaded[quarter % 2], 32 * (quarter // 2) + 32)
                last = nc.tensor.matmul(psQ[0:RR, 0:QUARTER], wsum[:, kt, :], table(quarter, kt // QUAD)[:, kt % QUAD, :],
                                        start=(kt == 0), stop=(kt == KT - 1))
                if kt == KT - 1:
                    last.then_inc(update_full, 1)

            update_steps = {UPDATE_STEP + 3 * quarter + n: [(quarter, kt) for kt in range(3 * n, min(3 * n + 3, KT))]
                            for quarter in range(4) for n in range(3)}

            def body(i, final):
                for u in range(2):
                    b = 2 * i + u
                    more = not (final and u == 1)
                    for n in range(UNITS):
                        transposes(b, n)
                        if n + 2 < UNITS:
                            scores(b, i, u, n + 2)
                        elif more:
                            scores(b + 1, i + u, 1 - u, n + 2 - UNITS)
                        if n:
                            values(b, u, n - 1)
                        if more:
                            query_step(b + 1, 1 - u, n)
                        else:
                            for quarter, kt in update_steps.get(n, ()):
                                update_part(quarter, kt)
                    values(b, u, UNITS - 1)

            with pe.Fori(0, PAIRS - 1) as i:
                body(i, False)
            body(PAIRS - 1, True)

        @block.vector
        def _(dve):
            dve.sem_inc(psT_copied[0], 1)
            dve.sem_inc(psQ_lo, 1)
            dve.sem_inc(o_ready, 1)
            def split(b, use, prologue=False):
                bank = psS[:, use % 4, :] if prologue else psQ[:, :]
                dve.wait_ge(psQ_full, Q_USES * b + use + 1)
                if use < XFILLS:
                    cols = slice(2 * use, 2 * use + 2)
                    hi, lo, src = xT_hi[:, cols, :], xT_lo[:, cols, :], bank.rearrange("p (k n) -> p k n", k=2)
                    high = plain(xT_hi)[:, cols, :]
                else:
                    t = use - XFILLS
                    if t % QUAD == 0:
                        dve.wait_ge(q_stacked[t // QUAD], 16 * QUAD_DMAS * b + 1)
                    hi, lo, src, high = q_hi[:, t, :], q_lo[:, t, :], bank[:, 0:S], plain(q_hi)[:, t, :]
                nc.vector.tensor_copy(hi, src).then_inc(psQ_hi, 1)
                dve.wait_ge(psQ_hi, Q_USES * b + use + 1)
                nc.vector.tensor_tensor(lo, src, high, ALU.subtract).then_inc(psQ_lo, 1)

            def maximum(b, n):
                dve.wait_ge(scores_full, UNITS * b + n + 1)
                bank = 2 * (n % 2)
                nc.vector.tensor_reduce(negmax[:, n % 2, :], psS[:, bank:bank + 2, :].rearrange("p a (j k) -> p (a j) k", k=S),
                                        AX_X, ALU.max, negate=True).then_inc(max_ready, 1)

            def normalise_o(b, t):
                if t % QUAD == 0:
                    dve.wait_ge(o_stored[t // QUAD], 16 * JH0 * b + 1)
                dve.wait_ge(psO_full, KT * b + t + 1)
                nc.vector.tensor_copy(recipT[:, :], psO[:, 1, :]).then_inc(recipT_ready, 1)
                dve.wait_ge(recipT_ready, KT * b + t + 1)
                nc.vector.tensor_tensor(oT[:, t, :], psO[:, 0, :], recipT[:, :], ALU.mult).then_inc(o_ready, 1)

            for use in range(Q_USES - 1):
                split(0, use, True)
            maximum(0, 0)
            maximum(0, 1)
            dve.wait_ge(coefs_loaded, 16 * 4 * NE)
            nc.vector.tensor_tensor(coefs[:, :, :, :], coefs[:, :, :, :], masks[:, :, :, :], ALU.mult).then_inc(masked_done, 1)
            dve.wait_ge(masked_done, 1)
            nc.vector.tensor_tensor(wsum[:, :, :], coefs[:, 0, :, :], coefs[:, 1, :, :], ALU.add).then_inc(masked_done, 1)
            dve.wait_ge(masked_done, 2)
            nc.vector.tensor_tensor(wsum[:, :, :], wsum[:, :, :], coefs[:, 2, :, :], ALU.add).then_inc(summed, 1)

            def copy_update(quarter):
                dve.wait_ge(update_full, quarter + 1)
                nc.vector.tensor_scalar(update[:, quarter * QUARTER:(quarter + 1) * QUARTER], psQ[0:RR, 0:QUARTER], 0.5, None, ALU.mult
                                        ).then_inc(update_copied, 1)

            def body(i, final):
                for u in range(2):
                    b = 2 * i + u
                    more = not (final and u == 1)
                    for n in range(UNITS):
                        if n == 0:
                            split(b, Q_USES - 1)
                        elif n in COPY_STEP and more:
                            split(b + 1, COPY_STEP[n])
                        if n in BANK0_DVE:
                            dve.wait_ge(psT_full[0], UNITS * b + n + 1)
                            nc.vector.tensor_copy(probT[:, n % 2, 0, :, :],
                                                  psT[:, 0, :].rearrange("p (j q) -> p j q", j=JH0)).then_inc(psT_copied[0], 1)
                        if n % 2:
                            t = n // 2
                            dve.wait_ge(exp_done, UNITS * b + n + 1)
                            nc.vector.reciprocal(recip_head[:, t % 2], sums[:, t % 2]).then_inc(head_ready, 1)
                        if n + 2 < UNITS:
                            maximum(b, n + 2)
                        elif more:
                            maximum(b + 1, n + 2 - UNITS)
                        if n and n % 2 == 0:
                            normalise_o(b, n // 2 - 1)
                        if n == 6 and not final:
                            dve.wait_ge(x_loaded[u], 16 * i + 16)
                            norm.stats_of(x[:, u], 0)
                        if n == 9 and not final:
                            norm.moments_of(dve, b + 2, x[:, u], last_tile_only=True)
                        if n == 12 and not final:
                            norm.normalise(dve, b + 2, x[:, u], x[:, u], norm.STEPS_RMS)
                        if n > UPDATE_STEP and (n - UPDATE_STEP) % 3 == 0 and not more:
                            copy_update((n - UPDATE_STEP) // 3 - 1)
                    normalise_o(b, KT - 1)
                    if not more:
                        copy_update(3)

            with dve.Fori(0, PAIRS - 1) as i:
                body(i, False)
            body(PAIRS - 1, True)

        @block.scalar
        def _(act):
            act.sem_inc(psT_copied[1], 1)
            def exponentials(b, n):
                act.wait_ge(max_ready, UNITS * b + n + 1)
                t, qb = n // TT, n % TT
                for j in range(JH0):
                    last = nc.scalar.activation(prob[:, n % 2, j, :],
                                                psS[:, 2 * (n % 2) + j // 2, (j % 2) * S:(j % 2 + 1) * S], ACT.Exp,
                                                bias=negmax[:, n % 2, j:j + 1], accum_out=sums[:, t % 2, qb, j:j + 1])
                last.then_inc(exp_done, 1)

            exponentials(0, 0)
            exponentials(0, 1)

            def body(i, final):
                for u in range(2):
                    b = 2 * i + u
                    more = not (final and u == 1)
                    for n in range(UNITS):
                        for kt in range(TT):
                            if kt == 0 and n in BANK0_DVE:
                                continue
                            act.wait_ge(psT_full[kt], UNITS * b + n + 1)
                            nc.scalar.copy(probT[:, n % 2, kt, :, :],
                                           psT[:, kt, :].rearrange("p (j q) -> p j q", j=JH0)).then_inc(psT_copied[kt], 1)
                        if n + 2 < UNITS:
                            exponentials(b, n + 2)
                        elif more:
                            exponentials(b + 1, n + 2 - UNITS)

            with act.Fori(0, PAIRS - 1) as i:
                body(i, False)
            body(PAIRS - 1, True)


def proj0_stage(nc, sh, c, scratch, quant, w_ffn, rows):
    ident = sh.ident
    with ExitStack() as es:
        sems = []
        es.callback(lambda: free_semaphores(nc, sems))

        def sb(name, shape, dt=F32):
            return es.enter_context(nc.sbuf_tensor("p_" + name, shape, dt))

        def sem(name):
            sems.append(nc.alloc_semaphore("p_" + name))
            return sems[-1]

        w_hi = sb("w_hi", [P, KT, D], F32R)
        w_lo = sb("w_lo", [P, KT, D], F32R)
        raw = rows.blocks
        SLOTS = len(raw)
        o_lo = sb("o_lo", [P, 2, KT, S], F32R)
        o_hi = sb("o_hi", [P, 2, KT, S], F32R)
        x = sb("x", [P, 2, TT, D])
        weight = raw[2]
        update = sb("update", [P, D])
        enc = sb("enc", [P, 2, P])
        base = sb("base", [P, 2, HALF_N])
        full = sb("full", [P, 2, HALF_N])
        psW = es.enter_context(nc.psum_tensor("p_psW", [P, 4, HALF_N], F32))
        psY = es.enter_context(nc.psum_tensor("p_psY", [P, 4, HALF_N], F32))

        raw_loaded = [sem(f"raw_loaded{n}") for n in range(SLOTS)]
        w_full, whi_ready = sem("w_full"), sem("whi_ready")
        wlo_ready = sem("wlo_ready")
        o_loaded = [sem(f"o_loaded{u}") for u in range(2)]
        x_loaded = [sem(f"x_loaded{u}") for u in range(2)]
        ohi_ready, olo_ready, psY_full = sem("ohi_ready"), sem("olo_ready"), sem("psY_full")
        x1_ready = sem("x1_ready")
        x1_stored = [sem(f"x1_stored{u}") for u in range(2)]
        weight_loaded = sem("weight_loaded")
        columns_loaded = [sem(f"columns_loaded{u}") for u in range(2)]
        zeroed, update_loaded, tile_full, tile_hi = sem("zeroed"), sem("update_loaded"), sem("tile_full"), sem("tile_hi")
        base_copied = sem("base_copied")
        full_ready = sem("full_ready")
        tile_lo = sem("tile_lo")
        wmax_done = sem("wmax_done")

        block = es.enter_context(nc.Block())

        @block.sync
        def _(sp):
            def load_batch(b, u):
                sp.dma_start(plain(o_lo)[:, u, :, :], scratch["o"][bass.ds(b, 1)].rearrange("b (k p) s -> p (b k) s", p=P)
                             ).then_inc(o_loaded[u], 16)
                sp.dma_start(x[:, u, :, :], c["x"][bass.ds(b, 1)].rearrange("b (t p) d -> p (b t) d", p=P)
                             ).then_inc(x_loaded[u], 16)

            def store_batch(i, u):
                sp.wait_ge(x1_ready, 4 * (2 * i + u) + 8)
                sp.dma_start(scratch["x1"][bass.ds(2 * i + u, 1)].rearrange("b (t p) d -> p (b t) d", p=P),
                             x[:, u, :, :]).then_inc(x1_stored[u], 16)

            def load_columns(kt, u):
                sp.dma_start(raw[u].rearrange("p (t d) -> p t d", t=KT),
                             c["W_base"][:, bass.ds(kt * P, P)].rearrange("(t p) d -> p t d", p=P)
                             ).then_inc(columns_loaded[u], 16)
                for name, lo, r in (("enc0", 0, R0), ("enc1", R0, R1)):
                    sp.dma_start(enc[lo:lo + r, u, :], c[name][:, bass.ds(kt * P, P)]).then_inc(columns_loaded[u], 16)

            def load_weight(kt):
                sp.dma_start(weight, c["weight"][bass.ds(kt * P, P), :]).then_inc(weight_loaded, 16)

            sp.wait_ge(rows.wo_loaded, 16 * SLOTS)
            for n in range(SLOTS):
                sp.sem_inc(raw_loaded[n], 16)
            load_batch(0, 0)
            for n in range(SLOTS):
                sp.wait_ge(w_full, 2 * n + 2)
                sp.dma_start(raw[n], c["wo"][(SLOTS + n) * P:(SLOTS + n + 1) * P, :]).then_inc(raw_loaded[n], 16)
            sp.wait_ge(zeroed, 2)
            sp.dma_start(update[0:RR, :], scratch["update"]).then_inc(update_loaded, 16)
            for u in range(2):
                sp.wait_ge(w_full, 2 * (SLOTS + u) + 2)
                load_columns(u, u)
            load_batch(1, 1)
            sp.wait_ge(w_full, 2 * (SLOTS + 2) + 2)
            load_weight(0)
            with sp.Fori(0, PAIRS - 1) as i:
                for u in range(2):
                    sp.wait_ge(tile_full, 4 * i + 2 * u + 2)
                    load_columns(2 * i + u + 2, u)
                    sp.wait_ge(wmax_done, 2 * i + u + 1)
                    load_weight(2 * i + u + 1)
                    store_batch(i, u)
                    sp.wait_ge(x1_stored[u], 16 * i + 16)
                    load_batch(2 * i + u + 2, u)
            for u in range(2):
                if u == 0:
                    sp.wait_ge(wmax_done, B - 1)
                    load_weight(B - 1)
                store_batch(PAIRS - 1, u)
            for u in range(2):
                sp.wait_ge(x1_stored[u], 16 * PAIRS)

        @block.tensor
        def _(pe):
            with pe.Fori(0, KT // SLOTS) as i:
                for n in range(SLOTS):
                    pe.wait_ge(raw_loaded[n], 16 * i + 16)
                    for half in range(2):
                        bank = 2 * (n % 2) + half
                        pe.wait_ge(wlo_ready, 2 * SLOTS * i + 2 * n + half + 1)
                        for q in range(4):
                            kt = 4 * half + q
                            last = nc.tensor.transpose(psW[:, bank, q * P:(q + 1) * P],
                                                       raw[n][:, kt * P:(kt + 1) * P], ident[:, :])
                        last.then_inc(w_full, 1)
            pe.wait_ge(wlo_ready, 2 * KT + 4)
            pe.wait_ge(zeroed, 2)
            pe.wait_ge(update_loaded, 16)

            def weight_tile(b, i, u):
                pe.wait_ge(columns_loaded[u], 48 * i + 48)
                pe.wait_ge(base_copied, 2 * b + 2)
                pe.wait_ge(full_ready, 2 * b + 2)
                for h in range(2):
                    for q in range(4):
                        ot = 4 * h + q
                        nc.tensor.transpose(psW[:, h, q * P:(q + 1) * P], raw[u][:, ot * P:(ot + 1) * P], ident[:, :])
                    nc.tensor.matmul(psW[:, 2 + h, :], enc[:, u, :], update[:, h * HALF_N:(h + 1) * HALF_N],
                                     start=True, stop=True).then_inc(tile_full, 1)

            with pe.Fori(0, PAIRS) as i:
                for u in range(2):
                    b = 2 * i + u
                    for t in range(TT):
                        for h in range(2):
                            pe.wait_ge(x1_ready, 4 * b + 2 * t + h + 1)
                            for kt in range(KT):
                                if t == 0 and h == 0 and kt % 2 == 0:
                                    pe.wait_ge(olo_ready, 4 * b + kt // 2 + 1)
                                for a, w in ((o_hi, w_hi), (o_hi, w_lo), (o_lo, w_hi)):
                                    last = nc.tensor.matmul(psY[:, 2 * t + h, :], a[:, u, kt, t * P:(t + 1) * P],
                                                            w[:, kt, h * HALF_N:(h + 1) * HALF_N],
                                                            start=(kt == 0 and a is o_hi and w is w_hi),
                                                            stop=(kt == KT - 1 and a is o_lo))
                            last.then_inc(psY_full, 1)
                        if t == 0:
                            weight_tile(b, i, u)

        @block.vector
        def _(dve):
            dve.sem_inc(wlo_ready, 4)
            dve.sem_inc(x1_ready, 4)
            with dve.Fori(0, KT // SLOTS) as i:
                for n in range(SLOTS):
                    for half in range(2):
                        bank = 2 * (n % 2) + half
                        dve.wait_ge(whi_ready, 2 * SLOTS * i + 2 * n + half + 1)
                        cols = bass.ds((SLOTS * i + n) * P, P)
                        nc.vector.tensor_tensor(w_lo[:, 4 * half:4 * half + 4, cols],
                                                psW[:, bank, :].rearrange("p (k n) -> p k n", k=4),
                                                plain(w_hi)[:, 4 * half:4 * half + 4, cols],
                                                ALU.subtract).then_inc(wlo_ready, 1)
            dve.sem_inc(full_ready, 2)

            def low_parts(b, u):
                for n in range(4):
                    dve.wait_ge(ohi_ready, 4 * b + n + 1)
                    cols = slice(2 * n, 2 * n + 2)
                    nc.vector.tensor_tensor(o_lo[:, u, cols, :], plain(o_lo)[:, u, cols, :], plain(o_hi)[:, u, cols, :],
                                            ALU.subtract).then_inc(olo_ready, 1)

            low_parts(0, 0)

            def body(i, final):
                for u in range(2):
                    b = 2 * i + u
                    if not (final and u == 1):
                        low_parts(b + 1, 1 - u)
                    dve.wait_ge(weight_loaded, 16 * b + 16)
                    nc.vector.tensor_reduce(quant.w_max[:, bass.ds(b, 1)], weight, AX_X, ALU.max,
                                            apply_absolute_value=True).then_inc(wmax_done, 1)
                    dve.wait_ge(x_loaded[u], 16 * i + 16)
                    for t in range(TT):
                        for h in range(2):
                            dve.wait_ge(psY_full, 4 * b + 2 * t + h + 1)
                            cols = slice(h * HALF_N, (h + 1) * HALF_N)
                            nc.vector.scalar_tensor_tensor(x[:, u, t, cols], psY[:, 2 * t + h, :], sh.gates[:, 0:1],
                                                           x[:, u, t, cols], op0=ALU.mult, op1=ALU.add
                                                           ).then_inc(x1_ready, 1)
                        if t == 0:
                            for h in range(2):
                                dve.wait_ge(base_copied, 2 * b + h + 3)
                                dve.wait_ge(tile_lo, 2 * b + h + 1)
                                nc.vector.tensor_tensor(full[:, h, :], base[:, h, :], psW[:, 2 + h, :], ALU.add
                                                        ).then_inc(full_ready, 1)

            with dve.Fori(0, PAIRS - 1) as i:
                body(i, False)
            body(PAIRS - 1, True)
            dve.wait_ge(wmax_done, B)
            nc.vector.tensor_reduce(quant.part_max[:, 1:2], quant.w_max[:, :], AX_X, ALU.max).then_inc(quant.part_done, 1)
            quant.scale_of(nc, dve, 1, 1)
            nc.vector.tensor_scalar(quant.w_shift[:, :], quant.scale[:, 1:2], FP8_SHIFT, None, ALU.mult)

        @block.gpsimd
        def _(pool):
            pool.sem_inc(tile_lo, 2)
            nc.gpsimd.memset(update[:, :], 0.0).then_inc(zeroed, 1)
            nc.gpsimd.memset(enc[:, :, :], 0.0).then_inc(zeroed, 1)
            with pool.Fori(0, KT) as kt:
                for h in range(2):
                    pool.wait_ge(tile_hi, 2 * kt + h + 1)
                    dst = bass.ds(h * HALF_N, HALF_N)
                    nc.gpsimd.tensor_tensor(w_ffn.lo[:, bass.ds(kt, 1), dst].rearrange("p a n -> p (a n)"), full[:, h, :],
                                            plain(w_ffn.hi)[:, bass.ds(kt, 1), dst].rearrange("p a n -> p (a n)"),
                                            ALU.subtract).then_inc(tile_lo, 1)
            pool.wait_ge(quant.part_done, 1)
            nc.gpsimd.partition_all_reduce(quant.all_max[:, 1:2], quant.part_max[:, 1:2], P, ABSMAX
                                           ).then_inc(quant.all_done, 1)

        @block.scalar
        def _(act):
            with act.Fori(0, KT // SLOTS) as i:
                for n in range(SLOTS):
                    for half in range(2):
                        bank = 2 * (n % 2) + half
                        act.wait_ge(w_full, 2 * SLOTS * i + 2 * n + half + 1)
                        nc.scalar.copy(w_hi[:, 4 * half:4 * half + 4, bass.ds((SLOTS * i + n) * P, P)],
                                       psW[:, bank, :].rearrange("p (k n) -> p k n", k=4)).then_inc(whi_ready, 1)

            act.sem_inc(base_copied, 2)

            def high_parts(b, i, u):
                act.wait_ge(o_loaded[u], 16 * i + 16)
                for n in range(4):
                    cols = slice(2 * n, 2 * n + 2)
                    nc.scalar.copy(o_hi[:, u, cols, :], plain(o_lo)[:, u, cols, :]).then_inc(ohi_ready, 1)

            high_parts(0, 0, 0)

            def body(i, final):
                for u in range(2):
                    b = 2 * i + u
                    if not (final and u == 1):
                        high_parts(b + 1, i + u, 1 - u)
                    for h in range(2):
                        act.wait_ge(tile_full, 2 * b + h + 1)
                        nc.scalar.copy(base[:, h, :], psW[:, h, :]).then_inc(base_copied, 1)
                    for h in range(2):
                        act.wait_ge(full_ready, 2 * b + h + 3)
                        nc.scalar.copy(w_ffn.hi[:, bass.ds(b, 1), h * HALF_N:(h + 1) * HALF_N].rearrange("p a n -> p (a n)"),
                                       full[:, h, :]).then_inc(tile_hi, 1)

            with act.Fori(0, PAIRS - 1) as i:
                body(i, False)
            body(PAIRS - 1, True)


def ffn0_stage(nc, sh, c, scratch, w_ffn, x, x2_norm, quant, attn1_bias):
    ident = sh.ident
    with ExitStack() as es:
        def sb(name, shape, dt=F32):
            return es.enter_context(nc.sbuf_tensor("f_" + name, shape, dt))

        def sem(name):
            return es.enter_context(nc.semaphore("f_" + name))

        bias = sb("bias", [P, D])
        xn = sb("xn", [P, TT, D])
        xT_hi = sb("xT_hi", [P, 2, KT, S], F32R)
        xT_lo = sb("xT_lo", [P, 2, KT, S], F32R)
        wraw = sb("wraw", [P, D])
        wscaled = sb("wscaled", [P, D])
        wshifted = sb("wshifted", [P, D])
        wmagic = sb("wmagic", [P, D])
        psT = es.enter_context(nc.psum_tensor("f_psT", [P, 4, HALF_N], F32))
        psY = es.enter_context(nc.psum_tensor("f_psY", [P, 4, HALF_N], F32))
        norm = Norm(nc, es, "f_norm", sh)

        bias_loaded, bias_gated = sem("bias_loaded"), sem("bias_gated")
        x_loaded = [sem(f"x_loaded{u}") for u in range(2)]
        psT_full, xhi_ready, xlo_ready = sem("psT_full"), sem("xhi_ready"), sem("xlo_ready")
        biased, psY_full, x2_ready = sem("biased"), sem("psY_full"), sem("x2_ready")

        wraw_loaded = sem("wraw_loaded")
        w_scaled = sem("w_scaled")
        wsteps = sem("wsteps")

        block = es.enter_context(nc.Block())

        @block.sync
        def _(sp):
            def load_x(b, u):
                sp.dma_start(batch_of(x, b),
                             scratch["x1"][bass.ds(b, 1)].rearrange("b (t p) d -> p (b t) d", p=P)).then_inc(x_loaded[u], 16)

            load_x(0, 0)
            sp.wait_ge(x_loaded[0], 16)
            load_x(1, 1)
            sp.dma_start(bias[:, :], c["b_base"].partition_broadcast(P)).then_inc(bias_loaded, 16)

            def load_weight(tile):
                sp.dma_start(wraw[:, :], c["weight"][bass.ds(tile * P, P), :]).then_inc(wraw_loaded, 16)

            load_weight(0)
            attn1_bias.load(sp, c)
            with sp.Fori(1, PAIRS) as i:
                for u in range(2):
                    sp.wait_ge(x_loaded[u], 16 * i)
                    load_x(2 * i + u, u)
                for u in range(2):
                    sp.wait_ge(w_scaled, 2 * i + u - 1)
                    load_weight(2 * i + u - 1)
            sp.wait_ge(w_scaled, B - 1)
            load_weight(B - 1)

        @block.gpsimd
        def _(pool):
            nc.gpsimd.memset(x2_norm.eps[:, :], LN_EPS).then_inc(x2_norm.eps_filled, 1)
            pool.wait_ge(x2_norm.eps_filled, 1)
            norm.rstd_of(pool, 0, rms=False)
            norm.rstd_of(pool, 1, rms=False)
            pool.wait_ge(bias_gated, 1)

            def body(i, final):
                for u in range(2):
                    b = 2 * i + u
                    pool.wait_ge(norm.normed, b + 1)
                    for t in range(TT):
                        rows = x[:, bass.ds(b, 1), t, :].rearrange("p b d -> p (b d)")
                        nc.gpsimd.tensor_tensor(rows, rows, bias[:, :], ALU.add).then_inc(biased, 1)
                    if not final:
                        norm.rstd_of(pool, b + 2, rms=False)
                    x2_norm.rstd_of_batch(pool, b)

            with pool.Fori(0, PAIRS - 1) as i:
                body(i, False)
            body(PAIRS - 1, True)

        @block.tensor
        def _(pe):
            def transposes(b):
                pe.wait_ge(norm.normed, b + 1)
                if not (isinstance(b, int) and b == 0):
                    pe.wait_ge(xlo_ready, 4 * b)
                for n in range(4):
                    for q in range(2):
                        for t in range(TT):
                            last = nc.tensor.transpose(psT[:, n, (q * TT + t) * P:(q * TT + t + 1) * P],
                                                       xn[:, t, (2 * n + q) * P:(2 * n + q + 1) * P], ident[:, :])
                    last.then_inc(psT_full, 1)

            transposes(0)

            def body(i, final):
                for u in range(2):
                    b = 2 * i + u
                    pe.wait_ge(xlo_ready, 4 * b + 4)
                    for t in range(TT):
                        for h in range(2):
                            if not (isinstance(i, int) and i == 0 and u == 0):
                                pe.wait_ge(x2_ready, 4 * b + 2 * t + h - 3)
                            for kt in range(KT):
                                rows = slice(t * P, (t + 1) * P)
                                cols = slice(h * HALF_N, (h + 1) * HALF_N)
                                for a, w in ((xT_hi, w_ffn.hi), (xT_hi, w_ffn.lo), (xT_lo, w_ffn.hi)):
                                    last = nc.tensor.matmul(psY[:, 2 * t + h, :], a[:, u, kt, rows], w[:, kt, cols],
                                                            start=(kt == 0 and a is xT_hi and w is w_ffn.hi),
                                                            stop=(kt == KT - 1 and a is xT_lo))
                            last.then_inc(psY_full, 1)
                        if t == 0 and not (final and u == 1):
                            transposes(b + 1)

            body(0, False)
            with pe.Fori(1, PAIRS - 1) as i:
                body(i, False)
            body(PAIRS - 1, True)

        @block.vector
        def _(dve):
            dve.sem_inc(wsteps, 1)

            def moments(i, u, b):
                dve.wait_ge(x_loaded[u], 16 * i + 16)
                hold(dve, sh)
                norm.moments_of(dve, b, batch_of(x, b))

            moments(0, 0, 0)
            norm.normalise(dve, 0, batch_of(x, 0), xn, norm.STEPS)

            def split_low(b, u):
                for n in range(4):
                    dve.wait_ge(xhi_ready, 4 * b + n + 1)
                    cols = slice(2 * n, 2 * n + 2)
                    nc.vector.tensor_tensor(xT_lo[:, u, cols, :].rearrange("p k n -> p (k n)"), psT[:, n, :],
                                            plain(xT_hi)[:, u, cols, :].rearrange("p k n -> p (k n)"),
                                            ALU.subtract).then_inc(xlo_ready, 1)

            split_low(0, 0)
            moments(0, 1, 1)
            norm.normalise(dve, 1, batch_of(x, 1), xn, norm.STEPS)
            dve.wait_ge(bias_loaded, 16)
            nc.vector.tensor_scalar(bias[:, :], bias[:, :], sh.gates[:, 2:3], None, ALU.mult).then_inc(bias_gated, 1)

            def round_weight(b):
                rounded = quant.weight[:, bass.ds(b, 1), :].rearrange("p a n -> p (a n)")
                dve.wait_ge(w_scaled, b + 1)
                fp8_magic(nc, wmagic[:, :], wshifted[:, :]).then_inc(wsteps, 1)
                dve.wait_ge(wsteps, 4 * b + 2)
                fp8_add_magic(nc, wshifted[:, :], wmagic[:, :], wscaled[:, :]).then_inc(wsteps, 1)
                dve.wait_ge(wsteps, 4 * b + 3)
                fp8_minus_rounded(nc, rounded, wmagic[:, :], wshifted[:, :]).then_inc(wsteps, 1)
                dve.wait_ge(wsteps, 4 * b + 4)
                fp8_clip(nc, rounded).then_inc(wsteps, 1)

            def body(i, final):
                for u in range(2):
                    b = 2 * i + u
                    round_weight(b)
                    if not (final and u == 1):
                        split_low(b + 1, 1 - u)
                    dve.wait_ge(biased, 2 * b + 2)
                    for t in range(TT):
                        for h in range(2):
                            dve.wait_ge(psY_full, 4 * b + 2 * t + h + 1)
                            cols = slice(h * HALF_N, (h + 1) * HALF_N)
                            rows = x[:, bass.ds(b, 1), t, cols].rearrange("p b d -> p (b d)")
                            nc.vector.scalar_tensor_tensor(rows, psY[:, 2 * t + h, :], sh.gates[:, 2:3], rows,
                                                           op0=ALU.mult, op1=ALU.add).then_inc(x2_ready, 1)
                        dve.wait_ge(x2_ready, 4 * b + 2 * t + 2)
                        hold(dve, sh)
                        last = x2_norm.stats_of(batch_of(x, b), t)
                        if t == 0 and not final:
                            moments(i + 1, u, b + 2)
                        if t == 1 and not final:
                            norm.normalise(dve, b + 2, batch_of(x, b + 2), xn, norm.STEPS)
                    last.then_inc(x2_norm.stats_done, 1)
                    x2_norm.aggregate(dve, b)
                    x2_norm.keep(dve, b)

            with dve.Fori(0, PAIRS - 1) as i:
                body(i, False)
            body(PAIRS - 1, True)

        @block.scalar
        def _(act):
            with act.Fori(0, PAIRS) as i:
                for u in range(2):
                    b = 2 * i + u
                    for n in range(4):
                        act.wait_ge(psT_full, 4 * b + n + 1)
                        nc.scalar.copy(xT_hi[:, u, 2 * n:2 * n + 2, :].rearrange("p k n -> p (k n)"), psT[:, n, :]
                                       ).then_inc(xhi_ready, 1)
                    act.wait_ge(wraw_loaded, 16 * b + 16)
                    act.wait_ge(wsteps, 4 * b + 1)
                    nc.scalar.mul(wscaled[:, :], wraw[:, :], quant.scale[:, 1:2])
                    nc.scalar.mul(wshifted[:, :], wraw[:, :], quant.w_shift[:, :]).then_inc(w_scaled, 1)


class Attn1Bias:

    def __init__(self, nc, es):
        self.q = es.enter_context(nc.sbuf_tensor("bias1_q", [P, CT1], F32))
        self.out = es.enter_context(nc.sbuf_tensor("bias1_out", [P, CT1], F32))
        self.loaded = es.enter_context(nc.semaphore("bias1_loaded"))

    def load(self, sp, c):
        for h in range(HT1):
            sp.dma_start(self.q[h * HD1:(h + 1) * HD1, :], c["bq1"].rearrange("(c t h) -> h c t", c=HD1, t=CT1)[h],
                         allow_slow_non_contiguous=True).then_inc(self.loaded, 16)
        sp.dma_start(self.out[:, :], c["bm1"].rearrange("(t p) -> p t", p=P), allow_slow_non_contiguous=True
                     ).then_inc(self.loaded, 16)
        sp.wait_ge(self.loaded, 16 * (HT1 + 1))


def attn1_stage(nc, sh, c, scratch, quant, x, x2_norm, bias):
    ident = sh.ident
    NT = D // P
    WIDTH = NH1 * NK1
    NQ = 2 * CT1
    TILES = [(t, h) for h in range(2) for t in range(CT1)]
    PLAN = [("q", 0), ("o", 2), ("o", 3), ("q", 1), ("q", 2), ("q", 3), ("o", 0), ("o", 1)]
    GH = HT1 // 2
    HALF_P = P // 2

    def use_of(b, n, first=False, last=False):
        if first and n == 0:
            return NQ
        return NT * b + 2 + n - (sum(kind == "q" for kind, _ in PLAN[:n]) if last else 0)

    def bank_of(m, scores_idle):
        return psS[:, m // 2, m % 2 * HALF_N:(m % 2 + 1) * HALF_N] if scores_idle else psQ[:, :]

    with ExitStack() as es:
        def sb(name, shape, dt=F32):
            return es.enter_context(nc.sbuf_tensor("b_" + name, shape, dt))

        def sem(name):
            return es.enter_context(nc.semaphore("b_" + name))

        raw = sb("raw", [P, 2, CT1, S])
        wm_perm = sb("wm_perm", [P, CT1, S])
        wqT = sb("wqT", [P, CT1, S])
        wmT = sb("wmT", [P, CT1, S])
        bq, bm = bias.q, bias.out
        mask = sb("mask", [P, HT1, NK1])
        xn = sb("xn", [P, CT1, D])
        group_mask = sb("group_mask", [P, GH, NK1])
        q = sb("q", [P, 2, HALF_N])
        q_hi = sb("q_hi", [P, 2, HALF_N], F32R)
        q_lo = sb("q_lo", [P, 2, HALF_N], F32R)
        q_stack = sb("q_stack", [P, CT1, 2, D], F32R)
        keys = sb("keys", [P, CT1, 2, NK1])
        keys_hi = sb("keys_hi", [P, CT1, 2, NK1], F32R)
        keys_lo = sb("keys_lo", [P, CT1, 2, NK1], F32R)
        kbd = sb("kbd", [P, 2, 2, CT1, 2, GH, NK1], F32R)
        v1 = sb("v1", [P, 2, NH1 // 2, 2 * HD1])
        maxes = sb("maxes", [P, 2, NH1])
        prob = sb("prob", [P, 2, WIDTH])
        probT = sb("probT", [P, 2, NH1 // 2, P])
        halves = sb("halves", [P, 2, NH1, NK1 // 2])
        quarters = sb("quarters", [P, 2, NH1, NK1 // 4])
        sums = sb("sums", [P, 2, NH1])
        recip_head = sb("recip_head", [P, 2, NH1])
        recip = sb("recip", [P, 2, NH1, HD1])
        recipT = sb("recipT", [P, CT1, P])
        o = sb("o", [P, 2, CT1, D])
        x3n = sb("x3n", [P, TT, D])
        y = sb("y", [P, 2, HALF_N])
        psS = es.enter_context(nc.psum_tensor("b_psS", [P, 2, WIDTH], F32))
        psT = es.enter_context(nc.psum_tensor("b_psT", [P, 2, HALF_N], F32))
        psO = es.enter_context(nc.psum_tensor("b_psO", [P, 2, CT1, P], F32))
        psQ = es.enter_context(nc.psum_tensor("b_psQ", [P, HALF_N], F32))
        norm3 = Norm(nc, es, "b_norm3", sh)

        raw_loaded = [sem(f"raw_loaded{m}") for m in range(2)]
        bm_gated = sem("bm_gated")
        consts_done, perm_done = sem("consts_done"), sem("perm_done")
        w_full, w_copied = sem("w_full"), sem("w_copied")
        kv_loaded = [sem(f"kv_loaded{u}") for u in range(2)]
        keys_hi_ready, keys_lo_ready, kbd_ready = sem("keys_hi_ready"), sem("keys_lo_ready"), sem("kbd_ready")
        q_lo_ready = sem("q_lo_ready")
        q_stacked = [sem(f"q_stacked{m}") for m in range(NQ)]
        psT_full = [sem(f"psT_full{p}") for p in range(2)]
        psT_copied = [sem(f"psT_copied{p}") for p in range(2)]
        psQ_full = sem("psQ_full")
        psQ_used = sem("psQ_used")
        added = sem("added")
        scores_full, max_ready, shifted, exp_done = sem("scores_full"), sem("max_ready"), sem("shifted"), sem("exp_done")
        halves_ready, quarters_ready, sums_ready, head_ready, recip_ready = (
            sem("halves_ready"), sem("quarters_ready"), sem("sums_ready"), sem("head_ready"), sem("recip_ready"))
        psO_full, recipT_ready = sem("psO_full"), sem("recipT_ready")
        o_ready = sem("o_ready")

        block = es.enter_context(nc.Block())

        @block.sync
        def _(sp):
            for m in range(NQ):
                sp.sem_inc(q_stacked[m], 1)

            def load_kv(b, u):
                for half in range(2):
                    for g in range(2):
                        sp.dma_start(keys[half * HALF_P:(half + 1) * HALF_P, :, g, :],
                                     scratch["k1"][bass.ds(b, 1), g * HALF_P:(g + 1) * HALF_P].rearrange(
                                         "b p (t k) -> p (b t) k", t=CT1)).then_inc(kv_loaded[u], 16)
                sp.dma_start(v1[:, u].rearrange("p a n -> p (a n)"),
                             scratch["v1"][bass.ds(b, 1)].rearrange("b p n -> p (b n)")).then_inc(kv_loaded[u], 16)

            def stack_query(b, m, first=False):
                t, h = TILES[m]
                if not first:
                    sp.wait_ge(scores_full, NT * (b - 1) + NT // 2 * (h + 1))
                    hold(sp, sh)
                sp.wait_ge(q_lo_ready, NQ * b + m + 3)
                cols = slice(h * HALF_N, (h + 1) * HALF_N)
                for g in range(2):
                    rows = slice(g * HALF_P, (g + 1) * HALF_P)
                    for src, half in ((q_hi, g), (q_lo, 1 - g)):
                        sp.dma_start(plain(q_stack)[half * HALF_P:(half + 1) * HALF_P, t, g, cols],
                                     plain(src)[rows, m % 2, :]).then_inc(q_stacked[m], 16)

            def load_projection(m, name):
                sp.dma_start(raw[:, m, :, :], c[name].rearrange("(t p) d -> p t d", p=P)).then_inc(raw_loaded[m], 16)

            load_projection(0, "Wq1")
            load_kv(0, 0)
            load_projection(1, "Wm1")
            for m in range(NQ):
                stack_query(0, m, True)

            def body(i, first, final):
                for u in range(2):
                    b = 2 * i + u
                    if not (first and u == 0):
                        sp.wait_ge(o_ready, NT * b + 1)
                    if not (final and u == 1):
                        if first and u == 0:
                            sp.wait_ge(keys_lo_ready, 1)
                        load_kv(b + 1, 1 - u)
                        for m in range(NQ):
                            stack_query(b + 1, m)

            body(0, True, False)
            with sp.Fori(1, PAIRS - 1) as i:
                body(i, False, False)
            body(PAIRS - 1, False, True)
        @block.gpsimd
        def _(pool):
            pool.sem_inc(added, 2)
            pool.sem_inc(q_lo_ready, 2)
            nc.gpsimd.memset(mask[:, :, :], HD1 ** -0.5).then_inc(consts_done, 1)
            pool.wait_ge(consts_done, 1)
            nc.gpsimd.affine_select(out=mask[:, :, :], in_=mask[:, :, :], compare_op=ALU.is_ge, fill=0.0, base=0,
                                    pattern=[[-HD1, HT1], [0, NK1]], channel_multiplier=1).then_inc(consts_done, 1)
            pool.wait_ge(consts_done, 2)
            nc.gpsimd.affine_select(out=mask[:, :, :], in_=mask[:, :, :], compare_op=ALU.is_ge, fill=0.0, base=HD1 - 1,
                                    pattern=[[HD1, HT1], [0, NK1]], channel_multiplier=-1).then_inc(consts_done, 1)
            pool.wait_ge(consts_done, 3)

            nc.gpsimd.tensor_tensor(group_mask[:, :, :], mask[:, 0:GH, :], mask[:, GH:HT1, :], ALU.add).then_inc(consts_done, 1)
            pool.wait_ge(consts_done, 4)

            def low_keys(b):
                pool.wait_ge(keys_hi_ready, b + 1)
                nc.gpsimd.tensor_tensor(keys_lo[:, :, :, :], keys[:, :, :, :], plain(keys_hi)[:, :, :, :], ALU.subtract
                                        ).then_inc(keys_lo_ready, 1)

            def block_keys(b, u, part, t):
                pool.wait_ge((keys_hi_ready, keys_lo_ready)[part], b + 1)
                src = plain((keys_hi, keys_lo)[part])
                nc.gpsimd.tensor_tensor(kbd[:, u, part, t], group_mask[:, :, :].unsqueeze(1).broadcast_to([P, 2, GH, NK1]),
                                        src[:, t, :, :].unsqueeze(2).broadcast_to([P, 2, GH, NK1]), ALU.mult
                                        ).then_inc(kbd_ready, 1)

            def low_query(use, b, m):
                pool.wait_ge(psQ_used, use + 2)
                nc.gpsimd.tensor_tensor(q_lo[:, m % 2, :], q[:, m % 2, :], plain(q_hi)[:, m % 2, :], ALU.subtract
                                        ).then_inc(q_lo_ready, 1)

            def add_output(use, b, t, h):
                pool.wait_ge(psQ_used, use + 2)
                cols = slice(h * HALF_N, (h + 1) * HALF_N)
                rows = x[:, bass.ds(b, 1), t, cols].rearrange("p b d -> p (b d)")
                nc.gpsimd.tensor_tensor(rows, rows, y[:, TILES.index((t, h)) % 2, :], ALU.add).then_inc(added, 1)

            low_keys(0)
            for part in range(2):
                for t in range(CT1):
                    block_keys(0, 0, part, t)
            for m in range(NQ):
                low_query(m, 0, m)

            def body(i, first, final):
                for u in range(2):
                    b = 2 * i + u
                    more = not (final and u == 1)
                    alone = first and u == 0
                    for n in range(NT):
                        pool.wait_ge(exp_done, NT * b + n + 1)
                        unit = prob[:, n % 2, :].rearrange("p (h k) -> p h k", h=NH1)
                        nc.gpsimd.tensor_tensor(halves[:, n % 2], unit[:, :, 0:NK1 // 2], unit[:, :, NK1 // 2:NK1], ALU.add
                                                ).then_inc(halves_ready, 1)
                        pool.wait_ge(halves_ready, NT * b + n + 1)
                        nc.gpsimd.tensor_tensor(quarters[:, n % 2], halves[:, n % 2, :, 0:NK1 // 4],
                                                halves[:, n % 2, :, NK1 // 4:NK1 // 2], ALU.add).then_inc(quarters_ready, 1)
                        kind, m = PLAN[n - 1]
                        if n == 0 and not alone:
                            add_output(use_of(b - 1, NT - 1), b - 1, *TILES[m])
                        elif n and kind == "q" and more:
                            low_query(use_of(b, n - 1, alone), b + 1, m)
                        elif n and kind == "o" and not (alone and m >= 2):
                            add_output(use_of(b, n - 1, alone, not more), b - m // 2, *TILES[m])
                        if more and n == 3:
                            low_keys(b + 1)
                        if more and 2 <= n <= 5:
                            block_keys(b + 1, 1 - u, (n - 2) // CT1, (n - 2) % CT1)
                        if n == 6 and not alone:
                            norm3.rstd_of(pool, b - 1, rms=False)

            body(0, True, False)
            with pool.Fori(1, PAIRS - 1) as i:
                body(i, False, False)
            body(PAIRS - 1, False, True)
            for k, m in enumerate((1, 2, 3)):
                add_output(use_of(B - 1, NT - 1 + k, False, True), B - 1, *TILES[m])
            norm3.rstd_of(pool, B - 1, rms=False)

        @block.tensor
        def _(pe):
            def weight_transposes(m):
                src = (raw[:, 0], wm_perm)[m]
                for t in range(CT1):
                    for ot in range(CT1):
                        last = nc.tensor.transpose(psT[:, m, t * S + ot * P:t * S + (ot + 1) * P],
                                                   src[:, ot, t * P:(t + 1) * P], ident[:, :])
                last.then_inc(w_full, 1)

            pe.wait_ge(raw_loaded[0], 16)
            weight_transposes(0)

            def query(use, t, h, prologue=False):
                if not prologue:
                    pe.wait_ge(psQ_used, use + 1)
                for dt in range(CT1):
                    last = nc.tensor.matmul(bank_of(use, prologue), wqT[:, dt, t * P:(t + 1) * P], xn[:, dt, h * HALF_N:(h + 1) * HALF_N],
                                            start=(dt == 0), stop=(dt == CT1 - 1))
                last.then_inc(psQ_full, 1)

            def output(use, u, t, h, o_count, tail=False):
                if not tail:
                    pe.wait_ge(psQ_used, use + 1)
                pe.wait_ge(o_ready, o_count + 1)
                for dt in range(CT1):
                    last = nc.tensor.matmul(bank_of(TILES.index((t, h)), tail), wmT[:, dt, t * P:(t + 1) * P],
                                            o[:, u, dt, h * HALF_N:(h + 1) * HALF_N],
                                            start=(dt == 0), stop=(dt == CT1 - 1))
                last.then_inc(psQ_full, 1)

            def scores(b, u, n):
                if n == 0:
                    pe.wait_ge(kbd_ready, 2 * CT1 * (b + 1))
                if n % (NT // 2) == 0:
                    for t in range(CT1):
                        pe.wait_ge(q_stacked[TILES.index((t, n // (NT // 2)))], 64 * (b + 1) + 1)
                for t in range(CT1):
                    for g in range(2):
                        for part in range(2):
                            cols = slice((2 * t + g) * GH * NK1, (2 * t + g + 1) * GH * NK1)
                            last = nc.tensor.matmul(psS[:, n % 2, cols], q_stack[:, t, g, n * P:(n + 1) * P],
                                                    kbd[:, u, part, t, g, :, :].rearrange("p h k -> p (h k)"),
                                                    start=(part == 0), stop=(part == 1))
                last.then_inc(scores_full, 1)

            def transposes(b, n):
                pe.wait_ge(exp_done, NT * b + n + 1)
                for t in range(CT1):
                    pe.wait_ge(psT_copied[t], NT * b + n + 1)
                    for j in range(4):
                        last = nc.tensor.transpose(psT[:, t, j * P:(j + 1) * P],
                                                   prob[:, n % 2, (4 * t + j) * P:(4 * t + j + 1) * P], ident[:, :])
                    last.then_inc(psT_full[t], 1)

            def values(b, u, n):
                pe.wait_ge(o_ready, NT * b + n + 1)
                for t in range(CT1):
                    pe.wait_ge(psT_copied[t], NT * b + n + 2)
                for t in range(CT1):
                    for j in range(4):
                        nc.tensor.matmul(psO[j * 2 * HD1:(j + 1) * 2 * HD1, 0, t, :], v1[:, u, 4 * t + j, :],
                                         probT[:, n % 2, 4 * t + j, :], start=True, stop=True)
                pe.wait_ge(recip_ready, NT * b + n + 1)
                for t in range(CT1):
                    last = nc.tensor.transpose(psO[:, 1, t, :], recip[:, n % 2, t * HT1:(t + 1) * HT1, :].rearrange(
                        "p h c -> p (h c)"), ident[:, :])
                last.then_inc(psO_full, 1)

            pe.wait_ge(w_copied, 1)
            pe.wait_ge(x2_norm.normed, TT)
            for m, (t, h) in enumerate(TILES):
                query(m, t, h, True)
            pe.wait_ge(perm_done, 1)
            weight_transposes(1)
            pe.wait_ge(w_copied, 2)
            pe.wait_ge(psQ_used, NQ // 2 + 1)
            scores(0, 0, 0)
            pe.wait_ge(psQ_used, NQ + 1)
            scores(0, 0, 1)

            def body(i, first, final):
                for u in range(2):
                    b = 2 * i + u
                    more = not (final and u == 1)
                    alone = first and u == 0
                    for n in range(NT):
                        transposes(b, n)
                        if n + 2 < NT:
                            scores(b, u, n + 2)
                        elif more:
                            scores(b + 1, 1 - u, n + 2 - NT)
                        if n:
                            values(b, u, n - 1)
                        elif not alone:
                            values(b - 1, 1 - u, NT - 1)
                        kind, m = PLAN[n]
                        t, h = TILES[m]
                        use = use_of(b, n, alone, not more)
                        if kind == "q" and more:
                            pe.wait_ge(x2_norm.normed, TT * b + 2 * TT)
                            query(use, t, h)
                        elif kind == "o" and not (alone and m >= 2):
                            output(use, 1 - u if m >= 2 else u, t, h, NT * (b - m // 2) + NT // 2 * (h + 1))

            body(0, True, False)
            with pe.Fori(1, PAIRS - 1) as i:
                body(i, False, False)
            body(PAIRS - 1, False, True)
            values(B - 1, 1, NT - 1)
            for m in (2, 3):
                t, h = TILES[m]
                output(None, 1, t, h, NT * (B - 1) + NT // 2 * (h + 1), True)

        @block.vector
        def _(dve):
            dve.sem_inc(o_ready, 1)
            dve.sem_inc(psQ_used, 1)

            nc.vector.tensor_scalar(bm[:, :], bm[:, :], sh.gates[:, 1:2], None, ALU.mult).then_inc(bm_gated, 1)
            for t in range(TT):
                x2_norm.normalise_tile(0, t, batch_of(x, 0), xn)
            dve.wait_ge(w_full, 1)
            nc.vector.tensor_copy(wqT[:, :, :].rearrange("p t (h c) -> p t h c", h=NH1),
                                  psT[:, 0, :].rearrange("p (t c h) -> p t h c", t=CT1, h=NH1)).then_inc(w_copied, 1)
            dve.wait_ge(raw_loaded[1], 16)
            nc.vector.tensor_copy(wm_perm[:, :, :].rearrange("p t (h c) -> p t h c", h=NH1),
                                  raw[:, 1, :, :].rearrange("p t (c h) -> p t h c", h=NH1)).then_inc(perm_done, 1)
            dve.wait_ge(w_full, 2)
            nc.vector.tensor_copy(wmT[:, :, :].rearrange("p t d -> p (t d)"), psT[:, 1, :]).then_inc(w_copied, 1)

            def maximum(b, n):
                dve.wait_ge(scores_full, NT * b + n + 1)
                nc.vector.tensor_reduce(maxes[:, n % 2, :], psS[:, n % 2, :].rearrange("p (h k) -> p h k", h=NH1), AX_X,
                                        ALU.max).then_inc(max_ready, 1)

            def shift(b, n):
                dve.wait_ge(max_ready, NT * b + n + 1)
                nc.vector.tensor_tensor(prob[:, n % 2, :].rearrange("p (h k) -> p h k", h=NH1),
                                        psS[:, n % 2, :].rearrange("p (h k) -> p h k", h=NH1),
                                        maxes[:, n % 2, :].unsqueeze(2).broadcast_to([P, NH1, NK1]),
                                        ALU.subtract).then_inc(shifted, 1)

            def reciprocals(b, n):
                dve.wait_ge(quarters_ready, NT * b + n + 1)
                nc.vector.tensor_reduce(sums[:, n % 2, :], quarters[:, n % 2], AX_X, ALU.add).then_inc(sums_ready, 1)
                dve.wait_ge(sums_ready, NT * b + n + 1)
                nc.vector.reciprocal(recip_head[:, n % 2, :], sums[:, n % 2, :]).then_inc(head_ready, 1)

            def normalise_o(b, u, n):
                dve.wait_ge(recipT_ready, NT * b + n + 1)
                nc.vector.tensor_tensor(o[:, u, :, n * P:(n + 1) * P], psO[:, 0, :, :], recipT[:, :, :], ALU.mult
                                        ).then_inc(o_ready, 1)

            def normalise_x3(k, t):
                dve.wait_ge(norm3.rstd_steps, norm3.STEPS * (k + 1))
                nc.vector.tensor_scalar(x3n[:, t, :], batch_of(x, k)[:, t, :], norm3.moments[:, t, 0:1],
                                        norm3.rstd[:, t:t + 1], ALU.subtract, ALU.mult).then_inc(norm3.normed, 1)

            def keep_x3(k):
                dve.wait_ge(norm3.rstd_steps, norm3.STEPS * (k + 1))
                at = bass.ds(k, 1)
                nc.vector.tensor_copy(quant.mean[:, at, :].rearrange("p b t -> p (b t)"), norm3.moments[:, :, 0])
                nc.vector.tensor_copy(quant.rstd[:, at, :].rearrange("p b t -> p (b t)"), norm3.rstd[:, :])

            def largest_x3(k, t):
                dve.wait_ge(norm3.normed, TT * k + t + 1)
                nc.vector.tensor_reduce(quant.row_max[:, bass.ds(k, 1), t], x3n[:, t, :], AX_X, ALU.max,
                                        apply_absolute_value=True)

            dve.wait_ge(psQ_full, NQ)
            for t in range(TT):
                x2_norm.normalise_tile(1, t, batch_of(x, 1), xn)
            for n in range(2):
                maximum(0, n)
                shift(0, n)

            def body(i, first, final):
                for u in range(2):
                    b = 2 * i + u
                    more = not (final and u == 1)
                    alone = first and u == 0
                    for n in range(NT):
                        if n + 2 < NT:
                            maximum(b, n + 2)
                        elif more:
                            maximum(b + 1, n + 2 - NT)
                        reciprocals(b, n)
                        if n + 2 < NT:
                            shift(b, n + 2)
                        elif more:
                            shift(b + 1, n + 2 - NT)
                        if n:
                            normalise_o(b, u, n - 1)
                        elif not alone:
                            normalise_o(b - 1, 1 - u, NT - 1)
                        if not alone:
                            if n == 4:
                                dve.wait_ge(added, NQ * (b - 1) + NQ + 2)
                                hold(dve, sh)
                                norm3.stats_of(batch_of(x, b - 1), 0)
                            if n == 5:
                                norm3.moments_of(dve, b - 1, batch_of(x, b - 1), last_tile_only=True)
                        if not first:
                            if n == 0:
                                keep_x3(b - 2)
                            if n in (0, 2):
                                normalise_x3(b - 2, n // 2)
                            if n in (1, 3):
                                largest_x3(b - 2, n // 2)
                        if n >= 6 and not final:
                            dve.wait_ge(psQ_full, use_of(b, 5) + 1)
                            x2_norm.normalise_tile(b + 2, n - 6, batch_of(x, b + 2), xn)

            body(0, True, False)
            with dve.Fori(1, PAIRS - 1) as i:
                body(i, False, False)
            body(PAIRS - 1, False, True)
            normalise_o(B - 1, 1, NT - 1)
            keep_x3(B - 2)
            for t in range(TT):
                normalise_x3(B - 2, t)
                largest_x3(B - 2, t)
            dve.wait_ge(added, NQ * B + 2)
            norm3.moments_of(dve, B - 1, batch_of(x, B - 1))
            for t in range(TT):
                normalise_x3(B - 1, t)
            keep_x3(B - 1)
            for t in range(TT):
                largest_x3(B - 1, t)

        @block.scalar
        def _(act):
            for p in range(2):
                act.sem_inc(psT_copied[p], 1)

            def copy_query(use, b, m, prologue=False):
                t = TILES[m][0]
                act.wait_ge(psQ_full, use + 1)
                act.wait_ge(q_lo_ready, NQ * b + m + 1)
                act.wait_ge(q_stacked[(m + 2) % NQ], 64 * (b + m // 2) + 1)
                hold(act, sh)
                for dst in (q, q_hi):
                    last = nc.scalar.activation(dst[:, m % 2, :], bank_of(use, prologue), ACT.Identity, bias=bq[:, t:t + 1])
                last.then_inc(psQ_used, 1)

            def high_keys(b, i, u):
                act.wait_ge(kv_loaded[u], 80 * i + 80)
                nc.scalar.copy(keys_hi[:, :, :, :], keys[:, :, :, :]).then_inc(keys_hi_ready, 1)

            def spread_reciprocals(b, n):
                act.wait_ge(head_ready, NT * b + n + 1)
                nc.scalar.copy(recip[:, n % 2], recip_head[:, n % 2].unsqueeze(2).broadcast_to([P, NH1, HD1])
                               ).then_inc(recip_ready, 1)

            def exponential(b, n):
                act.wait_ge(shifted, NT * b + n + 1)
                nc.scalar.activation(prob[:, n % 2, :], prob[:, n % 2, :], ACT.Exp).then_inc(exp_done, 1)

            def copy_reciprocals(b, n):
                act.wait_ge(psO_full, NT * b + n + 1)
                nc.scalar.copy(recipT[:, :, :], psO[:, 1, :, :]).then_inc(recipT_ready, 1)

            def copy_output(use, b, t, h, tail=False):
                m = TILES.index((t, h))
                act.wait_ge(psQ_full, use + 1)
                act.wait_ge(added, NQ * b + m + 1)
                nc.scalar.activation(y[:, m % 2, :], bank_of(m, tail), ACT.Identity, bias=bm[:, t:t + 1], scale=sh.gates[:, 1:2]
                                     ).then_inc(psQ_used, 1)

            act.wait_ge(bm_gated, 1)
            high_keys(0, 0, 0)
            for m in range(NQ):
                copy_query(m, 0, m, True)
            exponential(0, 0)
            exponential(0, 1)

            def body(i, first, final):
                for u in range(2):
                    b = 2 * i + u
                    more = not (final and u == 1)
                    for n in range(NT):
                        alone = first and u == 0
                        kind, m = PLAN[n - 1]
                        if n == 0 and not alone:
                            copy_output(use_of(b - 1, NT - 1), b - 1, *TILES[m])
                        elif n and kind == "q" and more:
                            copy_query(use_of(b, n - 1, alone), b + 1, m)
                        elif n and kind == "o" and not (alone and m >= 2):
                            copy_output(use_of(b, n - 1, alone, not more), b - m // 2, *TILES[m])
                        for t in range(CT1):
                            act.wait_ge(psT_full[t], NT * b + n + 1)
                            nc.scalar.copy(probT[:, n % 2, 4 * t:4 * t + 4, :],
                                           psT[:, t, :].rearrange("p (j q) -> p j q", j=4)).then_inc(psT_copied[t], 1)
                        if n:
                            copy_reciprocals(b, n - 1)
                        elif not (first and u == 0):
                            copy_reciprocals(b - 1, NT - 1)
                        if n + 2 < NT:
                            exponential(b, n + 2)
                        elif more:
                            exponential(b + 1, n + 2 - NT)
                        spread_reciprocals(b, n)
                        if n == 1 and more:
                            high_keys(b + 1, i + u, 1 - u)

            body(0, True, False)
            with act.Fori(1, PAIRS - 1) as i:
                body(i, False, False)
            body(PAIRS - 1, False, True)
            copy_reciprocals(B - 1, NT - 1)
            for k, m in enumerate((1, 2, 3)):
                copy_output(use_of(B - 1, NT - 1 + k, False, True), B - 1, *TILES[m], m > 1)


def ffn1_stage(nc, sh, out, quant, x):
    with ExitStack() as es:
        def sb(name, shape, dt=F32):
            return es.enter_context(nc.sbuf_tensor("q_" + name, shape, dt))

        def sem(name):
            return es.enter_context(nc.semaphore("q_" + name))

        ident16 = sb("ident16", [P, P], BF16)
        factor = sb("factor", [P, B, TT])
        out_scale = sb("out_scale", [P, 1])
        scaled = sb("scaled", [P, 2, TT, D])
        shifted = sb("shifted", [P, TT, D])
        magic = sb("magic", [P, TT, D])
        total = sb("total", [P, TT, D])
        xq = sb("xq", [P, 2, TT, D], BF16)
        xqT = sb("xqT", [P, 2, KT, S], BF16)
        y = sb("y", [P, 2, TT, D])
        psT = es.enter_context(nc.psum_tensor("q_psT", [P, 2, 2 * HALF_N], BF16))
        psY = es.enter_context(nc.psum_tensor("q_psY", [P, 4, HALF_N], F32))

        ident_ready = sem("ident_ready")
        factors_ready, out_scale_ready = sem("factors_ready"), sem("out_scale_ready")
        scaled_ready, shifted_ready, magic_ready = sem("scaled_ready"), sem("shifted_ready"), sem("magic_ready")
        total_ready, rounded, quantised = sem("total_ready"), sem("rounded"), sem("quantised")
        psT_full = sem("psT_full")
        xqT_ready = sem("xqT_ready")
        psY_full = sem("psY_full")
        y_scaled = sem("y_scaled")
        y_ready = sem("y_ready")
        y_stored = [sem(f"y_stored{u}") for u in range(2)]

        block = es.enter_context(nc.Block())

        @block.sync
        def _(sp):
            for u in range(2):
                sp.sem_inc(y_stored[u], 1)
            with sp.Fori(0, PAIRS) as i:
                for u in range(2):
                    sp.wait_ge(y_ready, 8 * i + 4 * u + 4)
                    sp.dma_start(out[bass.ds(2 * i + u, 1)].rearrange("b (t p) d -> p (b t) d", p=P), y[:, u, :, :]
                                 ).then_inc(y_stored[u], 16)
            for u in range(2):
                sp.wait_ge(y_stored[u], 16 * PAIRS + 1)

        @block.gpsimd
        def _(pool):
            pool.wait_ge(quant.part_done, 2)
            nc.gpsimd.partition_all_reduce(quant.all_max[:, 0:1], quant.part_max[:, 0:1], P, ABSMAX
                                           ).then_inc(quant.all_done, 1)
            nc.gpsimd.tensor_copy(ident16[:, :], sh.ident[:, :]).then_inc(ident_ready, 1)
            with pool.Fori(0, PAIRS) as i:
                for u in range(2):
                    b = 2 * i + u
                    for t in range(TT):
                        for h in range(2):
                            pool.wait_ge(y_scaled, 4 * b + 2 * t + h + 5)
                            cols = slice(h * HALF_N, (h + 1) * HALF_N)
                            nc.gpsimd.tensor_tensor(y[:, u, t, cols], y[:, u, t, cols],
                                                    x[:, bass.ds(b, 1), t, cols].rearrange("p b d -> p (b d)"), ALU.add
                                                    ).then_inc(y_ready, 1)

        @block.tensor
        def _(pe):
            pe.wait_ge(ident_ready, 1)

            def transposes(b, u):
                pe.wait_ge(quantised, b + 1)
                for n in range(2):
                    pe.wait_ge(xqT_ready, 2 * b + n + 1)
                    for q in range(4):
                        for t in range(TT):
                            kt = 4 * n + q
                            last = nc.tensor.transpose(psT[:, n, (q * TT + t) * P:(q * TT + t + 1) * P],
                                                       xq[:, u, t, kt * P:(kt + 1) * P], ident16[:, :])
                    last.then_inc(psT_full, 1)

            transposes(0, 0)

            def body(i, final):
                for u in range(2):
                    b = 2 * i + u
                    for t in range(TT):
                        for h in range(2):
                            pe.wait_ge(y_scaled, 4 * b + 2 * t + h + 1)
                            for kt in range(KT):
                                if t == 0 and h == 0 and kt % 4 == 0:
                                    pe.wait_ge(xqT_ready, 2 * b + kt // 4 + 3)
                                last = nc.tensor.matmul(psY[:, 2 * t + h, :], xqT[:, u, kt, t * P:(t + 1) * P],
                                                        quant.weight[:, kt, h * HALF_N:(h + 1) * HALF_N],
                                                        start=(kt == 0), stop=(kt == KT - 1))
                            last.then_inc(psY_full, 1)
                        if t == 0 and not (final and u == 1):
                            transposes(b + 1, 1 - u)

            with pe.Fori(0, PAIRS - 1) as i:
                body(i, False)
            body(PAIRS - 1, True)

        @block.vector
        def _(dve):
            nc.vector.tensor_reduce(quant.part_max[:, 0:1], quant.row_max[:, :, :].rearrange("p b t -> p (b t)"), AX_X,
                                    ALU.max).then_inc(quant.part_done, 1)
            quant.scale_of(nc, dve, 0, 2).then_inc(quant.steps, 1)
            nc.vector.tensor_scalar(factor[:, :, :], quant.rstd[:, :, :], quant.scale[:, 0:1], None, ALU.mult
                                    ).then_inc(factors_ready, 1)
            dve.wait_ge(quant.steps, 7)
            nc.vector.tensor_tensor(out_scale[:, :], quant.inverse[:, 0:1], quant.inverse[:, 1:2], ALU.mult
                                    ).then_inc(quant.steps, 1)
            dve.wait_ge(quant.steps, 8)
            nc.vector.tensor_tensor(out_scale[:, :], out_scale[:, :], sh.gates[:, 3:4], ALU.mult).then_inc(out_scale_ready, 1)
            dve.wait_ge(factors_ready, 1)

            def scale(b, u):
                for t in range(TT):
                    rows = x[:, bass.ds(b, 1), t, :].rearrange("p b d -> p (b d)")
                    nc.vector.tensor_scalar(scaled[:, u, t, :], rows,
                                            quant.mean[:, bass.ds(b, 1), t], factor[:, bass.ds(b, 1), t],
                                            ALU.subtract, ALU.mult).then_inc(scaled_ready, 1)

            def magic_and_sum(b, u):
                for t in range(TT):
                    dve.wait_ge(shifted_ready, TT * b + t + 1)
                    fp8_magic(nc, magic[:, t, :], shifted[:, t, :]).then_inc(magic_ready, 1)
                for t in range(TT):
                    dve.wait_ge(magic_ready, TT * b + t + 1)
                    fp8_add_magic(nc, total[:, t, :], magic[:, t, :], scaled[:, u, t, :]).then_inc(total_ready, 1)

            def round_and_clip(b, u):
                dve.wait_ge(xqT_ready, 2 * b + 1)
                for t in range(TT):
                    dve.wait_ge(total_ready, TT * b + t + 1)
                    fp8_minus_rounded(nc, xq[:, u, t, :], magic[:, t, :], total[:, t, :]).then_inc(rounded, 1)
                dve.wait_ge(rounded, TT * b + TT)
                fp8_clip(nc, xq[:, u, :, :].rearrange("p t d -> p (t d)")).then_inc(quantised, 1)

            scale(0, 0)

            def body(i, final):
                for u in range(2):
                    b = 2 * i + u
                    magic_and_sum(b, u)
                    if not (final and u == 1):
                        scale(b + 1, 1 - u)
                    round_and_clip(b, u)

            with dve.Fori(0, PAIRS - 1) as i:
                body(i, False)
            body(PAIRS - 1, True)

        @block.scalar
        def _(act):
            act.sem_inc(xqT_ready, 2)
            act.sem_inc(y_scaled, 4)
            act.wait_ge(out_scale_ready, 1)

            def copy_transposed(b, u):
                for n in range(2):
                    act.wait_ge(psT_full, 2 * b + n + 1)
                    nc.scalar.copy(xqT[:, u, 4 * n:4 * n + 4, :].rearrange("p k n -> p (k n)"), psT[:, n, :]
                                   ).then_inc(xqT_ready, 1)

            def shift(b, u):
                for t in range(TT):
                    act.wait_ge(scaled_ready, TT * b + t + 1)
                    nc.scalar.mul(shifted[:, t, :], scaled[:, u, t, :], FP8_SHIFT).then_inc(shifted_ready, 1)

            shift(0, 0)
            shift(1, 1)
            copy_transposed(0, 0)

            def body(i, final):
                for u in range(2):
                    b = 2 * i + u
                    for t in range(TT):
                        for h in range(2):
                            act.wait_ge(psY_full, 4 * b + 2 * t + h + 1)
                            if t == 0 and h == 0:
                                act.wait_ge(y_stored[u], 16 * i + 1)
                            nc.scalar.mul(y[:, u, t, h * HALF_N:(h + 1) * HALF_N], psY[:, 2 * t + h, :], out_scale[:, 0:1]
                                          ).then_inc(y_scaled, 1)
                        if t == 0 and not (final and u == 1):
                            if not final:
                                shift(b + 2, u)
                            copy_transposed(b + 1, 1 - u)

            with act.Fori(0, PAIRS - 1) as i:
                body(i, False)
            body(PAIRS - 1, True)


_NAMES = {"wk": "L0_xattn_wk", "wv": "L0_xattn_wv", "wq": "L0_xattn_wq", "wo": "L0_xattn_wo", "ln_w": "L0_xattn_ln_w",
          "x": "x", "ctx": "ctx_4096", "W_base": "L0_ffn_W_base", "b_base": "L0_ffn_b_base", "enc0": "L0_ffn_enc0",
          "enc1": "L0_ffn_enc1", "coefs0": "L0_ffn_coefs0", "coefs1": "L0_ffn_coefs1", "mask0": "L0_ffn_mask0",
          "mask1": "L0_ffn_mask1", "Wq1": "L1_xattn_Wq", "bq1": "L1_xattn_bq", "Wk1": "L1_xattn_Wk", "bk1": "L1_xattn_bk",
          "Wv1": "L1_xattn_Wv", "bv1": "L1_xattn_bv", "proj_k": "L1_xattn_proj_k", "proj_v": "L1_xattn_proj_v",
          "Wm1": "L1_xattn_Wm", "bm1": "L1_xattn_bm", "weight": "L1_ffn_weight", "g_xattn": "g_xattn", "g_ffn": "g_ffn"}


def build(nc, a, out):
    scratch = {}
    for name in ("k0_hi", "k0_lo"):
        scratch[name] = nc.dram_tensor("scratch_" + name, [B, KV0, S], F32).ap()
    scratch["update"] = nc.dram_tensor("scratch_update", [RR, D], F32).ap()
    scratch["o"] = nc.dram_tensor("scratch_o", [B, D, S], F32).ap()
    for name, width in (("v0", TT * KV0), ("k1", CT1 * NK1), ("v1", S)):
        scratch[name] = nc.dram_tensor("scratch_" + name, [B, P, width], F32).ap()
    scratch["x1"] = nc.dram_tensor("scratch_x1", [B, S, D], F32).ap()
    with ExitStack() as es:
        sh = setup_stage(nc, es, a["g_xattn"], a["g_ffn"])
        quant = Quant(nc, es)
        with ExitStack() as held:
            with ExitStack() as early:
                rows = Rows(nc, early)
                with ExitStack() as first:
                    wq = SplitWeight(nc, first, "wq")
                    norm = Norm(nc, first, "norm0", sh)
                    norm.rstd_mid = first.enter_context(nc.semaphore("norm0_rstd_mid"))
                    context_stage(nc, sh, a, scratch, wq, rows.batches, norm)
                    attn0_stage(nc, sh, a, scratch, wq, rows, norm)
                w_ffn = SplitWeight(nc, held, "w_ffn", side="right")
                proj0_stage(nc, sh, a, scratch, quant, w_ffn, rows)
            stream = es.enter_context(nc.sbuf_tensor("stream", [P, B, TT, D], F32))
            quant.weight = quant.sb("weight", [P, KT, D], BF16)
            x2_norm = StreamNorm(nc, es, "x2_norm", sh)
            attn1_bias = Attn1Bias(nc, es)
            ffn0_stage(nc, sh, a, scratch, w_ffn, stream, x2_norm, quant, attn1_bias)
        attn1_stage(nc, sh, a, scratch, quant, stream, x2_norm, attn1_bias)
        ffn1_stage(nc, sh, out, quant, stream)


def inverse_rfft_table():
    o = np.arange(D)
    table = np.empty((D, D), np.float64)
    table[0] = D ** -0.5
    table[D - 1] = np.where(o % 2 == 0, 1.0, -1.0) * D ** -0.5
    k = np.arange(1, D // 2)[:, None]
    angle = 2.0 * np.pi * ((k * o) % D) / D
    table[1:D - 1:2] = (2.0 / D) ** 0.5 * np.cos(angle)
    table[2:D:2][:D // 2 - 1] = (2.0 / D) ** 0.5 * np.sin(angle)
    return table.astype(np.float32)


def kernel(**inputs):
    import concourse.bacc as bacc
    from concourse.bass_utils import run_bass_kernel_spmd

    nc = bacc.Bacc("TRN2", target_bir_lowering=False, num_devices=1)
    arrays, args = {}, {}
    for short, name in _NAMES.items():
        array = np.ascontiguousarray(inputs[name])
        arrays["in_" + short] = array
        args[short] = nc.dram_tensor("in_" + short, array.shape, mybir.dt.from_np(array.dtype), kind="ExternalInput").ap()
    arrays["irfft"] = inverse_rfft_table()
    args["irfft"] = nc.dram_tensor("irfft", (D, D), F32, kind="ExternalInput").ap()
    out = nc.dram_tensor("out", (B, S, D), F32, kind="ExternalOutput").ap()
    build(nc, args, out)
    return run_bass_kernel_spmd(nc, [arrays], core_ids=[0]).results[0]["out"]
```
